# Optimizing a Trainium2 kernel written in Bass

```python
import numpy as np
import jax
import jax.numpy as jnp

def _softmax(x, axis=-1):
    return jax.nn.softmax(x, axis=axis)

def _gelu(x):
    return jax.nn.gelu(x, approximate=True)

def _silu(x):
    return jax.nn.silu(x)

def _sigmoid(x):
    return jax.nn.sigmoid(x)

def _layernorm(x, axis=-1, eps=1e-05):
    m = jnp.mean(x, axis=axis, keepdims=True)
    v = jnp.var(x, axis=axis, keepdims=True)
    return (x - m) / jnp.sqrt(v + eps)

def _scatter_add(tgt, idx, src, axis=0):
    return tgt.at[idx].add(src)

def _segment_sum(src, seg, n):
    return jax.ops.segment_sum(src, seg, n)
kernel_name = 'mk_flamingo_gated_d2_seqx_r4_8cd950'

def setup_inputs(seed: int=0):
    np.random.seed(seed)
    _w = jnp.asarray

    def _rec_inputs():
        import jax
        import jax.numpy as jnp
        _rk = jax.random.key(seed)
        x = 0.002226 + 0.9996 * jax.random.normal(jax.random.fold_in(_rk, 1), (4, 1024, 256), jnp.float32)
        _lenS = 1024 - jax.random.randint(jax.random.fold_in(_rk, 7), (4,), 0, max(1, 1024 // 4) + 1, jnp.int32)
        _lenS2 = 154 - jax.random.randint(jax.random.fold_in(_rk, 8), (4,), 0, max(1, 154 // 4) + 1, jnp.int32)
        _ctx_1024P = jax.random.normal(jax.random.fold_in(_rk, 11), (4, 16, 256), jnp.float32)
        _ctx_1024c = jax.random.dirichlet(jax.random.fold_in(_rk, 511), 0.3 * jnp.ones((16,), jnp.float32), (4, 154))
        _ctx_1024t = jnp.einsum('bsk,bkd->bsd', _ctx_1024c, _ctx_1024P)
        _ctx_1024t = _ctx_1024t * jax.lax.rsqrt(jnp.mean(jnp.square(_ctx_1024t)) + 1e-12) * 0.953939
        ctx_1024 = -0.000125008 + 0.999885 * (_ctx_1024t + 0.3 * jax.random.normal(jax.random.fold_in(_rk, 611), (4, 154, 256), jnp.float32))
        _g = jax.random.normal(jax.random.fold_in(_rk, 9001), (2, 2), jnp.float32)
        _g = jnp.sign(_g) * jnp.maximum(jnp.abs(_g), 1.0) + (_g == 0) * 1.0
        g_xattn = _g[0]
        g_ffn = _g[1]
        return (x, ctx_1024, g_xattn, g_ffn)
    x, ctx_1024, g_xattn, g_ffn = _rec_inputs()

    def _L0_xattn_setup():
        import jax, jax.numpy as jnp
        import numpy as np
        B, M, N, DIM, DH, H = (8, 1024, 64, 256, 128, 8)
        INNER = DH * H
        EPS = 1e-05

        def _layernorm(x, g, b):
            mu = jnp.mean(x, axis=-1, keepdims=True)
            var = jnp.var(x, axis=-1, keepdims=True)
            return (x - mu) * jax.lax.rsqrt(var + EPS) * g + b
        key = jax.random.key(seed)
        ks = jax.random.split(key, 8)
        sd = 0.02
        return {'x': jax.random.normal(ks[0], (B, M, DIM), jnp.float32), 'latents': jax.random.normal(ks[1], (B, N, DIM), jnp.float32), 'gamma_media': jnp.ones((DIM,), jnp.float32), 'beta_media': jnp.zeros((DIM,), jnp.float32), 'gamma_lat': jnp.ones((DIM,), jnp.float32), 'beta_lat': jnp.zeros((DIM,), jnp.float32), 'Wq': jax.random.normal(ks[2], (DIM, INNER), jnp.float32) * sd, 'bq': jnp.zeros((INNER,), jnp.float32), 'Wkv': jax.random.normal(ks[3], (DIM, 2 * INNER), jnp.float32) * sd, 'bkv': jnp.zeros((2 * INNER,), jnp.float32), 'Wo': jax.random.normal(ks[4], (INNER, DIM), jnp.float32) * sd, 'bo': jnp.zeros((DIM,), jnp.float32)}
    _L0_xattn_all = _L0_xattn_setup()
    _L0_xattn_in = {k: v for k, v in _L0_xattn_all.items() if k in ('gamma_media', 'beta_media', 'gamma_lat', 'beta_lat', 'Wq', 'bq', 'Wkv', 'bkv', 'Wo', 'bo')}
    del _L0_xattn_all

    def _L0_ffn_setup():
        import jax, jax.numpy as jnp
        import numpy as np
        B, S, D = (4, 128, 256)
        E, K, H = (64, 8, 64)
        ES, HS = (2, 512)
        key = jax.random.key(seed)
        ks = jax.random.split(key, 8)
        scale = 0.02
        rn = lambda k, shape, s: jax.random.normal(k, shape, jnp.float32) * s
        return {'x': rn(ks[0], (B, S, D), 1.0), 'router_w': rn(ks[1], (D, E), scale), 'router_b': jnp.zeros((E,), jnp.float32), 'w1': rn(ks[2], (E, D, H), scale), 'b1': jnp.zeros((E, H), jnp.float32), 'w2': rn(ks[3], (E, H, D), scale), 'b2': jnp.zeros((E, D), jnp.float32), 'sw1': rn(ks[4], (ES, D, HS), scale), 'sb1': jnp.zeros((ES, HS), jnp.float32), 'sw2': rn(ks[5], (ES, HS, D), scale), 'sb2': jnp.zeros((ES, D), jnp.float32)}
    _L0_ffn_all = _L0_ffn_setup()
    _L0_ffn_in = {k: v for k, v in _L0_ffn_all.items() if k in ('router_w', 'router_b', 'w1', 'b1', 'w2', 'b2', 'sw1', 'sb1', 'sw2', 'sb2')}
    del _L0_ffn_all

    def _L1_xattn_setup():
        import jax, jax.numpy as jnp
        import numpy as np
        HIDDEN = 256
        HEADS = 16
        HEAD_DIM = HIDDEN // HEADS
        SCALE = 1.0 / np.sqrt(HEAD_DIM).astype(np.float32)
        key = jax.random.key(seed)
        ks = jax.random.split(key, 8)
        b, t = (2, 512)
        x = jax.random.normal(ks[0], (b, t, HIDDEN), dtype=jnp.float32)
        context = x
        s = 0.02
        Wq = jax.random.normal(ks[1], (HIDDEN, HIDDEN), dtype=jnp.float32) * s
        Wk = jax.random.normal(ks[2], (HIDDEN, HIDDEN), dtype=jnp.float32) * s
        Wv = jax.random.normal(ks[3], (HIDDEN, HIDDEN), dtype=jnp.float32) * s
        Wo = jax.random.normal(ks[4], (HIDDEN, HIDDEN), dtype=jnp.float32) * s
        bo = jnp.zeros((HIDDEN,), dtype=jnp.float32)
        return {'x': x, 'context': context, 'Wq': Wq, 'Wk': Wk, 'Wv': Wv, 'Wo': Wo, 'bo': bo}
    _L1_xattn_all = _L1_xattn_setup()
    _L1_xattn_in = {k: v for k, v in _L1_xattn_all.items() if k in ('Wq', 'Wk', 'Wv', 'Wo', 'bo')}
    del _L1_xattn_all

    def _L1_ffn_setup():
        import jax, jax.numpy as jnp
        import numpy as np
        B, S, D_MODEL, D_HIDDEN = (4, 512, 256, 1024)

        def act_quant(x):
            scale = 127.0 / jnp.clip(jnp.max(jnp.abs(x), axis=-1, keepdims=True), 1e-05)
            return jnp.clip(jnp.round(x * scale), -128, 127) / scale

        def weight_quant(w):
            scale = 1.0 / jnp.clip(jnp.mean(jnp.abs(w)), 1e-05)
            return jnp.clip(jnp.round(w * scale), -1, 1) / scale

        def bit_linear(x, w):
            xq = x + jax.lax.stop_gradient(act_quant(x) - x)
            wq = w + jax.lax.stop_gradient(weight_quant(w) - w)
            return jnp.einsum('bsd,hd->bsh', xq, wq)

        def depthwise_conv1d(x_bcl, w, b):
            y = jax.lax.conv_general_dilated(x_bcl, w, window_strides=(1,), padding=[(1, 1)], dimension_numbers=('NCH', 'OIH', 'NCH'), feature_group_count=x_bcl.shape[1])
            return y + b[None, :, None]
        key = jax.random.key(seed)
        ks = jax.random.split(key, 5)
        lim1 = 1.0 / np.sqrt(D_MODEL)
        lim2 = 1.0 / np.sqrt(D_HIDDEN)
        limc = 1.0 / np.sqrt(3.0)
        return {'x': jax.random.normal(ks[0], (B, S, D_MODEL), dtype=jnp.float32), 'w1': jax.random.uniform(ks[1], (D_HIDDEN, D_MODEL), jnp.float32, -lim1, lim1), 'conv_w': jax.random.uniform(ks[2], (D_HIDDEN, 1, 3), jnp.float32, -limc, limc), 'conv_b': jax.random.uniform(ks[3], (D_HIDDEN,), jnp.float32, -limc, limc), 'w2': jax.random.uniform(ks[4], (D_MODEL, D_HIDDEN), jnp.float32, -lim2, lim2)}
    _L1_ffn_all = _L1_ffn_setup()
    _L1_ffn_in = {k: v for k, v in _L1_ffn_all.items() if k in ('w1', 'conv_w', 'conv_b', 'w2')}
    del _L1_ffn_all
    return {'x': x, 'ctx_1024': ctx_1024, 'g_xattn': g_xattn, 'g_ffn': g_ffn, 'L0_xattn_gamma_media': _L0_xattn_in['gamma_media'], 'L0_xattn_beta_media': _L0_xattn_in['beta_media'], 'L0_xattn_gamma_lat': _L0_xattn_in['gamma_lat'], 'L0_xattn_beta_lat': _L0_xattn_in['beta_lat'], 'L0_xattn_Wq': _L0_xattn_in['Wq'], 'L0_xattn_bq': _L0_xattn_in['bq'], 'L0_xattn_Wkv': _L0_xattn_in['Wkv'], 'L0_xattn_bkv': _L0_xattn_in['bkv'], 'L0_xattn_Wo': _L0_xattn_in['Wo'], 'L0_xattn_bo': _L0_xattn_in['bo'], 'L0_ffn_router_w': _L0_ffn_in['router_w'], 'L0_ffn_router_b': _L0_ffn_in['router_b'], 'L0_ffn_w1': _L0_ffn_in['w1'], 'L0_ffn_b1': _L0_ffn_in['b1'], 'L0_ffn_w2': _L0_ffn_in['w2'], 'L0_ffn_b2': _L0_ffn_in['b2'], 'L0_ffn_sw1': _L0_ffn_in['sw1'], 'L0_ffn_sb1': _L0_ffn_in['sb1'], 'L0_ffn_sw2': _L0_ffn_in['sw2'], 'L0_ffn_sb2': _L0_ffn_in['sb2'], 'L1_xattn_Wq': _L1_xattn_in['Wq'], 'L1_xattn_Wk': _L1_xattn_in['Wk'], 'L1_xattn_Wv': _L1_xattn_in['Wv'], 'L1_xattn_Wo': _L1_xattn_in['Wo'], 'L1_xattn_bo': _L1_xattn_in['bo'], 'L1_ffn_w1': _L1_ffn_in['w1'], 'L1_ffn_conv_w': _L1_ffn_in['conv_w'], 'L1_ffn_conv_b': _L1_ffn_in['conv_b'], 'L1_ffn_w2': _L1_ffn_in['w2']}

def reference(x, ctx_1024, g_xattn, g_ffn, L0_xattn_gamma_media, L0_xattn_beta_media, L0_xattn_gamma_lat, L0_xattn_beta_lat, L0_xattn_Wq, L0_xattn_bq, L0_xattn_Wkv, L0_xattn_bkv, L0_xattn_Wo, L0_xattn_bo, L0_ffn_router_w, L0_ffn_router_b, L0_ffn_w1, L0_ffn_b1, L0_ffn_w2, L0_ffn_b2, L0_ffn_sw1, L0_ffn_sb1, L0_ffn_sw2, L0_ffn_sb2, L1_xattn_Wq, L1_xattn_Wk, L1_xattn_Wv, L1_xattn_Wo, L1_xattn_bo, L1_ffn_w1, L1_ffn_conv_w, L1_ffn_conv_b, L1_ffn_w2):
    import jax
    import jax.numpy as jnp

    def _L0_xattn_ref(x, latents, gamma_media, beta_media, gamma_lat, beta_lat, Wq, bq, Wkv, bkv, Wo, bo):
        import jax, jax.numpy as jnp
        import numpy as np
        B, M, N, DIM, DH, H = (8, 1024, 64, 256, 128, 8)
        INNER = DH * H
        EPS = 1e-05

        def _layernorm(x, g, b):
            mu = jnp.mean(x, axis=-1, keepdims=True)
            var = jnp.var(x, axis=-1, keepdims=True)
            return (x - mu) * jax.lax.rsqrt(var + EPS) * g + b
        b = x.shape[0]
        xn = _layernorm(x, gamma_media, beta_media)
        ln = _layernorm(latents, gamma_lat, beta_lat)
        q = ln @ Wq + bq
        kv_input = jnp.concatenate([xn, ln], axis=1)
        kv = kv_input @ Wkv + bkv
        k, v = jnp.split(kv, 2, axis=-1)

        def to_heads(t):
            return t.reshape(b, t.shape[1], H, DH).transpose(0, 2, 1, 3)
        q, k, v = (to_heads(q), to_heads(k), to_heads(v))
        q = q * DH ** (-0.5)
        sim = jnp.einsum('bhid,bhjd->bhij', q, k)
        attn = jax.nn.softmax(sim, axis=-1)
        out = jnp.einsum('bhij,bhjd->bhid', attn, v)
        out = out.transpose(0, 2, 1, 3).reshape(b, -1, INNER)
        return out @ Wo + bo

    def _L0_ffn_ref(x, router_w, router_b, w1, b1, w2, b2, sw1, sb1, sw2, sb2):
        import jax, jax.numpy as jnp
        import numpy as np
        B, S, D = (4, 128, 256)
        E, K, H = (64, 8, 64)
        ES, HS = (2, 512)
        b_, s_, d_ = x.shape
        xf = x.reshape(-1, d_)
        probs = jax.nn.softmax(xf @ router_w + router_b, axis=-1)
        tw, ti = jax.lax.top_k(probs, K)
        tw = tw / jnp.sum(tw, axis=-1, keepdims=True)

        def body(acc, p):
            W1, B1, W2, B2, e = p
            h = jax.nn.silu(xf @ W1 + B1) @ W2 + B2
            cw = jnp.sum(jnp.where(ti == e, tw, 0.0), axis=-1)
            return (acc + cw[:, None] * h, None)
        routed, _ = jax.lax.scan(body, jnp.zeros_like(xf), (w1, b1, w2, b2, jnp.arange(w1.shape[0])))

        def shared_mlp(W1, B1, W2, B2):
            return jax.nn.silu(xf @ W1 + B1) @ W2 + B2
        shared = jnp.sum(jax.vmap(shared_mlp)(sw1, sb1, sw2, sb2), axis=0)
        return (routed + shared).reshape(b_, s_, d_)

    def _L1_xattn_ref(x, context, Wq, Wk, Wv, Wo, bo):
        import jax, jax.numpy as jnp
        import numpy as np
        HIDDEN = 256
        HEADS = 16
        HEAD_DIM = HIDDEN // HEADS
        SCALE = 1.0 / np.sqrt(HEAD_DIM).astype(np.float32)
        b, t, c = x.shape
        kv_t = context.shape[1]
        q = x @ Wq.T
        k = context @ Wk.T
        v = context @ Wv.T
        q = q.reshape(b, t, HEADS, HEAD_DIM).transpose(0, 2, 1, 3)
        k = k.reshape(b, kv_t, HEADS, HEAD_DIM).transpose(0, 2, 1, 3)
        v = v.reshape(b, kv_t, HEADS, HEAD_DIM).transpose(0, 2, 1, 3)
        scores = jnp.einsum('bhqd,bhkd->bhqk', q, k) * SCALE
        causal = jnp.tril(jnp.ones((t, kv_t), dtype=bool))
        scores = jnp.where(causal[None, None, :, :], scores, -jnp.inf)
        probs = jax.nn.softmax(scores, axis=-1)
        y = jnp.einsum('bhqk,bhkd->bhqd', probs, v)
        y = y.transpose(0, 2, 1, 3).reshape(b, t, c)
        return y @ Wo.T + bo

    def _L1_ffn_ref(x, w1, conv_w, conv_b, w2):
        import jax, jax.numpy as jnp
        import numpy as np
        B, S, D_MODEL, D_HIDDEN = (4, 512, 256, 1024)

        def act_quant(x):
            scale = 127.0 / jnp.clip(jnp.max(jnp.abs(x), axis=-1, keepdims=True), 1e-05)
            return jnp.clip(jnp.round(x * scale), -128, 127) / scale

        def weight_quant(w):
            scale = 1.0 / jnp.clip(jnp.mean(jnp.abs(w)), 1e-05)
            return jnp.clip(jnp.round(w * scale), -1, 1) / scale

        def bit_linear(x, w):
            xq = x + jax.lax.stop_gradient(act_quant(x) - x)
            wq = w + jax.lax.stop_gradient(weight_quant(w) - w)
            return jnp.einsum('bsd,hd->bsh', xq, wq)

        def depthwise_conv1d(x_bcl, w, b):
            y = jax.lax.conv_general_dilated(x_bcl, w, window_strides=(1,), padding=[(1, 1)], dimension_numbers=('NCH', 'OIH', 'NCH'), feature_group_count=x_bcl.shape[1])
            return y + b[None, :, None]
        h = bit_linear(x, w1)
        h = depthwise_conv1d(h.transpose(0, 2, 1), conv_w, conv_b)
        h = h.transpose(0, 2, 1)
        h = jax.nn.silu(h)
        return bit_linear(h, w2)
    x = x + jnp.tanh(g_xattn[0]) * _L0_xattn_ref(ctx_1024, _layernorm(x, axis=-1), L0_xattn_gamma_media, L0_xattn_beta_media, L0_xattn_gamma_lat, L0_xattn_beta_lat, L0_xattn_Wq, L0_xattn_bq, L0_xattn_Wkv, L0_xattn_bkv, L0_xattn_Wo, L0_xattn_bo)
    x = x + jnp.tanh(g_ffn[0]) * _L0_ffn_ref(_layernorm(x, axis=-1), L0_ffn_router_w, L0_ffn_router_b, L0_ffn_w1, L0_ffn_b1, L0_ffn_w2, L0_ffn_b2, L0_ffn_sw1, L0_ffn_sb1, L0_ffn_sw2, L0_ffn_sb2)
    x = x + jnp.tanh(g_xattn[1]) * _L1_xattn_ref(_layernorm(x, axis=-1), ctx_1024, L1_xattn_Wq, L1_xattn_Wk, L1_xattn_Wv, L1_xattn_Wo, L1_xattn_bo)
    x = x + jnp.tanh(g_ffn[1]) * _L1_ffn_ref(_layernorm(x, axis=-1), L1_ffn_w1, L1_ffn_conv_w, L1_ffn_conv_b, L1_ffn_w2)
    return x

_drawn_inputs = setup_inputs


def setup_inputs(seed=0):
    import zlib

    import numpy as np

    out = dict(_drawn_inputs(seed))
    spreads = {'g_ffn': (-1.0, 0.6),
     'L0_xattn_gamma_media': (1.0, 0.6),
     'L0_xattn_beta_media': (0.0, 0.8),
     'L0_xattn_gamma_lat': (1.0, 0.6),
     'L0_xattn_beta_lat': (0.0, 0.55),
     'L0_xattn_bq': (0.0, 0.8),
     'L0_xattn_bkv': (0.0, 0.1),
     'L0_xattn_bo': (0.0, 0.1),
     'L0_ffn_router_b': (0.0, 0.53),
     'L0_ffn_b1': (0.0, 0.8),
     'L0_ffn_b2': (0.0, 0.304),
     'L0_ffn_sb1': (0.0, 0.304),
     'L0_ffn_sb2': (0.0, 0.1),
     'L1_xattn_bo': (0.0, 0.1)}
    factors = {'L0_xattn_Wq': 8.0,
     'L0_xattn_Wkv': 2.968,
     'L0_ffn_w1': 8.0,
     'L0_ffn_w2': 7.608,
     'L1_xattn_Wq': 8.0,
     'L1_xattn_Wk': 8.0}
    for name, (base, spread) in spreads.items():
        noise = np.random.default_rng([zlib.crc32(name.encode()), seed]).standard_normal(out[name].shape)
        drawn = base * np.exp(spread * noise) if base else spread * noise
        out[name] = jnp.asarray(drawn.astype(out[name].dtype))
    for name, factor in factors.items():
        out[name] = (out[name] * factor).astype(out[name].dtype)
    return out
```

```python
from contextlib import ExitStack
import numpy as np
import concourse.bass as bass
from concourse import mybir

F32 = mybir.dt.float32
F32R = mybir.dt.float32r
BF16 = mybir.dt.bfloat16
ACT = mybir.ActivationFunctionType
ALU = mybir.AluOpType
AX = mybir.AxisListType

P = 128
BATCH, SEQ, DIM = 4, 1024, 256
CTX = 154
TOKENS = BATCH * SEQ
TILES = TOKENS // P
KT = DIM // P
CH = 512
CHUNKS = TOKENS // CH
TPC = CH // P
TPB = SEQ // P
EPS = 1e-5


class Chain:

    def __init__(self, eng, sem):
        self.eng, self.sem, self.base, self.k, self.start, self.per = eng, sem, 0, 0, 0, 0

    def step(self, ins):
        ins.then_inc(self.sem, 1)
        self.k += 1
        return self.k

    def wait(self, k=None):
        self.eng.wait_ge(self.sem, self.base + (self.k if k is None else k))

    def link(self, ins):
        self.step(ins)
        self.wait()

    def enter(self, it, per):
        self.start, self.per, self.base, self.k = self.base + self.k, per, it * per + (self.base + self.k), 0

    def leave(self, rounds):
        assert self.k == self.per, (self.k, self.per)
        self.base, self.k = self.start + rounds * self.per, 0


def newton_rsqrt(own, dve, var, root, r):
    own.link(dve.reciprocal(r, root))
    own.link(dve.tensor_tensor(root, r, r, ALU.mult))
    own.link(dve.tensor_tensor(root, root, var, ALU.mult))
    own.link(dve.tensor_scalar(root, root, -0.5, 1.5, ALU.mult, ALU.add))
    own.link(dve.tensor_tensor(r, r, root, ALU.mult))


R_HEADS, R_DH = 8, 128
R_INNER = R_HEADS * R_DH
R_KV = SEQ + CTX
R_BLK = -(-R_KV // P)
R_ROW = R_BLK * P
R_SCALE = float(R_DH) ** -0.5
R_BIG = 3.0e38


def resample_stage(nc, xres, ident, A):
    with ExitStack() as ctx:
        def sb(name, shape, dt=F32):
            return ctx.enter_context(nc.sbuf_tensor("x0_" + name, shape, dt))

        def sem(name):
            return nc.alloc_semaphore("x0_" + name)

        p = sb("p", [P, 4, R_ROW])
        kvf = [p[:, k, 0:R_KV] for k in range(KT)]
        z = [p[:, 2 + t // 4, (t % 4) * DIM:(t % 4 + 1) * DIM] for t in range(TPB)]
        mA, mB = sb("mA", [P, DIM]), sb("mB", [CTX - P, DIM])
        kvh, kvl = sb("kvh", [P, KT, R_KV], F32R), sb("kvl", [P, KT, R_KV], F32R)
        wraw, wh, wl = sb("wraw", [P, 2, 4, DIM]), sb("wh", [P, 2, 4, DIM], F32R), sb("wl", [P, 2, 4, DIM], F32R)
        full = sb("full", [P, 2, CH])
        vf = sb("vf", [P, R_ROW])
        kh, kl = sb("kh", [P, 2, R_KV], F32R), sb("kl", [P, 2, R_KV], F32R)
        qh, ql = sb("qh", [P, 2, SEQ], F32R), sb("ql", [P, 2, SEQ], F32R)
        vh, vl = sb("vh", [P, 2, R_ROW], F32R), sb("vl", [P, 2, R_ROW], F32R)
        pth, ptl = sb("pth", [P, 2, R_BLK, 2 * P], F32R), sb("ptl", [P, 2, R_BLK, 2 * P], F32R)
        oh, ol = sb("oh", [P, 2 * P], F32R), sb("ol", [P, 2 * P], F32R)
        cA, cB = p[:, :, DIM:2 * DIM], p[0:CTX - P, :, 2 * DIM:3 * DIM]
        cols = sb("cols", [P, 4, KT])
        bias = sb("bias", [P, 3, R_HEADS])
        tbo = sb("tbo", [P, DIM])
        tg = sb("tg", [P, 1])
        NST = TILES + 2 * BATCH
        st, mv = sb("st", [P, NST, 6]), sb("mv", [P, NST, 2])
        mv2 = sb("mv2", [P, TILES, 2])
        var, root = sb("var", [P, NST]), sb("root", [P, NST])
        r1, r2 = sb("r1", [P, NST]), sb("r2", [P, TILES])
        nmx, sums, rt = sb("nmx", [P, 2]), sb("sums", [P, 2 * TPB]), sb("rt", [P, 2])
        ps = ctx.enter_context(nc.psum_tensor("x0_ps", [P, 8, CH], F32))
        scores = ps[:, 0:3, :].rearrange("p b c -> p (b c)")[:, 0:R_KV]
        TURN, PV, JOB = 3, 5, 6

        d_c, d_x, d_in, d_wq, d_wo = sem("d_c"), sem("d_x"), sem("d_in"), [sem("d_wq0"), sem("d_wq1")], [sem("d_wo0"), sem("d_wo1")]
        alone_pool, alone_act, alone_pe = sem("alone_pool"), sem("alone_act"), sem("alone_pe")
        batch_sem, it_sem = sem("batch_own"), sem("it_own")
        dve_own, set_up, tanhed, stats, rooted = sem("dve_own"), sem("set_up"), sem("tanhed"), sem("stats"), sem("rooted")
        z_ready, z_turned, z_full, z_split = sem("z_ready"), sem("z_turned"), sem("z_full"), sem("z_split")
        wq_high, wq_split, wo_high, wo_split = (sem(n) for n in ("wq_high", "wq_split", "wo_high", "wo_split"))
        job_done, job_full, job_high, job_low, vt_high, vt_low = (
            sem(n) for n in ("job_done", "job_full", "job_high", "job_low", "vt_high", "vt_low"))
        s_done, s_read, exp_done, turned, hi_done, lo_done = (
            sem(n) for n in ("s_done", "s_read", "exp_done", "turned", "hi_done", "lo_done"))
        pv_done, o_high, o_split, y_done, y_added = (sem(n) for n in ("pv_done", "o_high", "o_split", "y_done", "y_added"))
        block = ctx.enter_context(nc.Block())

        STEPS = 2 * TPB
        UNITS = STEPS // 2
        LAG = 2
        ITERS = R_HEADS // 2
        GRP = ((0, 4), (4, 8), (8, R_BLK))
        CUT = ((0, CH), (CH, 2 * CH), (2 * CH, R_KV))
        JOBS = [("k", *CUT[0]), ("k", *CUT[1]), ("k", *CUT[2]), ("q", *CUT[0]), ("q", *CUT[1]),
                ("v", *CUT[0]), ("v", *CUT[1]), ("v", *CUT[2])] + [("t", lo * P, hi * P) for lo, hi in GRP]
        NF, NS, NV, NJ = 8, 5, 3, len(JOBS)
        PLAN = [[0, 1, 2, 3], [4, 5], [6, 7, 8], [9, 10, 11], [12, 13], [14, 15], [16, 17, 18], [19, 20, 21]]

        @block.sync
        def _(sp):
            xt = A["x"].rearrange("b (t p) d -> p (b t) d", p=P)
            for i in range(4):
                sp.dma_start(xres[:, TPB * i:TPB * (i + 1), :], xt[:, TPB * i:TPB * (i + 1), :]).then_inc(d_x, 16)
            sp.dma_start(cA, A["ctx_1024"][:, 0:P, :].rearrange("b j d -> j b d")).then_inc(d_in, 16)
            sp.dma_start(cB, A["ctx_1024"][:, P:CTX, :].rearrange("b j d -> j b d")).then_inc(d_in, 16)
            sp.dma_start(tbo[:, :], A["L0_xattn_bo"].partition_broadcast(P)).then_inc(d_in, 16)
            with nc.allow_non_contiguous_dma(reason="small columns"):
                sp.dma_start(tg[:, :], A["g_xattn"][0:1].partition_broadcast(P)).then_inc(d_in, 16)
                for i, n in enumerate(("gamma_lat", "beta_lat", "gamma_media", "beta_media")):
                    sp.dma_start(cols[:, i, :], A["L0_xattn_" + n].rearrange("(k p) -> p k", p=P)).then_inc(d_in, 16)
                sp.dma_start(bias[:, 0, :], A["L0_xattn_bq"].rearrange("(h p) -> p h", p=P)).then_inc(d_in, 16)
                sp.dma_start(bias[:, 1:3, :], A["L0_xattn_bkv"].rearrange("(i h p) -> p i h", p=P, i=2)).then_inc(d_in, 16)
            wq = A["L0_xattn_Wq"].rearrange("(k p) n -> p k n", p=P)
            wkv = A["L0_xattn_Wkv"].rearrange("(k p) n -> p k n", p=P)
            wo = A["L0_xattn_Wo"].rearrange("(h p) n -> p h n", p=P)
            with sp.Fori(0, BATCH) as b:
                sp.wait_ge(z_turned, 6 * b + 6)
                sp.dma_start(mA[:, :], A["ctx_1024"][bass.ds(b, 1), 0:P, :].rearrange("b j d -> (b j) d")).then_inc(d_c, 16)
                sp.dma_start(mB[:, :], A["ctx_1024"][bass.ds(b, 1), P:CTX, :].rearrange("b j d -> (b j) d")).then_inc(d_c, 16)
                with sp.Fori(0, ITERS) as hp:
                    it = b * ITERS + hp
                    for j in range(2):
                        h = hp * 2 + j
                        raw = wraw[:, j, :, :].rearrange("p w (k n) -> p w k n", k=KT)
                        sp.wait_ge(wq_split, 2 * it + j + 1)
                        sp.dma_start(raw[:, 0, :, :], wq[:, :, bass.ds(h * P, P)]).then_inc(d_wq[j], 16)
                        sp.dma_start(raw[:, 1, :, :], wkv[:, :, bass.ds(h * P, P)]).then_inc(d_wq[j], 16)
                        sp.dma_start(raw[:, 2, :, :], wkv[:, :, bass.ds(h * P + R_INNER, P)]).then_inc(d_wq[j], 16)
                        sp.wait_ge(wo_split, 2 * it + j + 1)
                        sp.dma_start(wraw[:, j, 3, :], wo[:, bass.ds(h, 1), :]).then_inc(d_wo[j], 16)
        ND = 10

        def split_buffer(kind):
            return {"k": (kh, kl), "q": (qh, ql)}[kind]

        @block.gpsimd
        def _(pool):
            pool.sem_inc(wq_split, 2)
            pool.sem_inc(wo_split, 2)
            pool.sem_inc(job_low, 2)
            for i in range(4):
                pool.memset(p[:, i, R_KV:R_ROW], 0.0).then_inc(set_up, 1)
            pool.memset(vf[:, R_KV:R_ROW], 0.0).then_inc(set_up, 1)

            def alone():
                pool.sem_inc(alone_pool, 1)

            def split_q(it, j):
                pool.wait_ge(job_done, 2 * NJ * it + NJ * j + NF)
                pool.wait_ge(d_wq[j], 48 * (it + 1))
                alone()
                pool.tensor_copy(wh[:, j, 0:3, :], wraw[:, j, 0:3, :]).then_inc(wq_high, 1)
                pool.wait_ge(wq_high, 2 * it + j + 1)
                pool.tensor_tensor(wl[:, j, 0:3, :], wraw[:, j, 0:3, :], wh[:, j, 0:3, :].bitcast(F32), ALU.subtract).then_inc(wq_split, 1)

            def split_o(it, j):
                pool.wait_ge(y_done, UNITS * it + UNITS // 2 * (j + 1))
                pool.wait_ge(d_wo[j], 16 * (it + 1))
                alone()
                pool.tensor_copy(wh[:, j, 3, :], wraw[:, j, 3, :]).then_inc(wo_high, 1)
                pool.wait_ge(wo_high, 2 * it + j + 1)
                pool.tensor_tensor(wl[:, j, 3, :], wraw[:, j, 3, :], wh[:, j, 3, :].bitcast(F32), ALU.subtract).then_inc(wo_split, 1)

            def lows(it):
                for j in range(2):
                    for m in range(NS):
                        kind, lo, hi = JOBS[m]
                        f = 2 * NS * it + NS * j + m
                        h, l = split_buffer(kind)
                        pool.wait_ge(job_high, f + 1)
                        pool.tensor_tensor(l[:, j, lo:hi], full[:, (NS * j + m) % 2, 0:hi - lo], h[:, j, lo:hi].bitcast(F32),
                                           ALU.subtract).then_inc(job_low, 1)
                    split_o(it, j)

            split_q(0, 0)
            split_q(0, 1)
            with pool.Fori(0, BATCH * ITERS - 1) as it:
                lows(it)
                split_q(it + 1, 0)
                split_q(it + 1, 1)
            lows(BATCH * ITERS - 1)

        @block.scalar
        def _(act):
            act.wait_ge(d_in, 16 * ND)
            act.activation(tg[:, :], tg[:, :], ACT.Tanh).then_inc(tanhed, 1)
            act.wait_ge(stats, 1)
            act.activation(root[:, :], var[:, :], ACT.Sqrt).then_inc(rooted, 1)
            act.wait_ge(stats, 2)
            act.activation(root[:, 0:TILES], var[:, 0:TILES], ACT.Sqrt).then_inc(rooted, 1)
            act.wait_ge(tanhed, 2)
            with act.Fori(0, BATCH) as b:
                for n, (k, (lo, hi)) in enumerate((k, c) for k in range(KT) for c in CUT):
                    g = 0 if hi <= SEQ else 2
                    act.wait_ge(z_turned, 6 * b + n + 1 + 6)
                    act.activation(kvf[k][:, lo:hi], ps[:, n, 0:hi - lo], ACT.Identity, bias=cols[:, g + 1, k:k + 1],
                                   scale=cols[:, g, k:k + 1]).then_inc(z_full, 1)
                with act.Fori(0, ITERS) as hp:
                    it = b * ITERS + hp

                    def job(j, m):
                        kind, lo, hi = JOBS[m]
                        M = 2 * NJ * it + NJ * j + m
                        bank = ps[:, JOB + (NJ * j + m) % 2, 0:hi - lo]
                        act.wait_ge(job_done, M + 1 + 2 * NJ)
                        if kind == "t":
                            act.activation(vh[:, j, lo:hi], bank, ACT.Copy).then_inc(vt_high, 1)
                            return
                        if kind != "v":
                            act.wait_ge(job_low, 2 * NS * it + NS * j + m + 1)
                        dst = vf[:, lo:hi] if kind == "v" else full[:, (NS * j + m) % 2, 0:hi - lo]
                        i = "qkv".index(kind)
                        act.sem_inc(alone_act, 1)
                        act.activation(dst, bank, ACT.Identity, bias=bias[:, i, bass.ds(hp * 2 + j, 1)],
                                       scale=R_SCALE if kind == "q" else 1.0).then_inc(job_full, 1)

                    for w in range(STEPS + LAG + 2):
                        for m in PLAN[w] if w < len(PLAN) else ():
                            job(m // NJ, m % NJ)
                        if LAG <= w < STEPS + LAG:
                            v = w - LAG
                            for g, (lo, hi) in enumerate(GRP):
                                G = 3 * (STEPS * it + v) + g
                                act.wait_ge(turned, G + 1 + 12)
                                act.activation(pth[:, (v // 2) % 2, lo:hi, (v % 2) * P:(v % 2 + 1) * P],
                                               ps[:, TURN + (v + g) % 2, 0:(hi - lo) * P].rearrange("p (n t) -> p n t", t=P),
                                               ACT.Copy).then_inc(hi_done, 1)
                        y = w - LAG - 2
                        if y >= 0 and y % 2 == 0:
                            act.wait_ge(pv_done, UNITS * it + y // 2 + 1)
                            act.activation(oh[:, :], ps[:, PV, 0:2 * P], ACT.Copy).then_inc(o_high, 1)
                        if w < STEPS:
                            act.wait_ge(s_read, STEPS * it + w + 1 + 1)
                            act.activation(p[:, w % 4, 0:R_KV], p[:, w % 4, 0:R_KV], ACT.Exp, bias=nmx[:, w % 2:w % 2 + 1], scale=-1.0,
                                           accum_out=sums[:, w:w + 1]).then_inc(exp_done, 1)

        @block.vector
        def _(dve):
            own = Chain(dve, dve_own)
            dve.sem_inc(s_read, 1)
            dve.sem_inc(lo_done, 2)
            dve.sem_inc(y_added, 1)
            dve.sem_inc(vt_low, 2 * NV)
            own.link(dve.memset(mv[:, :, :], 1.0))
            dve.wait_ge(d_in, 16 * ND)
            for b in range(BATCH):
                own.step(dve.bn_stats(st[:, TILES + b, :], p[:, b, DIM:2 * DIM]))
                own.step(dve.bn_stats(st[0:CTX - P, TILES + BATCH + b, :], p[0:CTX - P, b, 2 * DIM:3 * DIM]))
            for t in range(TILES):
                if t % TPB == 0:
                    dve.wait_ge(d_x, 16 * BATCH)
                own.step(dve.bn_stats(st[:, t, :], xres[:, t, :]))
            own.wait()
            for n in range(NST):
                rows = slice(0, P) if n < TILES + BATCH else slice(0, CTX - P)
                own.step(dve.bn_aggr(mv[rows, n, :], st[rows, n, :]))
            own.wait()
            dve.tensor_scalar(var[:, :], mv[:, :, 1], EPS, None, ALU.add).then_inc(stats, 1)
            dve.wait_ge(rooted, 1)
            newton_rsqrt(own, dve, var[:, :], root[:, :], r1[:, :])
            for t in range(TILES):
                once = p[:, t % 4, 0:DIM]
                if t >= 4:
                    own.wait(own.k - 6)
                own.link(dve.tensor_scalar(once, xres[:, t, :], mv[:, t, 0:1], r1[:, t:t + 1], ALU.subtract, ALU.mult))
                own.step(dve.bn_stats(st[:, t, :], once))
            own.wait()
            for t in range(TILES):
                own.step(dve.bn_aggr(mv2[:, t, :], st[:, t, :]))
            own.wait()
            dve.tensor_scalar(var[:, 0:TILES], mv2[:, :, 1], EPS, None, ALU.add).then_inc(stats, 1)
            dve.wait_ge(rooted, 2)
            newton_rsqrt(own, dve, var[:, 0:TILES], root[:, 0:TILES], r2[:, :])
            dve.wait_ge(tanhed, 1)
            own.link(dve.tensor_scalar(tbo[:, :], tbo[:, :], tg[:, 0:1], None, ALU.mult))
            dve.tensor_scalar(bias[:, 0, :], bias[:, 0, :], R_SCALE, None, ALU.mult).then_inc(tanhed, 1)
            dve.wait_ge(set_up, 5)

            PREP, PER = TPB + 6, 2 * UNITS
            batch_own, it_own = Chain(dve, batch_sem), Chain(dve, it_sem)
            with dve.Fori(0, BATCH) as b:
                own = batch_own
                own.enter(b, PREP)
                for t in range(TPB):
                    n = TPB * b + t
                    own.step(dve.tensor_scalar(z[t], xres[:, bass.ds(n, 1), :], mv[:, bass.ds(n, 1), 0], r1[:, bass.ds(n, 1)],
                                               ALU.subtract, ALU.mult))
                dve.wait_ge(d_c, 32 * (b + 1))
                for m, rows, at in ((mA, slice(0, P), TILES), (mB, slice(0, CTX - P), TILES + BATCH)):
                    dve.tensor_scalar(m[:, :], m[:, :], mv[rows, bass.ds(b + at, 1), 0], r1[rows, bass.ds(b + at, 1)],
                                      ALU.subtract, ALU.mult).then_inc(z_ready, 1)
                own.wait()
                for t in range(TPB):
                    n = TPB * b + t
                    dve.tensor_scalar(z[t], z[t], mv2[:, bass.ds(n, 1), 0], r2[:, bass.ds(n, 1)],
                                      ALU.subtract, ALU.mult).then_inc(z_ready, 1)
                part = xres[:, bass.ds(TPB * b, TPB), :]
                dve.tensor_tensor(part, part, tbo[:, :].unsqueeze(1).broadcast_to([P, TPB, DIM]), ALU.add)
                for n, (k, (lo, hi)) in enumerate((k, c) for k in range(KT) for c in CUT):
                    dve.wait_ge(z_full, 6 * b + n + 1)
                    own.link(dve.tensor_copy(kvh[:, k, lo:hi], kvf[k][:, lo:hi]))
                    dve.tensor_tensor(kvl[:, k, lo:hi], kvf[k][:, lo:hi], kvh[:, k, lo:hi].bitcast(F32), ALU.subtract).then_inc(z_split, 1)
                own.leave(BATCH)
                own = it_own
                with dve.Fori(0, ITERS) as hp:
                    it = b * ITERS + hp
                    own.enter(it, PER)

                    def job(j, m):
                        kind, lo, hi = JOBS[m]
                        if kind == "t":
                            dve.wait_ge(vt_high, 2 * NV * it + NV * j + m - NF + 1)
                            dve.tensor_tensor(vl[:, j, lo:hi], ps[:, JOB + (NJ * j + m) % 2, 0:hi - lo], vh[:, j, lo:hi].bitcast(F32),
                                              ALU.subtract).then_inc(vt_low, 1)
                        elif kind != "v":
                            h, l = split_buffer(kind)
                            dve.wait_ge(job_full, 2 * NF * it + NF * j + m + 1)
                            dve.tensor_copy(h[:, j, lo:hi], full[:, (NS * j + m) % 2, 0:hi - lo]).then_inc(job_high, 1)

                    def lows(v, gs):
                        for g in gs:
                            lo, hi = GRP[g]
                            dve.wait_ge(hi_done, 3 * (STEPS * it + v) + g + 1)
                            dst = (slice(None), (v // 2) % 2, slice(lo, hi), slice((v % 2) * P, (v % 2 + 1) * P))
                            dve.tensor_tensor(ptl[dst], ps[:, TURN + (v + g) % 2, 0:(hi - lo) * P].rearrange("p (n t) -> p n t", t=P),
                                              pth[dst].bitcast(F32), ALU.subtract).then_inc(lo_done, 1)

                    for w in range(STEPS + LAG + 2):
                        W = STEPS * it + w
                        for m in PLAN[w] if w < len(PLAN) else ():
                            job(m // NJ, m % NJ)
                        if LAG <= w < STEPS + LAG:
                            lows(w - LAG, (0, 1))
                        if w < STEPS:
                            dve.wait_ge(s_done, W + 1)
                            dve.wait_ge(turned, 3 * W + 3)
                            dve.tensor_scalar(p[:, w % 4, 0:R_KV], scores, -1.0, R_BIG, ALU.mult, ALU.min,
                                              accum_out=nmx[:, w % 2:w % 2 + 1]).then_inc(s_read, 1)
                        if LAG <= w < STEPS + LAG:
                            lows(w - LAG, (2,))
                        y = w - LAG - 2
                        if y >= 0 and y % 2 == 0:
                            dve.wait_ge(o_high, UNITS * it + y // 2 + 1)
                            dve.tensor_tensor(ol[:, :], ps[:, PV, 0:2 * P], oh[:, :].bitcast(F32), ALU.subtract).then_inc(o_split, 1)
                        y = w - LAG - 3
                        if y >= 0 and y % 2 == 0:
                            u = y // 2
                            t = 2 * (u % (UNITS // 2))
                            own.link(dve.reciprocal(rt[:, :], sums[:, 2 * u:2 * u + 2]))
                            own.link(dve.tensor_scalar(rt[:, :], rt[:, :], tg[:, 0:1], None, ALU.mult))
                            dve.wait_ge(y_done, UNITS * it + u + 1 + UNITS)
                            for i in range(2):
                                part = xres[:, bass.ds(TPB * b + t + i, 1), :].rearrange("p a d -> p (a d)")
                                last = dve.scalar_tensor_tensor(part, ps[:, PV, i * DIM:(i + 1) * DIM], rt[:, i:i + 1], part,
                                                                ALU.mult, ALU.add)
                            last.then_inc(y_added, 1)
                    own.leave(BATCH * ITERS)

        @block.tensor
        def _(pe):
            pe.sem_inc(job_done, 2 * NJ)
            pe.sem_inc(y_done, UNITS)
            pe.sem_inc(z_turned, 6)
            pe.sem_inc(turned, 12)
            with pe.Fori(0, BATCH) as b:
                pe.wait_ge(z_ready, (TPB + 2) * (b + 1))
                pe.wait_ge(s_read, STEPS * ITERS * b + 1)
                pe.wait_ge(lo_done, 3 * STEPS * ITERS * b + 2)
                pe.wait_ge(y_added, UNITS * ITERS * b + 1)
                for n, (k, (lo, hi)) in enumerate((k, c) for k in range(KT) for c in CUT):
                    cut = slice(k * P, (k + 1) * P)
                    if hi <= SEQ:
                        for t in range(lo // P, hi // P):
                            last = pe.transpose(ps[:, n, t * P - lo:(t + 1) * P - lo], z[t][:, cut], ident[:, :])
                    else:
                        pe.transpose(ps[:, n, 0:P], mA[:, cut], ident[:, :])
                        last = pe.transpose(ps[:, n, P:CTX], mB[:, cut], ident[0:CTX - P, 0:CTX - P])
                    last.then_inc(z_turned, 1)
                pe.wait_ge(z_split, 6 * (b + 1))
                pe.sem_inc(alone_pe, 1)
                with pe.Fori(0, ITERS) as hp:
                    it = b * ITERS + hp

                    def job(j, m):
                        kind, lo, hi = JOBS[m]
                        n = NJ * j + m
                        bank = ps[:, JOB + n % 2, :]
                        if n < 2:
                            pe.wait_ge(vt_low, 2 * NV * it + 2 * NV - 1 + n)
                        else:
                            pj, pm = (n - 2) // NJ, (n - 2) % NJ
                            if JOBS[pm][0] == "t":
                                pe.wait_ge(vt_low, 2 * NV * it + NV * pj + pm - NF + 1 + 2 * NV)
                            else:
                                pe.wait_ge(job_full, 2 * NF * it + NF * pj + pm + 1)
                        if m == 0:
                            pe.wait_ge(wq_split, 2 * it + j + 1 + 2)
                        if kind == "t":
                            if m == NF:
                                pe.wait_ge(job_full, 2 * NF * it + NF * (j + 1))
                            for c in range(lo, hi, P):
                                last = pe.transpose(bank[:, c - lo:c - lo + P], vf[:, c:c + P], ident[:, :])
                        else:
                            i = "qkv".index(kind)
                            s = 0
                            for k in range(KT):
                                for w, x in ((wh, kvh), (wh, kvl), (wl, kvh)):
                                    last = pe.matmul(bank[:, 0:hi - lo], w[:, j, i, k * P:(k + 1) * P], x[:, k, lo:hi],
                                                     start=(s == 0), stop=(s == 5))
                                    s += 1
                        last.then_inc(job_done, 1)

                    def turn(v, gs):
                        V = STEPS * it + v
                        for g in gs:
                            lo, hi = GRP[g]
                            if g == 0:
                                pe.wait_ge(exp_done, V + 1)
                            pe.wait_ge(lo_done, 3 * V + g + 1)
                            for n in range(lo, hi):
                                last = pe.transpose(ps[:, TURN + (v + g) % 2, (n - lo) * P:(n - lo + 1) * P],
                                                    p[:, v % 4, n * P:(n + 1) * P], ident[:, :])
                            last.then_inc(turned, 1)

                    def score(w):
                        j, t = w // TPB, w % TPB
                        pe.wait_ge(s_read, STEPS * it + w + 1)
                        if t in (0, TPB // 2):
                            pe.wait_ge(job_low, 2 * NS * it + NS * j + (NS - 1 if t == 0 else NS) + 2)
                        for n, (lo, hi) in enumerate(CUT):
                            for i, (q, k) in enumerate(((qh, kh), (qh, kl), (ql, kh))):
                                last = pe.matmul(ps[:, n, 0:hi - lo], q[:, j, t * P:(t + 1) * P], k[:, j, lo:hi],
                                                 start=(i == 0), stop=(i == 2))
                        last.then_inc(s_done, 1)

                    def values(u):
                        j = u // (UNITS // 2)
                        if u % (UNITS // 2) == 0:
                            pe.wait_ge(vt_low, 2 * NV * it + NV * (j + 1) + 2 * NV)
                        pe.wait_ge(lo_done, 6 * (UNITS * it + u + 1) + 2)
                        pe.wait_ge(y_added, UNITS * it + u + 1)
                        for n in range(R_BLK):
                            for i, (v, x) in enumerate(((vh, pth), (vh, ptl), (vl, pth))):
                                last = pe.matmul(ps[:, PV, 0:2 * P], v[:, j, n * P:(n + 1) * P], x[:, u % 2, n, :],
                                                 start=(n == 0 and i == 0), stop=(n == R_BLK - 1 and i == 2))
                        last.then_inc(pv_done, 1)

                    def project(u):
                        j = u // (UNITS // 2)
                        if u % (UNITS // 2) == 0:
                            pe.wait_ge(wo_split, 2 * it + j + 1 + 2)
                        pe.wait_ge(o_split, UNITS * it + u + 1)
                        for t in range(2):
                            for i, (o, w) in enumerate(((oh, wh), (oh, wl), (ol, wh))):
                                last = pe.matmul(ps[:, PV, t * DIM:(t + 1) * DIM], o[:, t * P:(t + 1) * P], w[:, j, 3, :],
                                                 start=(i == 0), stop=(i == 2))
                        last.then_inc(y_done, 1)

                    for w in range(STEPS + LAG + 2):
                        for m in PLAN[w] if w < len(PLAN) else ():
                            job(m // NJ, m % NJ)
                        if LAG <= w < STEPS + LAG:
                            turn(w - LAG, (0, 1))
                        if w < STEPS:
                            score(w)
                        if LAG <= w < STEPS + LAG:
                            turn(w - LAG, (2,))
                        y = w - LAG - 2
                        if y >= 0 and y % 2 == 0:
                            values(y // 2)
                        y = w - LAG - 3
                        if y >= 0 and y % 2 == 0:
                            project(y // 2)


EXPERTS, TOPK, EH = 64, 8, 64
SHARED, SH = 2, 512
PAIRS = EXPERTS * EH // P
GB = 8
ROUTED = PAIRS // GB
GROUPS = ROUTED + SHARED * SH // P // GB
FREE = 2


def moe_stage(nc, xres, ident, A):
    with ExitStack() as ctx:
        def sb(name, shape, dt=F32):
            return ctx.enter_context(nc.sbuf_tensor("moe_" + name, shape, dt))

        def sem(name):
            return nc.alloc_semaphore("moe_" + name)

        lnT = sb("lnT", [P, KT, TOKENS])
        cwT = sb("cwT", [P, TOKENS], F32R)
        pick = sb("pick", [P, EXPERTS, EH], F32R)
        w1r, w2r = sb("w1r", [P, KT, GB * P]), sb("w2r", [P, GB, DIM])
        w1h, w1l = sb("w1h", [P, KT, GB * P], F32R), sb("w1l", [P, KT, GB * P], F32R)
        w2h, w2l = sb("w2h", [P, GB, DIM], F32R), sb("w2l", [P, GB, DIM], F32R)
        xh, xl = sb("xh", [P, 2, KT, CH], F32R), sb("xl", [P, 2, KT, CH], F32R)
        sil, gf = sb("sil", [P, 2, CH]), sb("gf", [P, 2, CH])
        gh, gl = sb("gh", [P, 2, CH], F32R), sb("gl", [P, 2, CH], F32R)
        stage = sb("stage", [P, KT, CH])
        rw, rb = sb("rw", [P, KT, EXPERTS]), sb("rb", [P, EXPERTS])
        b1, sb1 = sb("b1", [P, PAIRS]), sb("sb1", [P, GB])
        b2r, b2h, b2l = sb("b2r", [P, DIM]), sb("b2h", [P, DIM], F32R), sb("b2l", [P, DIM], F32R)
        sb2 = sb("sb2", [P, SHARED, KT])
        tg, tsb2 = sb("tg", [P, 1]), sb("tsb2", [P, KT])
        st, mv, rstd = sb("st", [P, TILES, 6]), sb("mv", [P, TILES, 2]), sb("rstd", [P, TILES])
        var, root = sb("var", [P, TILES]), sb("root", [P, TILES])
        lg, pr, rep = (sb(n, [P, TPC, EXPERTS]) for n in ("lg", "pr", "rep"))
        s4 = sb("s4", [P, TPC])
        top = sb("top", [P, TPC, TOPK])
        cwp = sb("cwp", [P, TPC, 2, EXPERTS], F32R)
        xn = sil[:, :, :].rearrange("p a c -> p (a c)").rearrange("p (t d) -> p t d", d=DIM)
        ps = ctx.enter_context(nc.psum_tensor("moe_ps", [P, 8, CH], F32))
        HID, REP, OUT, TURN = 0, 2, 4, 6

        d_const, d_w, w_high, w_split = sem("d_const"), sem("d_w"), sem("w_high"), sem("w_split")
        dve_own, act_own, pool_own = sem("dve_own"), sem("act_own"), sem("pool_own")
        alone_pool, alone_dve = sem("alone_pool"), sem("alone_dve")
        stats, rooted = sem("stats"), sem("rooted")
        pick_set, consts, b2_split = sem("pick_set"), sem("consts"), sem("b2_split")
        normed, turned, staged, routed, shifted, exped = (
            sem(n) for n in ("normed", "turned", "staged", "routed", "shifted", "exped"))
        cw_ready, cw_turned, cw_kept = sem("cw_ready"), sem("cw_turned"), sem("cw_kept")
        x_free, x_high, x_split = sem("x_free"), sem("x_high"), sem("x_split")
        hid_done, rep_done, silu_done, gate_done, high_done, g_split = (
            sem(n) for n in ("hid_done", "rep_done", "silu_done", "gate_done", "high_done", "g_split"))
        out_done, y_kept, y_turned, y_added = sem("out_done"), sem("y_kept"), sem("y_turned"), sem("y_added")
        block = ctx.enter_context(nc.Block())
        NCONST = 9

        @block.sync
        def _(sp):
            for dst, src in ((rw[:, :, :], A["L0_ffn_router_w"].rearrange("(k p) e -> p k e", p=P)),
                             (rb[:, :], A["L0_ffn_router_b"].partition_broadcast(P)),
                             (tg[:, :], A["g_ffn"][0:1].partition_broadcast(P)),
                             (b2r[0:EXPERTS, :], A["L0_ffn_b2"]), (b2r[EXPERTS:P, :], A["L0_ffn_b2"]),
                             (sb1[:, :], A["L0_ffn_sb1"].rearrange("s (b p) -> p (s b)", p=P)),
                             (sb2[:, 0, :], A["L0_ffn_sb2"][0].rearrange("(k p) -> p k", p=P)),
                             (sb2[:, 1, :], A["L0_ffn_sb2"][1].rearrange("(k p) -> p k", p=P)),
                             (b1[:, :], A["L0_ffn_b1"].rearrange("(q e) h -> (e h) q", e=2))):
                with nc.allow_non_contiguous_dma(reason='small columns'):
                    sp.dma_start(dst, src).then_inc(d_const, 16)
            for g in range(GROUPS):
                if g:
                    sp.wait_ge(w_split, 2 * g)
                for k in range(KT):
                    if g < ROUTED:
                        e = slice(2 * GB * g, 2 * GB * (g + 1))
                        src = A["L0_ffn_w1"][e, k * P:(k + 1) * P, :]
                    else:
                        src = A["L0_ffn_sw1"][:, k * P:(k + 1) * P, :]
                    sp.dma_start(w1r[:, k, :].rearrange("p (e h) -> p e h", h=src.shape[2]),
                                 src.rearrange("e p h -> p e h")).then_inc(d_w, 16)
                if g < ROUTED:
                    src = A["L0_ffn_w2"][e].rearrange("(q e) h d -> (e h) q d", e=2)
                else:
                    src = A["L0_ffn_sw2"].rearrange("s (b p) d -> p (s b) d", p=P)
                sp.dma_start(w2r[:, :, :], src).then_inc(d_w, 16)

        @block.gpsimd
        def _(pool):
            own = Chain(pool, pool_own)
            pool.sem_inc(x_free, FREE)
            one = lnT[:, 0, :].rearrange("p (e h) -> p e h", h=EH)
            own.link(pool.memset(one, 0.0))
            for part in (0, EXPERTS):
                own.link(pool.affine_select(out=one, in_=one, compare_op=ALU.not_equal, fill=1.0, base=-part,
                                            pattern=[[-1, EXPERTS], [0, EH]], channel_multiplier=1))
            pool.tensor_copy(pick[:, :, :], one).then_inc(pick_set, 1)
            pool.wait_ge(cw_kept, CHUNKS)
            for g in range(GROUPS):
                with pool.Fori(0, CHUNKS // 2) as cc:
                    for j in range(2):
                        n = g * CHUNKS + 2 * cc + j
                        src = lnT[:, :, bass.ds((2 * cc + j) * CH, CH)]
                        pool.wait_ge(x_free, n + 1)
                        pool.tensor_copy(xh[:, j, :, :], src).then_inc(x_high, 1)
                        pool.wait_ge(x_high, n + 1)
                        pool.sem_inc(alone_pool, 1)
                        pool.tensor_tensor(xl[:, j, :, :], src, xh[:, j, :, :].bitcast(F32), ALU.subtract).then_inc(x_split, 1)

        @block.scalar
        def _(act):
            own = Chain(act, act_own)
            act.sem_inc(silu_done, FREE)
            act.sem_inc(y_kept, FREE)
            act.wait_ge(d_const, 16 * NCONST)
            act.activation(tg[:, :], tg[:, :], ACT.Tanh).then_inc(consts, 1)
            act.wait_ge(pick_set, 1)
            act.wait_ge(stats, 1)
            act.activation(root[:, :], var[:, :], ACT.Sqrt).then_inc(rooted, 1)
            with act.Fori(0, CHUNKS) as c:
                for k in range(KT):
                    act.wait_ge(turned, 2 * c + k + 1)
                    act.activation(stage[:, k, :], ps[:, k, :], ACT.Copy).then_inc(staged, 1)
                for k in range(KT):
                    act.activation(lnT[:, k, bass.ds(c * CH, CH)], ps[:, k, :], ACT.Copy).then_inc(staged, 1)
                act.wait_ge(shifted, c + 1)
                act.activation(pr[:, :, :], lg[:, :, :], ACT.Exp).then_inc(exped, 1)
                act.wait_ge(cw_turned, c + 1)
                act.activation(cwT[:, bass.ds(c * CH, CH)], ps[:, 3, :], ACT.Copy).then_inc(cw_kept, 1)
            for g in range(GROUPS):
                act.wait_ge(d_w, 48 * (g + 1))
                if g:
                    act.wait_ge(out_done, g * CHUNKS * GB + FREE)
                act.activation(w1h[:, :, :], w1r[:, :, :], ACT.Copy).then_inc(w_high, 1)
                act.activation(w2h[:, :, :], w2r[:, :, :], ACT.Copy).then_inc(w_high, 1)
                act.wait_ge(consts, 2)
                with act.Fori(0, CHUNKS // 2) as cc:
                    for j in range(2):
                        n = g * CHUNKS + 2 * cc + j
                        for q in range(GB):
                            u = n * GB + q
                            act.wait_ge(hid_done, u + 1)
                            if g < ROUTED:
                                act.wait_ge(gate_done, u + 1)
                                dst, bias = sil, b1[:, g * GB + q:g * GB + q + 1]
                            else:
                                act.wait_ge(g_split, u + 1)
                                dst, bias = gf, sb1[:, q:q + 1]
                            act.activation(dst[:, q % 2, :], ps[:, HID + q % 2, :], ACT.Silu, bias=bias).then_inc(silu_done, 1)
                        act.wait_ge(out_done, GB * n + GB + FREE)
                        act.wait_ge(y_turned, 2 * n + FREE)
                        for k in range(KT):
                            bias = tsb2[:, k:k + 1] if g == GROUPS - 1 else 0.0
                            act.activation(stage[:, k, :], ps[:, OUT + k, :], ACT.Identity, bias=bias,
                                           scale=tg[:, 0:1]).then_inc(y_kept, 1)

        @block.vector
        def _(dve):
            own = Chain(dve, dve_own)
            dve.sem_inc(gate_done, FREE)
            dve.sem_inc(g_split, FREE)
            dve.sem_inc(y_added, FREE)
            dve.wait_ge(consts, 1)
            own.link(dve.tensor_tensor(tsb2[:, :], sb2[:, 0, :], sb2[:, 1, :], ALU.add))
            dve.tensor_scalar(tsb2[:, :], tsb2[:, :], tg[:, 0:1], None, ALU.mult).then_inc(consts, 1)
            own.link(dve.tensor_copy(b2h[:, :], b2r[:, :]))
            dve.tensor_tensor(b2l[:, :], b2r[:, :], b2h[:, :].bitcast(F32), ALU.subtract).then_inc(b2_split, 1)

            def over(x, n=EXPERTS):
                return x.unsqueeze(2).broadcast_to([P, TPC, n])

            for t in range(TILES):
                own.step(dve.bn_stats(st[:, t, :], xres[:, t, :]))
            own.wait()
            for t in range(TILES):
                own.step(dve.bn_aggr(mv[:, t, :], st[:, t, :]))
            own.wait()
            dve.tensor_scalar(var[:, :], mv[:, :, 1], EPS, None, ALU.add).then_inc(stats, 1)
            dve.wait_ge(rooted, 1)
            newton_rsqrt(own, dve, var[:, :], root[:, :], rstd[:, :])

            PER = 16
            with dve.Fori(0, CHUNKS) as c:
                own.enter(c, PER)
                for t in range(TPC):
                    dve.tensor_scalar(xn[:, t, :], xres[:, bass.ds(c * TPC + t, 1), :], mv[:, bass.ds(c * TPC + t, 1), 0],
                                      rstd[:, bass.ds(c * TPC + t, 1)],
                                      ALU.subtract, ALU.mult).then_inc(normed, 1)
                dve.wait_ge(routed, c + 1)
                logits = ps[:, 2, 0:TPC * EXPERTS].rearrange("p (t e) -> p t e", e=EXPERTS)
                own.link(dve.tensor_tensor(lg[:, :, :], logits, rb[:, :].unsqueeze(1).broadcast_to([P, TPC, EXPERTS]), ALU.add))
                own.link(dve.tensor_reduce(s4[:, :], lg[:, :, :], AX.X, ALU.max))
                dve.tensor_tensor(lg[:, :, :], lg[:, :, :], over(s4[:, :]), ALU.subtract).then_inc(shifted, 1)
                dve.wait_ge(exped, c + 1)
                own.link(dve.tensor_reduce(s4[:, :], pr[:, :, :], AX.X, ALU.add))
                own.link(dve.reciprocal(s4[:, :], s4[:, :]))
                own.link(dve.tensor_tensor(pr[:, :, :], pr[:, :, :], over(s4[:, :]), ALU.mult))
                dve.sem_inc(alone_dve, 1)
                for t in range(TPC):
                    k = own.step(dve.max(top[:, t, :], pr[:, t, :]))
                own.wait()
                dve.sem_inc(alone_dve, 1)
                for t in range(TPC):
                    last = dve.match_replace(rep[:, t, :], top[:, t, :], pr[:, t, :], -1.0)
                    if t == TPC - 1:
                        own.link(last)
                own.link(dve.tensor_tensor(rep[:, :, :], rep[:, :, :], pr[:, :, :], ALU.not_equal))
                own.link(dve.tensor_tensor(pr[:, :, :], pr[:, :, :], rep[:, :, :], ALU.mult))
                own.link(dve.tensor_reduce(s4[:, :], pr[:, :, :], AX.X, ALU.add))
                own.link(dve.reciprocal(s4[:, :], s4[:, :]))
                own.link(dve.tensor_tensor(rep[:, :, :], pr[:, :, :], over(s4[:, :]), ALU.mult))
                own.link(dve.tensor_copy(cwp[:, :, 0, :], rep[:, :, :]))
                dve.tensor_tensor(cwp[:, :, 1, :], rep[:, :, :], cwp[:, :, 0, :].bitcast(F32), ALU.subtract).then_inc(cw_ready, 1)
                own.leave(CHUNKS)

            def add_y(n, c):
                for b in range(2):
                    dve.wait_ge(y_turned, 2 * n + b + 1 + FREE)
                    part = xres[:, bass.ds(c * TPC + 2 * b, 2), :].rearrange("p t d -> p (t d)")
                    dve.tensor_tensor(part, part, ps[:, TURN + b, :], ALU.add).then_inc(y_added, 1)

            for g in range(GROUPS):
                for i, (r, h, l) in enumerate(((w1r, w1h, w1l), (w2r, w2h, w2l))):
                    dve.wait_ge(w_high, 2 * g + i + 1)
                    if g and i == 0:
                        dve.wait_ge(out_done, g * CHUNKS * GB + FREE)
                    dve.tensor_tensor(l[:, :, :], r[:, :, :], h[:, :, :].bitcast(F32), ALU.subtract).then_inc(w_split, 1)
                with dve.Fori(0, CHUNKS // 2) as cc:
                    for j in range(2):
                        n = g * CHUNKS + 2 * cc + j
                        for q in range(GB):
                            u = n * GB + q
                            dve.wait_ge(silu_done, u + 1 + FREE)
                            if g < ROUTED:
                                dve.wait_ge(rep_done, u + 1)
                                dve.tensor_tensor(gf[:, q % 2, :], sil[:, q % 2, :], ps[:, REP + q % 2, :], ALU.mult).then_inc(gate_done, 1)
                                dve.wait_ge(gate_done, u + 1 + FREE)
                            dve.wait_ge(out_done, u + 1)
                            dve.tensor_copy(gh[:, q % 2, :], gf[:, q % 2, :]).then_inc(high_done, 1)
                            dve.wait_ge(high_done, u + 1)
                            dve.tensor_tensor(gl[:, q % 2, :], gf[:, q % 2, :], gh[:, q % 2, :].bitcast(F32),
                                              ALU.subtract).then_inc(g_split, 1)
                            if j == 1 and q == 1:
                                add_y(n - 1, 2 * cc)
                    add_y(n, 2 * cc + 1)

        @block.tensor
        def _(pe):
            pe.sem_inc(out_done, FREE)
            pe.sem_inc(y_turned, FREE)
            pe.wait_ge(d_const, 16 * NCONST)
            with pe.Fori(0, CHUNKS) as c:
                for t in range(TPC):
                    pe.wait_ge(normed, TPC * c + t + 1)
                for k in range(KT):
                    for t in range(TPC):
                        last = pe.transpose(ps[:, k, t * P:(t + 1) * P], xn[:, t, k * P:(k + 1) * P], ident[:, :])
                    last.then_inc(turned, 1)
                pe.wait_ge(staged, 4 * c + 2)
                for t in range(TPC):
                    for k in range(KT):
                        last = pe.matmul(ps[:, 2, t * EXPERTS:(t + 1) * EXPERTS], stage[:, k, t * P:(t + 1) * P], rw[:, k, :],
                                         start=(k == 0), stop=(k == KT - 1))
                last.then_inc(routed, 1)
                pe.wait_ge(cw_ready, c + 1)
                for t in range(TPC):
                    last = pe.transpose(ps[:, 3, t * P:(t + 1) * P],
                                        cwp[:, t, :, :].bitcast(F32).rearrange("p a e -> p (a e)"), ident[:, :])
                last.then_inc(cw_turned, 1)
                pe.wait_ge(staged, 4 * c + 4)
                pe.wait_ge(cw_kept, c + 1)
            pe.wait_ge(b2_split, 1)
            pe.wait_ge(pick_set, 1)

            def hidden(g, n, j, q, cw):
                u = n * GB + q
                if g < ROUTED:
                    pe.wait_ge(gate_done, u + 1)
                    e = 2 * (g * GB + q)
                    pe.matmul(ps[:, REP + q % 2, :], pick[:, e:e + 2, :].rearrange("p e h -> p (e h)"), cw,
                              start=True, stop=True).then_inc(rep_done, 1)
                pe.wait_ge(silu_done, u + 1)
                if q == 0:
                    pe.wait_ge(x_split, n + 1)
                i = 0
                for k in range(KT):
                    for w, x in ((w1h, xh), (w1h, xl), (w1l, xh)):
                        last = pe.matmul(ps[:, HID + q % 2, :], w[:, k, q * P:(q + 1) * P], x[:, j, k, :],
                                         start=(i == 0), stop=(i == 3 * KT - 1))
                        i += 1
                last.then_inc(hid_done, 1)

            def project(g, n, q, cw):
                u = n * GB + q
                if q == 0:
                    pe.wait_ge(y_kept, 2 * n + FREE)
                if q == 0 and g == 0:
                    for k in range(KT):
                        for i, w in enumerate((b2h, b2l)):
                            pe.matmul(ps[:, OUT + k, :], w[:, k * P:(k + 1) * P], cw, start=(i == 0), stop=False)
                pe.wait_ge(g_split, u + 1 + FREE)
                for k in range(KT):
                    for i, (w, x) in enumerate(((w2h, gh), (w2h, gl), (w2l, gh))):
                        last = pe.matmul(ps[:, OUT + k, :], w[:, q, k * P:(k + 1) * P], x[:, q % 2, :],
                                         start=(g > 0 and q == 0 and i == 0), stop=(q == GB - 1 and i == 2))
                        if q == GB - 2 and k == 0 and i == 0:
                            last.then_inc(x_free, 1)
                last.then_inc(out_done, 1)

            def turn_y(n):
                pe.wait_ge(y_kept, 2 * n + 2 + FREE)
                for b in range(2):
                    pe.wait_ge(y_added, 2 * n + b + 1)
                    for t in range(2):
                        for k in range(KT):
                            last = pe.transpose(ps[:, TURN + b, (t * KT + k) * P:(t * KT + k + 1) * P],
                                                stage[:, k, (2 * b + t) * P:(2 * b + t + 1) * P], ident[:, :])
                    last.then_inc(y_turned, 1)

            for g in range(GROUPS):
                pe.wait_ge(w_split, 2 * (g + 1))
                with pe.Fori(0, CHUNKS // 2) as cc:
                    for j in range(2):
                        n = g * CHUNKS + 2 * cc + j
                        cw = cwT[:, bass.ds((2 * cc + j) * CH, CH)]
                        for q in range(GB):
                            hidden(g, n, j, q, cw)
                            if j == 1 and q == 1:
                                turn_y(n - 1)
                            if q >= 2:
                                project(g, n, q - 2, cw)
                        project(g, n, GB - 2, cw)
                        project(g, n, GB - 1, cw)
                    turn_y(n)


C_HEADS, C_DH = 16, 16
C_HPH = C_HEADS // 2
C_TAIL = 32
C_DUP = P + C_TAIL - CTX
C_NEG = -1.0e30


def ctx_attention_stage(nc, xres, ident, A):
    with ExitStack() as ctx:
        def sb(name, shape, dt=F32):
            return ctx.enter_context(nc.sbuf_tensor("x1_" + name, shape, dt))

        def sem(name):
            return nc.alloc_semaphore("x1_" + name)

        names = ("L1_xattn_Wq", "L1_xattn_Wk", "L1_xattn_Wv", "L1_xattn_Wo")
        ROW = C_HPH * (P + C_TAIL)
        p = sb("p", [P, 4, ROW])
        wraw = p[:, 0:2, :].rearrange("p a j -> p (a j)")[:, 0:4 * 2 * DIM].rearrange("p (w o d) -> p w o d", w=4, o=2)
        ctxA = p[:, 2:4, :].rearrange("p a j -> p (a j)")[:, 0:4 * DIM].rearrange("p (b d) -> p b d", b=4)
        ctxB = p[:, 2:4, :].rearrange("p a j -> p (a j)")[0:CTX - P, 4 * DIM:8 * DIM].rearrange("p (b d) -> p b d", b=4)
        NBLK = C_HPH + 2
        pth, ptl = sb("pth", [P, 2, NBLK, 2 * P], F32R), sb("ptl", [P, 2, NBLK, 2 * P], F32R)

        def early(t, at, shape):
            flat = t[:, :, :, :].rearrange("p a n c -> p (a n c)")[:, at:at + int(np.prod(shape))]
            names = " ".join("abc"[:len(shape)])
            return flat.rearrange(f"p ({names}) -> p {names}", **dict(zip("abc", shape)))

        xTh, xTl = (early(t, 0, (KT, SEQ)) for t in (pth, ptl))
        cth, ctl = (early(t, KT * SEQ, (KT, BATCH, CTX)) for t in (pth, ptl))
        at = KT * SEQ + KT * BATCH * CTX
        wh = [sb("wqh", [P, KT, DIM], F32R), early(pth, at, (KT, DIM)), early(pth, at + KT * DIM, (KT, DIM)), sb("woh", [P, KT, DIM], F32R)]
        wl = [sb("wql", [P, KT, DIM], F32R), early(ptl, at, (KT, DIM)), early(ptl, at + KT * DIM, (KT, DIM)), sb("wol", [P, KT, DIM], F32R)]
        kTh, kTl = sb("kTh", [P, 2, BATCH, CTX], F32R), sb("kTl", [P, 2, BATCH, CTX], F32R)
        vAh, vAl = sb("vAh", [P, BATCH, DIM], F32R), sb("vAl", [P, BATCH, DIM], F32R)
        vBh, vBl = sb("vBh", [P, BATCH, DIM], F32R), sb("vBl", [P, BATCH, DIM], F32R)
        hmask_one = sb("one_row", [P, P])
        hmask = sb("hmask", [P, C_HPH])
        onesT = sb("onesT", [P, 4, P], F32R)
        tmask = sb("tmask", [P, 4, P])[:, :, :].rearrange("p (a b) (h d) -> p a b h d", a=2, d=C_DH)
        DIAG = P + C_DH
        onesA = sb("onesA", [P, C_HPH * DIAG], F32R)
        zero = sb("zero", [P, DIAG])
        scratch = sb("scratch", [P, 4 * CTX])
        cm = scratch[:, :].rearrange("p (t h j) -> p t h j", t=2, h=2)
        causal = sb("causal", [P, 2, 2, CTX], F32R)
        identr = sb("identr", [P, P], F32R)
        kbh, kbl = sb("kbh", [P, 2, C_HPH, CTX], F32R), sb("kbl", [P, 2, C_HPH, CTX], F32R)
        vah, val = sb("vah", [P, 2, C_HPH * DIAG], F32R), sb("val", [P, 2, C_HPH * DIAG], F32R)
        vbh, vbl = sb("vbh", [P, 4, P], F32R), sb("vbl", [P, 4, P], F32R)
        bor = sb("bor", [1, DIM])
        boh, bol, one1 = sb("boh", [1, DIM], F32R), sb("bol", [1, DIM], F32R), sb("one1", [1, P], F32R)
        tg = sb("tg", [P, 1])
        st, mv = sb("st", [P, TILES, 6]), sb("mv", [P, TILES, 2])
        var, root, rstd = sb("var", [P, TILES]), sb("root", [P, TILES]), sb("rstd", [P, TILES])
        start = p[:, :, :].rearrange("p a j -> p (a j)")[:, 0:TPB * DIM]
        y, qf = start.rearrange("p (t d) -> p t d", d=DIM), start.rearrange("p (h c) -> p h c", h=2)
        qh, ql = sb("qh", [P, 2, SEQ], F32R), sb("ql", [P, 2, SEQ], F32R)
        tails = [t[:, :, 0:CH].rearrange("p k (b r j) -> p k b r j", b=BATCH, j=C_TAIL) for t in (qh, ql)]
        mx = sb("mx", [P, C_HPH])
        rs, of = scratch[:, 0:2 * P], scratch[:, 2 * P:4 * P]
        oh, ol = sb("oh", [P, 2, 2 * P], F32R), sb("ol", [P, 2, 2 * P], F32R)
        ps = ctx.enter_context(nc.psum_tensor("x1_ps", [P, 8, CH], F32))
        TURN, PV, WO = 4, 6, 7
        scores = ps[:, 0:4, 0:2 * CTX].rearrange("p b (h j) -> p b h j", j=CTX)

        d_in, set_up, dve_own, pool_own = sem("d_in"), sem("set_up"), sem("dve_own"), sem("pool_own")
        pre_done, pre_hi, pre_lo = sem("pre_done"), sem("pre_hi"), sem("pre_lo")
        tanhed, stats, rooted, ready = sem("tanhed"), sem("stats"), sem("rooted"), sem("ready")
        y_ready, x_turned, x_hi, x_lo = sem("y_ready"), sem("x_turned"), sem("x_hi"), sem("x_lo")
        q_done, q_full, q_split, k_spread, v_spread = (sem(n) for n in ("q_done", "q_full", "q_split", "k_spread", "v_spread"))
        s_done, s_read, exp_done, turned, hi_done, lo_done = (
            sem(n) for n in ("s_done", "s_read", "exp_done", "turned", "hi_done", "lo_done"))
        pv_done, o_read, o_split, wo_done, x_added, batch_done = (
            sem(n) for n in ("pv_done", "o_read", "o_split", "wo_done", "x_added", "batch_done"))
        tails_set = sem("tails_set")
        block = ctx.enter_context(nc.Block())
        STEPS = 2 * TPB
        LAG = 2
        NJOB = 16
        GRP = ((0, 4), (4, 8), (8, 10))

        def job_out(n):
            if n < 4:
                return 2 * DIM, wh[n][:, :, :].rearrange("p k d -> p (k d)"), wl[n][:, :, :].rearrange("p k d -> p (k d)")
            if n < 12:
                h, l = (cth, ctl) if n < 8 else (kTh, kTl)
                k, b = (n % 4) // 2, n % 2
                return 2 * CTX, *(t[:, k, 2 * b:2 * b + 2, :].rearrange("p b j -> p (b j)") for t in (h, l))
            h, l = (vAh, vAl) if n < 14 else (vBh, vBl)
            return 2 * DIM, *(t[:, 2 * (n % 2):2 * (n % 2) + 2, :].rearrange("p b d -> p (b d)") for t in (h, l))

        @block.sync
        def _(sp):
            for i, n in enumerate(names):
                sp.dma_start(wraw[:, i, :, :], A[n].rearrange("(o p) d -> p o d", p=P)).then_inc(d_in, 16)
            sp.dma_start(ctxA, A["ctx_1024"][:, 0:P, :].rearrange("b j d -> j b d")).then_inc(d_in, 16)
            sp.dma_start(ctxB, A["ctx_1024"][:, P:CTX, :].rearrange("b j d -> j b d")).then_inc(d_in, 16)
            sp.dma_start(bor[:, :], A["L1_xattn_bo"].rearrange("(a d) -> a d", a=1)).then_inc(d_in, 16)
            with nc.allow_non_contiguous_dma(reason="one column"):
                sp.dma_start(tg[:, :], A["g_xattn"][1:2].partition_broadcast(P)).then_inc(d_in, 16)
        ND = 8

        @block.gpsimd
        def _(pool):
            own = Chain(pool, pool_own)
            own.step(pool.memset(hmask[:, :], 1.0))
            own.step(pool.memset(tmask, 1.0))
            own.step(pool.memset(cm, 0.0))
            own.step(pool.memset(zero[:, :], 0.0))
            own.wait()
            own.link(pool.affine_select(out=hmask[:, :], in_=hmask[:, :], compare_op=ALU.is_ge, fill=0.0, base=0,
                                        pattern=[[-C_DH, C_HPH]], channel_multiplier=1))
            own.link(pool.affine_select(out=hmask[:, :], in_=hmask[:, :], compare_op=ALU.is_ge, fill=0.0, base=C_DH - 1,
                                        pattern=[[C_DH, C_HPH]], channel_multiplier=-1))
            for h in range(2):
                m = tmask[:, h, :, :, :]
                own.link(pool.affine_select(out=m, in_=m, compare_op=ALU.is_ge, fill=0.0, base=-C_DUP,
                                            pattern=[[P, 2], [-C_TAIL, C_HPH], [0, C_DH]], channel_multiplier=1))
                own.link(pool.affine_select(out=m, in_=m, compare_op=ALU.is_ge, fill=0.0, base=C_TAIL - 1,
                                            pattern=[[-P, 2], [C_TAIL, C_HPH], [0, C_DH]], channel_multiplier=-1))
            own.link(pool.affine_select(out=cm, in_=cm, compare_op=ALU.is_ge, fill=C_NEG, base=0,
                                        pattern=[[P, 2], [0, 2], [-1, CTX]], channel_multiplier=1))
            own.step(pool.tensor_copy(causal[:, :, :, :], cm))
            own.step(pool.tensor_copy(identr[:, :], ident[:, :]))
            own.step(pool.tensor_copy(onesT[:, :, :], tmask.rearrange("p a b h d -> p (a b) (h d)")))
            for h in range(C_HPH):
                own.step(pool.tensor_copy(onesA[:, h * DIAG:(h + 1) * DIAG], zero[:, :]))
                for t in (vah, val):
                    for i in range(2):
                        own.step(pool.tensor_copy(t[:, i, h * DIAG:(h + 1) * DIAG], zero[:, :]))
            own.link(pool.memset(hmask_one[:, :], 1.0))
            own.step(pool.tensor_copy(onesA[:, :].rearrange("p (h c) -> p h c", c=DIAG)[:, :, 0:C_DH],
                                      hmask_one[:, :].rearrange("p (h c) -> p h c", c=C_DH)))
            pool.tensor_copy(one1[:, :], hmask_one[0:1, :]).then_inc(set_up, 1)
            own.wait()
            pool.wait_ge(set_up, 1)
            pool.wait_ge(pre_lo, 8)
            for t, c in zip(tails, (cth, ctl)):
                for k in range(KT):
                    src = c[:, k, :, CTX - C_TAIL:CTX].bitcast(F32).unsqueeze(2).broadcast_to([P, BATCH, P // C_TAIL, C_TAIL])
                    pool.tensor_copy(t[:, k, :, :, :], src).then_inc(tails_set, 1)
            pool.wait_ge(pre_lo, NJOB)
            with pool.Fori(0, BATCH) as b:
                pool.wait_ge(batch_done, b + 1)
                hm = hmask[:, :].unsqueeze(2).broadcast_to([P, C_HPH, CTX])
                for h in range(2):
                    src = kTl[:, h, bass.ds(b, 1), :].bitcast(F32).broadcast_to([P, C_HPH, CTX])
                    pool.tensor_tensor(kbl[:, h, :, :], src, hm, ALU.mult).then_inc(k_spread, 1)
                for s, d in ((vAh, vah), (vAl, val)):
                    for h in range(2):
                        pool.tensor_copy(d[:, h, :].rearrange("p (h c) -> p h c", c=DIAG)[:, :, 0:C_DH],
                                         s[:, bass.ds(b, 1), h * P:(h + 1) * P].bitcast(F32).rearrange("p a (h c) -> p (a h) c", c=C_DH)).then_inc(v_spread, 1)
                for s, d in ((vBh, vbh), (vBl, vbl)):
                    for g in range(4):
                        h = g // 2
                        pool.tensor_tensor(d[:, g, :], s[:, bass.ds(b, 1), h * P:(h + 1) * P].bitcast(F32).rearrange("p a c -> p (a c)"),
                                           tmask[:, h, g % 2, :, :].rearrange("p h d -> p (h d)"), ALU.mult).then_inc(v_spread, 1)

        @block.scalar
        def _(act):
            act.wait_ge(d_in, 16 * ND)
            act.activation(tg[:, :], tg[:, :], ACT.Tanh).then_inc(tanhed, 1)
            for n in range(NJOB):
                size, h, _ = job_out(n)
                act.wait_ge(pre_done, n + 1)
                act.activation(h, ps[:, n % 8, 0:size], ACT.Copy).then_inc(pre_hi, 1)
            act.wait_ge(stats, 1)
            act.activation(root[:, :], var[:, :], ACT.Sqrt).then_inc(rooted, 1)
            with act.Fori(0, BATCH) as b:
                for i in range(4):
                    act.wait_ge(x_turned, 4 * b + i + 1)
                    act.activation(xTh[:, i // 2, (i % 2) * CH:(i % 2 + 1) * CH], ps[:, i, :], ACT.Copy).then_inc(x_hi, 1)
                for i in range(4):
                    act.wait_ge(q_done, 4 * b + i + 1)
                    act.activation(qf[:, i // 2, (i % 2) * CH:(i % 2 + 1) * CH], ps[:, 4 + i, :], ACT.Copy,
                                   scale=float(C_DH) ** -0.5).then_inc(q_full, 1)
                for w in range(STEPS + LAG):
                    W = STEPS * b + w
                    if w >= LAG:
                        v = w - LAG
                        for g, (lo, hi) in enumerate(GRP):
                            G = 3 * (W - LAG) + g
                            act.wait_ge(turned, G + 1 + 6)
                            act.activation(pth[:, (v // 2) % 2, lo:hi, (v % 2) * P:(v % 2 + 1) * P],
                                           ps[:, TURN + (v + g) % 2, 0:(hi - lo) * P].rearrange("p (n t) -> p n t", t=P),
                                           ACT.Copy).then_inc(hi_done, 1)
                    if w < STEPS:
                        act.wait_ge(s_read, W + 1 + 1)
                        act.activation(p[:, w % 4, :], p[:, w % 4, :], ACT.Exp).then_inc(exp_done, 1)

        @block.vector
        def _(dve):
            own = Chain(dve, dve_own)
            dve.sem_inc(s_read, 1)
            dve.sem_inc(lo_done, 2)
            dve.sem_inc(o_read, 1)
            dve.sem_inc(x_added, 1)
            for t in range(TILES):
                own.step(dve.bn_stats(st[:, t, :], xres[:, t, :]))
            own.wait()
            for t in range(TILES):
                own.step(dve.bn_aggr(mv[:, t, :], st[:, t, :]))
            own.wait()
            dve.tensor_scalar(var[:, :], mv[:, :, 1], EPS, None, ALU.add).then_inc(stats, 1)
            dve.wait_ge(d_in, 16 * ND)
            own.link(dve.tensor_copy(boh[:, :], bor[:, :]))
            dve.tensor_tensor(bol[:, :], bor[:, :], boh[:, :].bitcast(F32), ALU.subtract).then_inc(ready, 1)
            for n in range(NJOB):
                size, h, l = job_out(n)
                dve.wait_ge(pre_hi, n + 1)
                dve.tensor_tensor(l, ps[:, n % 8, 0:size], h.bitcast(F32), ALU.subtract).then_inc(pre_lo, 1)
            dve.wait_ge(rooted, 1)
            newton_rsqrt(own, dve, var[:, :], root[:, :], rstd[:, :])
            dve.wait_ge(set_up, 1)
            dve.wait_ge(tanhed, 1)
            dve.wait_ge(pre_lo, NJOB)

            PER = 16 + 4 + 2 * TPB
            with dve.Fori(0, BATCH) as b:
                own.enter(b, PER)
                for t in range(TPB):
                    n = TPB * b + t
                    dve.tensor_scalar(y[:, t, :], xres[:, bass.ds(n, 1), :], mv[:, bass.ds(n, 1), 0],
                                      rstd[:, bass.ds(n, 1)], ALU.subtract, ALU.mult).then_inc(y_ready, 1)
                for i in range(4):
                    dve.wait_ge(x_hi, 4 * b + i + 1)
                    h = xTh[:, i // 2, (i % 2) * CH:(i % 2 + 1) * CH]
                    dve.tensor_tensor(xTl[:, i // 2, (i % 2) * CH:(i % 2 + 1) * CH], ps[:, i, :], h.bitcast(F32),
                                      ALU.subtract).then_inc(x_lo, 1)
                dve.wait_ge(batch_done, b + 1)
                for h in range(2):
                    dve.tensor_tensor(kbh[:, h, :, :], kTh[:, h, bass.ds(b, 1), :].bitcast(F32).broadcast_to([P, C_HPH, CTX]),
                                      hmask[:, :].unsqueeze(2).broadcast_to([P, C_HPH, CTX]), ALU.mult).then_inc(k_spread, 1)
                for i in range(4):
                    dve.wait_ge(q_full, 4 * b + i + 1)
                    f, h, l = (t[:, i // 2, (i % 2) * CH:(i % 2 + 1) * CH] for t in (qf, qh, ql))
                    own.link(dve.tensor_copy(h, f))
                    dve.tensor_tensor(l, f, h.bitcast(F32), ALU.subtract).then_inc(q_split, 1)

                def lows(w, gs):
                    v = w - LAG
                    for g in gs:
                        lo, hi = GRP[g]
                        dve.wait_ge(hi_done, 3 * (STEPS * b + v) + g + 1)
                        dst = (slice(None), (v // 2) % 2, slice(lo, hi), slice((v % 2) * P, (v % 2 + 1) * P))
                        dve.tensor_tensor(ptl[dst], ps[:, TURN + (v + g) % 2, 0:(hi - lo) * P].rearrange("p (n t) -> p n t", t=P),
                                          pth[dst].bitcast(F32), ALU.subtract).then_inc(lo_done, 1)

                def outs(u):
                    V = TPB * b + u
                    dve.wait_ge(pv_done, V + 1)
                    own.link(dve.reciprocal(rs[:, :], ps[:, PV, 2 * P:4 * P]))
                    dve.tensor_tensor(of[:, :], ps[:, PV, 0:2 * P], rs[:, :], ALU.mult).then_inc(o_read, 1)
                    dve.wait_ge(o_read, V + 1 + 1)
                    own.link(dve.tensor_copy(oh[:, u % 2, :], of[:, :]))
                    dve.tensor_tensor(ol[:, u % 2, :], of[:, :], oh[:, u % 2, :].bitcast(F32), ALU.subtract).then_inc(o_split, 1)

                def add_x(s):
                    dve.wait_ge(wo_done, TPB // 2 * b + s + 1)
                    part = xres[:, bass.ds(TPB * b + 2 * s, 2), :].rearrange("p t d -> p (t d)")
                    dve.scalar_tensor_tensor(part, ps[:, WO, :], tg[:, 0:1], part, ALU.mult, ALU.add).then_inc(x_added, 1)

                for w in range(STEPS + LAG + 4):
                    W = STEPS * b + w
                    if LAG <= w < STEPS + LAG:
                        lows(w, (0, 1))
                    if w < STEPS:
                        dve.wait_ge(s_done, W + 1)
                        own.link(dve.tensor_reduce(mx[:, :], scores, AX.X, ALU.max))
                        dve.wait_ge(turned, 3 * W - 3 + 6)
                        m = mx[:, :].rearrange("p (b h) -> p b h", h=2).unsqueeze(3)
                        dve.tensor_tensor(p[:, w % 4, 0:C_HPH * P].rearrange("p (b h j) -> p b h j", h=2, j=P), scores[:, :, :, 0:P],
                                          m.broadcast_to([P, 4, 2, P]), ALU.subtract)
                        dve.tensor_tensor(p[:, w % 4, C_HPH * P:ROW].rearrange("p (b h j) -> p b h j", h=2, j=C_TAIL),
                                          scores[:, :, :, CTX - C_TAIL:CTX], m.broadcast_to([P, 4, 2, C_TAIL]),
                                          ALU.subtract).then_inc(s_read, 1)
                    if LAG <= w < STEPS + LAG:
                        lows(w, (2,))
                    z = w - LAG - 3
                    if z >= 0 and z % 2 == 0 and z // 2 < TPB:
                        outs(z // 2)
                    z = w - LAG - 6
                    if z >= 0 and z % 4 == 0:
                        add_x(z // 4)
                own.leave(BATCH)

        @block.tensor
        def _(pe):
            pe.sem_inc(turned, 6)
            pe.sem_inc(batch_done, 1)
            pe.wait_ge(d_in, 16 * ND)
            for n in range(NJOB):
                if n >= 8:
                    pe.wait_ge(pre_lo, n - 7)
                bank = ps[:, n % 8, :]
                if n < 4:
                    for k in range(KT):
                        for o in range(2):
                            last = pe.transpose(bank[:, k * DIM + o * P:k * DIM + (o + 1) * P], wraw[:, n, o, k * P:(k + 1) * P], ident[:, :])
                elif n < 8:
                    k = (n % 4) // 2
                    for i in range(2):
                        b = 2 * (n % 2) + i
                        pe.transpose(bank[:, i * CTX:i * CTX + P], ctxA[:, b, k * P:(k + 1) * P], ident[:, :])
                        last = pe.transpose(bank[:, i * CTX + P:(i + 1) * CTX], ctxB[:, b, k * P:(k + 1) * P], ident[0:CTX - P, 0:CTX - P])
                elif n < 12:
                    if n == 8:
                        pe.wait_ge(pre_lo, 8)
                    h, b = (n % 4) // 2, 2 * (n % 2)
                    i = 0
                    for k in range(KT):
                        for w, x in ((wh, cth), (wh, ctl), (wl, cth)):
                            last = pe.matmul(bank[:, 0:2 * CTX], w[1][:, k, h * P:(h + 1) * P],
                                             x[:, k, b:b + 2, :].rearrange("p b j -> p (b j)"), start=(i == 0), stop=(i == 5))
                            i += 1
                else:
                    if n == 14:
                        pe.wait_ge(tails_set, 4)
                    for b2 in range(2):
                        b, i = 2 * (n % 2) + b2, 0
                        for k in range(KT):
                            for w, x in ((wh, cth), (wh, ctl), (wl, cth)):
                                if n < 14:
                                    lhs = x[:, k, b, 0:P]
                                else:
                                    lhs = tails[x is ctl][:, k, b, :, :].rearrange("p r j -> p (r j)")
                                last = pe.matmul(bank[:, b2 * DIM:(b2 + 1) * DIM], lhs, w[2][:, k, :], start=(i == 0), stop=(i == 5))
                                i += 1
                last.then_inc(pre_done, 1)
            pe.wait_ge(ready, 1)
            pe.wait_ge(pre_lo, NJOB)
            pe.wait_ge(set_up, 1)

            with pe.Fori(0, BATCH) as b:
                for i in range(4):
                    k, c = i // 2, i % 2
                    if k == 0:
                        pe.wait_ge(y_ready, TPB * b + 4 * (c + 1))
                    if i == 0:
                        pe.wait_ge(s_read, STEPS * b + 1)
                    for t in range(4):
                        last = pe.transpose(ps[:, i, t * P:(t + 1) * P], y[:, 4 * c + t, k * P:(k + 1) * P], ident[:, :])
                    last.then_inc(x_turned, 1)
                pe.wait_ge(x_lo, 4 * (b + 1))
                pe.wait_ge(lo_done, 3 * STEPS * b + 2)
                pe.wait_ge(o_read, TPB * b + 1)
                pe.wait_ge(x_added, TPB // 2 * b + 1)
                for j in range(4):
                    h, c, i = j // 2, j % 2, 0
                    for k in range(KT):
                        for w, x in ((wh, xTh), (wh, xTl), (wl, xTh)):
                            last = pe.matmul(ps[:, 4 + j, :], w[0][:, k, h * P:(h + 1) * P], x[:, k, c * CH:(c + 1) * CH],
                                             start=(i == 0), stop=(i == 5))
                            i += 1
                    last.then_inc(q_done, 1)
                pe.wait_ge(k_spread, 4 * (b + 1))
                pe.wait_ge(q_split, 4 * (b + 1))

                def turn(w, gs):
                    v = w - LAG
                    V = STEPS * b + v
                    for g in gs:
                        lo, hi = GRP[g]
                        if g == 0:
                            pe.wait_ge(exp_done, V + 1)
                        pe.wait_ge(lo_done, 3 * V + g + 1)
                        for n in range(lo, hi):
                            last = pe.transpose(ps[:, TURN + (v + g) % 2, (n - lo) * P:(n - lo + 1) * P],
                                                p[:, v % 4, n * P:(n + 1) * P], ident[:, :])
                        last.then_inc(turned, 1)

                def score(w):
                    W = STEPS * b + w
                    u, h = w // 2, (w // 2) % 2
                    t = 2 * (u // 2) + w % 2
                    pe.wait_ge(s_read, W + 1)
                    for n in range(4):
                        out = ps[:, n, 0:2 * CTX]
                        for i, (q, k) in enumerate(((qh, kbh), (qh, kbl), (ql, kbh))):
                            last = pe.matmul(out, q[:, h, t * P:(t + 1) * P], k[:, h, 2 * n:2 * n + 2, :].rearrange("p h j -> p (h j)"),
                                             start=(i == 0), stop=(i == 2 and t > 1))
                        if t < 2:
                            last = pe.matmul(out, identr[:, :], causal[:, t, :, :].rearrange("p h j -> p (h j)"), start=False, stop=True)
                    last.then_inc(s_done, 1)

                def stat(h, n, vals):
                    if n < C_HPH:
                        return vals[0][:, h, n * P:(n + 1) * P]
                    return vals[1][:, 2 * h + n - C_HPH, :]

                def values(u):
                    V, h = TPB * b + u, u % 2
                    if u == 0:
                        pe.wait_ge(v_spread, 12 * (b + 1))
                    pe.wait_ge(lo_done, 6 * (V + 1) + 2)
                    pe.wait_ge(o_read, V + 1)
                    for n in range(NBLK):
                        for i, (v, x) in enumerate((((vah, vbh), pth), ((vah, vbh), ptl), ((val, vbl), pth))):
                            pe.matmul(ps[:, PV, 0:2 * P], stat(h, n, v), x[:, u % 2, n, :], start=(n == 0 and i == 0), stop=(n == NBLK - 1 and i == 2))

                def sums(u):
                    for n in range(NBLK):
                        w = onesA[:, n * P:(n + 1) * P] if n < C_HPH else onesT[:, n - C_HPH, :]
                        for i, x in enumerate((pth, ptl)):
                            last = pe.matmul(ps[:, PV, 2 * P:4 * P], w, x[:, u % 2, n, :], start=(n == 0 and i == 0), stop=(n == NBLK - 1 and i == 1))
                    last.then_inc(pv_done, 1)

                def project(s):
                    pe.wait_ge(o_split, TPB * b + 2 * (s + 1))
                    pe.wait_ge(x_added, TPB // 2 * b + s + 1)
                    for t in range(2):
                        out = ps[:, WO, t * DIM:(t + 1) * DIM]
                        pe.matmul(out, one1[:, :], boh[:, :], start=True, stop=False)
                        pe.matmul(out, one1[:, :], bol[:, :], start=False, stop=False)
                        for k in range(KT):
                            for i, (o, w) in enumerate(((oh, wh), (oh, wl), (ol, wh))):
                                last = pe.matmul(out, o[:, k, t * P:(t + 1) * P], w[3][:, k, :], start=False, stop=(k == 1 and i == 2))
                    last.then_inc(wo_done, 1)

                for w in range(STEPS + LAG + 4):
                    if LAG <= w < STEPS + LAG:
                        turn(w, (0, 1))
                    if w < STEPS:
                        score(w)
                    if LAG <= w < STEPS + LAG:
                        turn(w, (2,))
                    z = w - LAG - 2
                    if z >= 0 and z % 2 == 0 and z // 2 < TPB:
                        values(z // 2)
                    z = w - LAG - 3
                    if z >= 0 and z % 2 == 0 and z // 2 < TPB:
                        sums(z // 2)
                    z = w - LAG - 6
                    if z >= 0 and z % 4 == 0:
                        project(z // 4)
                pe.drain().then_inc(batch_done, 1)


HID = 1024
HB = HID // P
MAGIC = 1.5 * 2.0 ** 23
QMAX, QMIN = 127.0, -128.0
TINY = 1e-5


def ffn_stage(nc, xres, ident, A):
    with ExitStack() as ctx:
        def sb(name, shape, dt=F32):
            return ctx.enter_context(nc.sbuf_tensor("ffn_" + name, shape, dt))

        def sem(name):
            return nc.alloc_semaphore("ffn_" + name)

        w1, w2 = sb("w1", [P, HB, DIM]), sb("w2", [P, KT, HID])
        w1q, w2q = sb("w1q", [P, HB, DIM], BF16), sb("w2q", [P, KT, HID], BF16)
        w1T, w2T = sb("w1T", [P, KT, HID], BF16), sb("w2T", [P, HB, DIM], BF16)
        conv_w, conv_b = sb("conv_w", [P, HB, 3]), sb("conv_b", [P, HB])
        tg = sb("tg", [P, 1])
        wsum, winv, wsc, fac = sb("wsum", [P, 2]), sb("winv", [P, 2]), sb("wsc", [P, 2]), sb("fac", [P, 1])
        ones, identb = sb("ones", [P, P]), sb("identb", [P, P], BF16)
        st, mv = sb("st", [P, TILES, 6]), sb("mv", [P, TILES, 2])
        var, root, rstd = sb("var", [P, TILES]), sb("root", [P, TILES]), sb("rstd", [P, TILES])
        y = sb("y", [P, TPB, DIM])
        yq = sb("yq", [P, TPB, DIM], BF16)
        am, sc, d1 = sb("am", [P, TPB]), sb("sc", [P, TPB]), sb("d1", [P, TPB])
        diag = sb("diag", [P, TPB, P])
        rsc = sb("rsc", [P, SEQ])
        yT = sb("yT", [P, KT, SEQ], BF16)
        hb = [sb(f"hb{i}", [P, SEQ + 2]) for i in range(2)]
        acc = sb("acc", [P, 2, SEQ])
        hs = sb("hs", [P, HB, SEQ])
        am2, sc2, d2 = sb("am2", [P, TPB]), sb("sc2", [P, TPB]), sb("d2", [P, TPB])
        u = sb("u", [P, 2, HID])
        r2 = sb("r2", [P, 2, HID], BF16)
        r2T = sb("r2T", [P, 2, HB, P], BF16)
        ps = ctx.enter_context(nc.psum_tensor("ffn_ps", [P, 8, CH], F32))
        wide = [ps[:, 0:2, :].rearrange("p b c -> p (b c)"), ps[:, 2:4, :].rearrange("p b c -> p (b c)")]
        half = [ps[:, 4, :].bitcast(BF16), ps[:, 5, :].bitcast(BF16)]
        outp = [ps[:, 6, 0:DIM], ps[:, 7, 0:DIM]]

        d_w, dve_own = sem("d_w"), sem("dve_own")
        set_up, summed, totalled, w_quant, w_turned, w_kept, tanhed = (
            sem(n) for n in ("set_up", "summed", "totalled", "w_quant", "w_turned", "w_kept", "tanhed"))
        stats, rooted = sem("stats"), sem("rooted")
        y_quant, diag_set, y_turned, y_kept, rsc_done, rsc_kept = (
            sem(n) for n in ("y_quant", "diag_set", "y_turned", "y_kept", "rsc_done", "rsc_kept"))
        hid_done, h_done, conv_mid, conv_done, hs_done = (
            sem(n) for n in ("hid_done", "h_done", "conv_mid", "conv_done", "hs_done"))
        t_done, t_read, b_done, r2_done, r2_turned, r2_kept, out_done, out_added = (
            sem(n) for n in ("t_done", "t_read", "b_done", "r2_done", "r2_turned", "r2_kept", "out_done", "out_added"))
        block = ctx.enter_context(nc.Block())

        @block.sync
        def _(sp):
            sp.dma_start(w1[:, :, :], A["L1_ffn_w1"].rearrange("(b p) d -> p b d", p=P)).then_inc(d_w, 16)
            sp.dma_start(w2[:, :, :], A["L1_ffn_w2"].rearrange("(k p) h -> p k h", p=P)).then_inc(d_w, 16)
            sp.dma_start(conv_w[:, :, :], A["L1_ffn_conv_w"].rearrange("(b p) o w -> p b (o w)", p=P)).then_inc(d_w, 16)
            with nc.allow_non_contiguous_dma(reason="small columns"):
                sp.dma_start(conv_b[:, :], A["L1_ffn_conv_b"].rearrange("(b p) -> p b", p=P)).then_inc(d_w, 16)
                sp.dma_start(tg[:, :], A["g_ffn"][1:2].partition_broadcast(P)).then_inc(d_w, 16)

        @block.gpsimd
        def _(pool):
            pool.memset(ones[:, :], 1.0).then_inc(set_up, 1)
            pool.tensor_copy(identb[:, :], ident[:, :]).then_inc(set_up, 1)
            for h in hb:
                pool.memset(h[:, 0:1], 0.0).then_inc(set_up, 1)
                pool.memset(h[:, SEQ + 1:SEQ + 2], 0.0).then_inc(set_up, 1)

        @block.scalar
        def _(act):
            act.wait_ge(d_w, 80)
            act.activation(tg[:, :], tg[:, :], ACT.Tanh).then_inc(tanhed, 1)
            act.wait_ge(stats, 1)
            act.activation(root[:, :], var[:, :], ACT.Sqrt).then_inc(rooted, 1)
            for i, dst in enumerate((w1T, w2T)):
                n = dst.shape[1] // 2 if i else 1
                for k in range(2):
                    act.wait_ge(w_turned, 2 * i + k + 1)
                    act.activation(dst[:, k * n:(k + 1) * n, :].rearrange("p k h -> p (k h)"), half[k], ACT.Copy).then_inc(w_kept, 1)
            with act.Fori(0, BATCH) as b:
                for k in range(KT):
                    act.wait_ge(y_turned, KT * b + k + 1)
                    act.activation(yT[:, k, :], half[k], ACT.Copy).then_inc(y_kept, 1)
                act.wait_ge(rsc_done, b + 1)
                act.activation(rsc[:, :], wide[0], ACT.Copy).then_inc(rsc_kept, 1)

                def middle(q):
                    act.wait_ge(h_done, HB * b + q + 1)
                    act.activation(acc[:, q % 2, :], hb[q % 2][:, 1:SEQ + 1], ACT.Identity, bias=conv_b[:, q:q + 1],
                                   scale=conv_w[:, q, 1:2]).then_inc(conv_mid, 1)

                middle(0)
                for q in range(HB):
                    if q + 1 < HB:
                        if q:
                            act.wait_ge(hs_done, HB * b + q)
                        middle(q + 1)
                    act.wait_ge(conv_done, HB * b + q + 1)
                    act.activation(hs[:, q, :], acc[:, q % 2, :], ACT.Silu).then_inc(hs_done, 1)
                for t in range(TPB):
                    n = TPB * b + t
                    act.wait_ge(b_done, n + 1)
                    act.activation(r2[:, t % 2, :], u[:, t % 2, :], ACT.Copy, bias=-MAGIC).then_inc(r2_done, 1)
                    act.wait_ge(r2_turned, n + 1)
                    act.activation(r2T[:, t % 2, :, :].rearrange("p b t -> p (b t)"), half[t % 2], ACT.Copy).then_inc(r2_kept, 1)

        @block.vector
        def _(dve):
            own = Chain(dve, dve_own)
            for t in range(TILES):
                own.step(dve.bn_stats(st[:, t, :], xres[:, t, :]))
            own.wait()
            for t in range(TILES):
                own.step(dve.bn_aggr(mv[:, t, :], st[:, t, :]))
            own.wait()
            dve.tensor_scalar(var[:, :], mv[:, :, 1], EPS, None, ALU.add).then_inc(stats, 1)
            dve.wait_ge(d_w, 80)
            own.step(dve.tensor_reduce(wsum[:, 0:1], w1[:, :, :], AX.XY, ALU.add, apply_absolute_value=True))
            dve.tensor_reduce(wsum[:, 1:2], w2[:, :, :], AX.XY, ALU.add, apply_absolute_value=True).then_inc(summed, 1)
            own.wait()
            dve.wait_ge(totalled, 1)
            own.link(dve.tensor_scalar(winv[:, :], outp[0][:, 0:2], 1.0 / (HID * DIM), TINY, ALU.mult, ALU.max))
            own.link(dve.reciprocal(wsc[:, :], winv[:, :]))
            for i, (w, wq) in enumerate(((w1, w1q), (w2, w2q))):
                own.link(dve.tensor_scalar(w[:, :, :], w[:, :, :], wsc[:, i:i + 1], 1.0, ALU.mult, ALU.min))
                own.link(dve.tensor_scalar(w[:, :, :], w[:, :, :], -1.0, MAGIC, ALU.max, ALU.add))
                dve.tensor_scalar(wq[:, :, :], w[:, :, :], MAGIC, None, ALU.subtract).then_inc(w_quant, 1)
            dve.wait_ge(tanhed, 1)
            own.link(dve.tensor_scalar(fac[:, :], winv[:, 1:2], tg[:, 0:1], 1.0 / QMAX, ALU.mult, ALU.mult))
            dve.wait_ge(rooted, 1)
            newton_rsqrt(own, dve, var[:, :], root[:, :], rstd[:, :])
            dve.wait_ge(set_up, 6)

            PER = 71
            with dve.Fori(0, BATCH) as b:
                own.enter(b, PER)
                for t in range(TPB):
                    n = TPB * b + t
                    own.step(dve.tensor_scalar(y[:, t, :], xres[:, bass.ds(n, 1), :], mv[:, bass.ds(n, 1), 0],
                                               rstd[:, bass.ds(n, 1)], ALU.subtract, ALU.mult))
                own.wait()
                own.link(dve.tensor_reduce(am[:, :], y[:, :, :], AX.X, ALU.max, apply_absolute_value=True))
                own.link(dve.tensor_scalar(am[:, :], am[:, :], TINY, None, ALU.max))
                own.link(dve.reciprocal(sc[:, :], am[:, :]))
                own.link(dve.tensor_scalar(sc[:, :], sc[:, :], QMAX, None, ALU.mult))
                own.link(dve.reciprocal(d1[:, :], sc[:, :]))
                own.link(dve.tensor_scalar(d1[:, :], d1[:, :], winv[:, 0:1], None, ALU.mult))
                for t in range(TPB):
                    own.step(dve.tensor_scalar(y[:, t, :], y[:, t, :], sc[:, t:t + 1], QMAX, ALU.mult, ALU.min))
                own.wait()
                own.link(dve.tensor_scalar(y[:, :, :], y[:, :, :], QMIN, MAGIC, ALU.max, ALU.add))
                dve.tensor_scalar(yq[:, :, :], y[:, :, :], MAGIC, None, ALU.subtract).then_inc(y_quant, 1)
                for t in range(TPB):
                    dve.tensor_scalar(diag[:, t, :], ident[:, :], d1[:, t:t + 1], None, ALU.mult).then_inc(diag_set, 1)

                def scale(q):
                    dve.wait_ge(hid_done, HB * b + q + 1)
                    dve.tensor_tensor(hb[q % 2][:, 1:SEQ + 1], wide[q % 2], rsc[:, :], ALU.mult).then_inc(h_done, 1)

                dve.wait_ge(rsc_kept, b + 1)
                scale(0)
                for q in range(HB):
                    if q + 1 < HB:
                        scale(q + 1)
                    a = acc[:, q % 2, :]
                    dve.wait_ge(conv_mid, HB * b + q + 1)
                    own.link(dve.scalar_tensor_tensor(a, hb[q % 2][:, 0:SEQ], conv_w[:, q, 0:1], a, ALU.mult, ALU.add))
                    dve.scalar_tensor_tensor(a, hb[q % 2][:, 2:SEQ + 2], conv_w[:, q, 2:3], a, ALU.mult, ALU.add).then_inc(conv_done, 1)
                    if q + 2 < HB:
                        dve.wait_ge(conv_done, HB * b + q + 1)

                def add_out(t):
                    n = TPB * b + t
                    dve.wait_ge(out_done, n + 1)
                    part = xres[:, bass.ds(n, 1), :].rearrange("p a d -> p (a d)")
                    dve.scalar_tensor_tensor(part, outp[t % 2], d2[:, t:t + 1], part, ALU.mult, ALU.add).then_inc(out_added, 1)

                for t in range(TPB):
                    n = TPB * b + t
                    c = slice(t, t + 1)
                    dve.wait_ge(t_done, n + 1)
                    own.link(dve.tensor_reduce(am2[:, c], wide[t % 2], AX.X, ALU.max, apply_absolute_value=True))
                    own.link(dve.tensor_scalar(am2[:, c], am2[:, c], TINY, None, ALU.max))
                    own.link(dve.reciprocal(sc2[:, c], am2[:, c]))
                    own.link(dve.tensor_scalar(sc2[:, c], sc2[:, c], QMAX, None, ALU.mult))
                    if t >= 2:
                        dve.wait_ge(r2_done, n - 1)
                    dve.tensor_scalar(u[:, t % 2, :], wide[t % 2], sc2[:, c], QMAX, ALU.mult, ALU.min).then_inc(t_read, 1)
                    dve.wait_ge(t_read, n + 1)
                    dve.tensor_scalar(u[:, t % 2, :], u[:, t % 2, :], QMIN, MAGIC, ALU.max, ALU.add).then_inc(b_done, 1)
                    own.step(dve.tensor_scalar(d2[:, c], am2[:, c], fac[:, 0:1], None, ALU.mult))
                    if t:
                        if t == 1:
                            own.wait()
                        add_out(t - 1)
                own.wait()
                add_out(TPB - 1)
                own.leave(BATCH)

        @block.tensor
        def _(pe):
            pe.wait_ge(set_up, 6)
            pe.wait_ge(summed, 1)
            pe.wait_ge(d_w, 80)
            pe.matmul(outp[0][:, 0:2], ones[:, :], wsum[:, :], start=True, stop=True).then_inc(totalled, 1)
            pe.wait_ge(w_quant, 1)
            for k in range(KT):
                for b in range(HB):
                    last = pe.transpose(half[k][:, b * P:(b + 1) * P], w1q[:, b, k * P:(k + 1) * P], identb[:, :])
                last.then_inc(w_turned, 1)
            pe.wait_ge(w_quant, 2)
            for i in range(2):
                pe.wait_ge(w_kept, i + 1)
                for b in range(HB // 2):
                    for k in range(KT):
                        q = i * (HB // 2) + b
                        last = pe.transpose(half[i][:, (b * KT + k) * P:(b * KT + k + 1) * P], w2q[:, k, q * P:(q + 1) * P], identb[:, :])
                last.then_inc(w_turned, 1)
            pe.wait_ge(w_kept, 4)
            with pe.Fori(0, BATCH) as b:
                pe.wait_ge(y_quant, b + 1)
                for k in range(KT):
                    for t in range(TPB):
                        last = pe.transpose(half[k][:, t * P:(t + 1) * P], yq[:, t, k * P:(k + 1) * P], identb[:, :])
                    last.then_inc(y_turned, 1)
                pe.wait_ge(diag_set, TPB * (b + 1))
                for t in range(TPB):
                    last = pe.matmul(wide[0][:, t * P:(t + 1) * P], ones[:, :], diag[:, t, :], start=True, stop=True)
                last.then_inc(rsc_done, 1)
                pe.wait_ge(y_kept, KT * (b + 1))
                for q in range(HB):
                    if q == 0:
                        pe.wait_ge(rsc_kept, b + 1)
                    if q >= 2:
                        pe.wait_ge(h_done, HB * b + q - 1)
                    for c in range(SEQ // CH):
                        for k in range(KT):
                            last = pe.matmul(wide[q % 2][:, c * CH:(c + 1) * CH], w1T[:, k, q * P:(q + 1) * P],
                                             yT[:, k, c * CH:(c + 1) * CH], start=(k == 0), stop=(k == KT - 1))
                    last.then_inc(hid_done, 1)

                def turn(t):
                    n = TPB * b + t
                    if t >= 2:
                        pe.wait_ge(t_read, n - 1)
                    for q in range(HB):
                        last = pe.transpose(wide[t % 2][:, q * P:(q + 1) * P], hs[:, q, t * P:(t + 1) * P], ident[:, :])
                    last.then_inc(t_done, 1)

                pe.wait_ge(h_done, HB * (b + 1))
                pe.wait_ge(hs_done, HB * (b + 1))
                turn(0)
                for t in range(TPB):
                    n = TPB * b + t
                    if t + 1 < TPB:
                        turn(t + 1)
                    pe.wait_ge(r2_done, n + 1)
                    if t >= 2:
                        pe.wait_ge(r2_kept, n - 1)
                    for q in range(HB):
                        last = pe.transpose(half[t % 2][:, q * P:(q + 1) * P], r2[:, t % 2, q * P:(q + 1) * P], identb[:, :])
                    last.then_inc(r2_turned, 1)
                    pe.wait_ge(r2_kept, n + 1)
                    if t >= 2:
                        pe.wait_ge(out_added, n - 1)
                    for q in range(HB):
                        last = pe.matmul(outp[t % 2], r2T[:, t % 2, q, :], w2T[:, q, :], start=(q == 0), stop=(q == HB - 1))
                    last.then_inc(out_done, 1)
                pe.wait_ge(out_added, TPB * (b + 1))


def flamingo_program(nc, A, out):
    with ExitStack() as ctx:
        xres = ctx.enter_context(nc.sbuf_tensor("xres", [P, TILES, DIM], F32))
        ident = ctx.enter_context(nc.sbuf_tensor("ident", [P, P], F32))
        ident_set, stored = nc.alloc_semaphore("ident_set"), nc.alloc_semaphore("stored")
        with nc.Block() as block:
            @block.gpsimd
            def _(pool):
                pool.memset(ident[:, :], 0.0).then_inc(ident_set, 1)
                pool.wait_ge(ident_set, 1)
                pool.affine_select(out=ident[:, :], in_=ident[:, :], compare_op=ALU.not_equal, fill=1.0, base=0,
                                   pattern=[[-1, P]], channel_multiplier=1).then_inc(ident_set, 1)
                pool.wait_ge(ident_set, 2)
        resample_stage(nc, xres, ident, A)
        moe_stage(nc, xres, ident, A)
        ctx_attention_stage(nc, xres, ident, A)
        ffn_stage(nc, xres, ident, A)
        with nc.Block() as block:
            @block.sync
            def _(sp):
                sp.dma_start(out.rearrange("b (t p) d -> p (b t) d", p=P), xres[:, :, :]).then_inc(stored, 16)
                sp.wait_ge(stored, 16)


def kernel(**inputs):
    import concourse.bacc as bacc
    from concourse.bass_utils import run_bass_kernel_spmd

    nc = bacc.Bacc("TRN2", target_bir_lowering=False, num_devices=1)
    arrays, A = {}, {}
    for name, value in inputs.items():
        a = np.ascontiguousarray(value)
        arrays[f"in_{name}_dram"] = a
        A[name] = nc.dram_tensor(f"in_{name}_dram", a.shape, mybir.dt.from_np(a.dtype), kind="ExternalInput").ap()
    out = nc.dram_tensor("out_dram", (BATCH, SEQ, DIM), F32, kind="ExternalOutput").ap()
    flamingo_program(nc, A, out)
    r = run_bass_kernel_spmd(nc, [arrays], core_ids=[0])
    return r.results[0]["out_dram"]
```

```python
from contextlib import ExitStack
import numpy as np
import concourse.bass as bass
from concourse import mybir

F32 = mybir.dt.float32
F32R = mybir.dt.float32r
BF16 = mybir.dt.bfloat16
ACT = mybir.ActivationFunctionType
ALU = mybir.AluOpType
AX = mybir.AxisListType

P = 128
BATCH, SEQ, DIM = 4, 1024, 256
CTX = 154
TOKENS = BATCH * SEQ
TILES = TOKENS // P
KT = DIM // P
CH = 512
CHUNKS = TOKENS // CH
TPC = CH // P
TPB = SEQ // P
EPS = 1e-5


class Chain:

    def __init__(self, eng, sem):
        self.eng, self.sem, self.base, self.k, self.start, self.per = eng, sem, 0, 0, 0, 0

    def step(self, ins):
        ins.then_inc(self.sem, 1)
        self.k += 1
        return self.k

    def wait(self, k=None):
        self.eng.wait_ge(self.sem, self.base + (self.k if k is None else k))

    def link(self, ins):
        self.step(ins)
        self.wait()

    def enter(self, it, per):
        self.start, self.per, self.base, self.k = self.base + self.k, per, it * per + (self.base + self.k), 0

    def leave(self, rounds):
        assert self.k == self.per, (self.k, self.per)
        self.base, self.k = self.start + rounds * self.per, 0


def newton_rsqrt(own, dve, var, root, r):
    own.link(dve.reciprocal(r, root))
    own.link(dve.tensor_tensor(root, r, r, ALU.mult))
    own.link(dve.tensor_tensor(root, root, var, ALU.mult))
    own.link(dve.tensor_scalar(root, root, -0.5, 1.5, ALU.mult, ALU.add))
    own.link(dve.tensor_tensor(r, r, root, ALU.mult))


R_HEADS, R_DH = 8, 128
R_INNER = R_HEADS * R_DH
R_KV = SEQ + CTX
R_BLK = -(-R_KV // P)
R_ROW = R_BLK * P
R_SCALE = float(R_DH) ** -0.5
R_BIG = 3.0e38


def resample_stage(nc, xres, ident, A):
    with ExitStack() as ctx:
        def sb(name, shape, dt=F32):
            return ctx.enter_context(nc.sbuf_tensor("x0_" + name, shape, dt))

        def sem(name):
            return nc.alloc_semaphore("x0_" + name)

        p = sb("p", [P, 4, R_ROW])
        z = sb("z", [P, TPB // 2, DIM])
        mA, mB = sb("mA", [P, DIM]), sb("mB", [CTX - P, DIM])
        kvh, kvl = sb("kvh", [P, KT, R_KV], F32R), sb("kvl", [P, KT, R_KV], F32R)
        wraw, wh, wl = sb("wraw", [P, 2, 4, DIM]), sb("wh", [P, 2, 4, DIM], F32R), sb("wl", [P, 2, 4, DIM], F32R)
        full = sb("full", [P, 2, CH])
        vf = sb("vf", [P, R_ROW])
        kh, kl = sb("kh", [P, 2, R_KV], F32R), sb("kl", [P, 2, R_KV], F32R)
        qh, ql = sb("qh", [P, 2, SEQ], F32R), sb("ql", [P, 2, SEQ], F32R)
        vh, vl = sb("vh", [P, 2, R_ROW], F32R), sb("vl", [P, 2, R_ROW], F32R)
        pth, ptl = sb("pth", [P, 2, R_BLK, 2 * P], F32R), sb("ptl", [P, 2, R_BLK, 2 * P], F32R)
        oh, ol = sb("oh", [P, 2 * P], F32R), sb("ol", [P, 2 * P], F32R)
        cA, cB = p[:, :, 0:DIM], p[0:CTX - P, :, DIM:2 * DIM]
        cols = sb("cols", [P, 4, KT])
        bias = sb("bias", [P, 3, R_HEADS])
        tbo = sb("tbo", [P, DIM])
        tg = sb("tg", [P, 1])
        NST = TILES + 2 * BATCH
        mv = p[:, 0, R_KV:R_KV + 2 * NST].rearrange("p (n s) -> p n s", s=2)
        r1 = p[:, 1, R_KV:R_KV + NST]
        st = vf[:, 0:6 * NST].rearrange("p (n s) -> p n s", s=6)
        var, root, r2 = vf[:, 6 * NST:7 * NST], vf[:, 7 * NST:8 * NST], vf[:, 8 * NST:8 * NST + TILES]
        nmx, sums, rt = sb("nmx", [P, 2]), sb("sums", [P, 2 * TPB]), sb("rt", [P, 2])
        ps = ctx.enter_context(nc.psum_tensor("x0_ps", [P, 8, CH], F32))
        scores = ps[:, 0:3, :].rearrange("p b c -> p (b c)")[:, 0:R_KV]
        TURN, PV, JOB = 3, 5, 6

        d_m, d_x, d_in = sem("d_m"), [sem(f"d_x{i}") for i in range(BATCH)], sem("d_in")
        d_wq, d_wo = [sem("d_wq0"), sem("d_wq1")], [sem("d_wo0"), sem("d_wo1")]
        alone_pool, alone_act, alone_sp = sem("alone_pool"), sem("alone_act"), sem("alone_sp")
        dve_own, set_up, tanhed, stats, rooted = sem("dve_own"), sem("set_up"), sem("tanhed"), sem("stats"), sem("rooted")
        z_ready, rt_made = sem("z_ready"), sem("rt_made")
        wq_high, wq_split, wo_high, wo_split = (sem(n) for n in ("wq_high", "wq_split", "wo_high", "wo_split"))
        job_done, job_full, job_high, job_low, vt_high, vt_low = (
            sem(n) for n in ("job_done", "job_full", "job_high", "job_low", "vt_high", "vt_low"))
        s_done, s_read, exp_done, turned, hi_done, lo_done = (
            sem(n) for n in ("s_done", "s_read", "exp_done", "turned", "hi_done", "lo_done"))
        pv_done, o_high, o_split, y_done, y_added = (sem(n) for n in ("pv_done", "o_high", "o_split", "y_done", "y_added"))
        block = ctx.enter_context(nc.Block())

        STEPS = 2 * TPB
        UNITS = STEPS // 2
        LAG = 2
        SPILL = LAG + 2
        PAIRS_H = R_HEADS // 2
        GRP = ((0, 4), (4, 8), (8, R_BLK))
        CUT = ((0, CH), (CH, 2 * CH), (2 * CH, R_KV))
        JOBS = [("k", *CUT[0]), ("k", *CUT[1]), ("k", *CUT[2]), ("q", *CUT[0]), ("q", *CUT[1]),
                ("v", *CUT[0]), ("v", *CUT[1]), ("v", *CUT[2])] + [("t", lo * P, hi * P) for lo, hi in GRP]
        XJOBS = [(k, lo, hi) for lo, hi in CUT for k in range(KT)]
        NX, NF, NS, NV, NJ = len(XJOBS), 8, 5, 3, len(JOBS)
        PLAN = [[0], [1], [2, 3], [4], [5], [6], [7, 8], [9, 10]]
        XPLAN = [[0, 1], [2, 3], [4, 5]]
        PLAN_AFTER_X = [[], [], [], [0, 1], [2, 3, 4], [5, 6], [7, 8], [9, 10]]

        class Head:

            def __init__(self, b, hp, j):
                self.j, self.hp, self.h, self.it = j, hp, hp * 2 + j, b * PAIRS_H + hp
                self.first = isinstance(hp, int) and hp == 0 and j == 0
                self.job, self.full, self.split = (2 * n * self.it + NX * (b + 1) + n * j for n in (NJ, NF, NS))
                self.vt = 2 * NV * self.it + NV * j
                self.xfull = 2 * NF * self.it + NX * b

        class Inputs:

            def __init__(self, b):
                self.b = b
                self.job, self.full, self.split = (2 * n * PAIRS_H * b + NX * b for n in (NJ, NF, NS))
                self.vt = 2 * NV * PAIRS_H * b

        def walk(part, b, hp):
            if part != "start":
                for w in range(SPILL, STEPS):
                    s, jobs, norm = w % TPB, [], []
                    if w < TPB:
                        jobs = [(Head(b, hp, 1), m) for m in PLAN[s]]
                        norm = [(b + 1, s - SPILL)] if part == "cross" and s < SPILL + 2 else []
                    elif part == "body":
                        jobs = [(Head(b, hp + 1, 0), m) for m in PLAN[s]]
                    elif part == "cross":
                        jobs = [(Inputs(b + 1), m) for m in (XPLAN[s] if s < len(XPLAN) else ())]
                        jobs += [(Head(b + 1, 0, 0), m) for m in PLAN_AFTER_X[s]]
                        norm = [(b + 1, 2), (b + 1, 3)] if s == 0 else []
                    yield w, b, b * PAIRS_H + hp, b, jobs, norm
            if part == "end":
                for w in range(STEPS, STEPS + SPILL):
                    yield w, b, b * PAIRS_H + hp, b, [], []
            else:
                nb, nhp = {"start": (b, hp), "body": (b, hp + 1), "cross": (b + 1, 0)}[part]
                for w in range(SPILL):
                    yield w, nb, nb * PAIRS_H + nhp, None if part == "start" else b, [(Head(nb, nhp, 1), m) for m in PLAN[w]], []

        def run(eng, first, step):
            x0, h0 = Inputs(0), Head(0, 0, 0)
            first([(x0, m) for m in range(NX)] + [(h0, m) for m in range(NJ)])
            for s in walk("start", 0, 0):
                step(*s)
            with eng.Fori(0, BATCH - 1) as b:
                with eng.Fori(0, PAIRS_H - 1) as hp:
                    for s in walk("body", b, hp):
                        step(*s)
                for s in walk("cross", b, PAIRS_H - 1):
                    step(*s)
            with eng.Fori(0, PAIRS_H - 1) as hp:
                for s in walk("body", BATCH - 1, hp):
                    step(*s)
            for s in walk("end", BATCH - 1, PAIRS_H - 1):
                step(*s)

        @block.sync
        def _(sp):
            xt = A["x"].rearrange("b (t p) d -> p (b t) d", p=P)
            sp.dma_start(xres[:, 0:TPB, :], xt[:, 0:TPB, :]).then_inc(d_x[0], 16)
            sp.dma_start(cA, A["ctx_1024"][:, 0:P, :].rearrange("b j d -> j b d")).then_inc(d_in, 16)
            sp.dma_start(cB, A["ctx_1024"][:, P:CTX, :].rearrange("b j d -> j b d")).then_inc(d_in, 16)
            sp.dma_start(tbo[:, :], A["L0_xattn_bo"].partition_broadcast(P)).then_inc(d_in, 16)
            with nc.allow_non_contiguous_dma(reason="small columns"):
                sp.dma_start(tg[:, :], A["g_xattn"][0:1].partition_broadcast(P)).then_inc(d_in, 16)
                for i, n in enumerate(("gamma_lat", "beta_lat", "gamma_media", "beta_media")):
                    sp.dma_start(cols[:, i, :], A["L0_xattn_" + n].rearrange("(k p) -> p k", p=P)).then_inc(d_in, 16)
                sp.dma_start(bias[:, 0, :], A["L0_xattn_bq"].rearrange("(h p) -> p h", p=P)).then_inc(d_in, 16)
                sp.dma_start(bias[:, 1:3, :], A["L0_xattn_bkv"].rearrange("(i h p) -> p i h", p=P, i=2)).then_inc(d_in, 16)
            for i in range(1, BATCH):
                sp.dma_start(xres[:, TPB * i:TPB * (i + 1), :], xt[:, TPB * i:TPB * (i + 1), :]).then_inc(d_x[i], 16)
            wq = A["L0_xattn_Wq"].rearrange("(k p) n -> p k n", p=P)
            wkv = A["L0_xattn_Wkv"].rearrange("(k p) n -> p k n", p=P)
            wo = A["L0_xattn_Wo"].rearrange("(h p) n -> p h n", p=P)
            with sp.Fori(0, BATCH) as b:
                sp.dma_start(mA[:, :], A["ctx_1024"][bass.ds(b, 1), 0:P, :].rearrange("b j d -> (b j) d")).then_inc(d_m, 16)
                sp.dma_start(mB[:, :], A["ctx_1024"][bass.ds(b, 1), P:CTX, :].rearrange("b j d -> (b j) d")).then_inc(d_m, 16)
                with sp.Fori(0, PAIRS_H) as hp:
                    for j in range(2):
                        n = Head(b, hp, j)
                        raw = wraw[:, j, :, :].rearrange("p w (k n) -> p w k n", k=KT)
                        sp.wait_ge(wq_split, 2 * n.it + j + 1)
                        sp.dma_start(raw[:, 0, :, :], wq[:, :, bass.ds(n.h * P, P)]).then_inc(d_wq[j], 16)
                        sp.dma_start(raw[:, 1, :, :], wkv[:, :, bass.ds(n.h * P, P)]).then_inc(d_wq[j], 16)
                        sp.dma_start(raw[:, 2, :, :], wkv[:, :, bass.ds(n.h * P + R_INNER, P)]).then_inc(d_wq[j], 16)
                        sp.wait_ge(wo_split, 2 * n.it + j + 1)
                        sp.dma_start(wraw[:, j, 3, :], wo[:, bass.ds(n.h, 1), :]).then_inc(d_wo[j], 16)
                sp.wait_ge(job_done, Inputs(b).job + NX)
                sp.sem_inc(alone_sp, 1)
        ND = 10

        def split_parts(n, m):
            if isinstance(n, Inputs):
                k, lo, hi = XJOBS[m]
                return full[:, m % 2, 0:hi - lo], kvh[:, k, lo:hi], kvl[:, k, lo:hi]
            kind, lo, hi = JOBS[m]
            h, l = {"k": (kh, kl), "q": (qh, ql)}[kind]
            return full[:, (NS * n.j + m) % 2, 0:hi - lo], h[:, n.j, lo:hi], l[:, n.j, lo:hi]

        def bank(n, m):
            if isinstance(n, Inputs):
                return ps[:, JOB + m % 2, :]
            return ps[:, JOB + (NX + NJ * n.j + m) % 2, :]

        @block.gpsimd
        def _(pool):
            pool.sem_inc(wq_split, 2)
            pool.sem_inc(wo_split, 2)
            pool.sem_inc(job_low, 2)
            for i in range(4):
                pool.memset(p[:, i, R_KV + (2 * NST, NST, 0, 0)[i]:R_ROW], 0.0).then_inc(set_up, 1)
            pool.memset(vf[:, R_KV:R_ROW], 0.0).then_inc(set_up, 1)

            def alone():
                pool.sem_inc(alone_pool, 1)

            def split_q(it, j):
                pool.wait_ge(d_wq[j], 48 * (it + 1))
                alone()
                pool.tensor_copy(wh[:, j, 0:3, :], wraw[:, j, 0:3, :]).then_inc(wq_high, 1)
                pool.wait_ge(wq_high, 2 * it + j + 1)
                pool.tensor_tensor(wl[:, j, 0:3, :], wraw[:, j, 0:3, :], wh[:, j, 0:3, :].bitcast(F32), ALU.subtract).then_inc(wq_split, 1)

            def low(n, m):
                f, h, l = split_parts(n, m)
                pool.wait_ge(job_high, n.split + m + 1)
                pool.tensor_tensor(l, f, h.bitcast(F32), ALU.subtract).then_inc(job_low, 1)

            def head(n, more):
                for m in range(NS):
                    low(n, m)
                pool.wait_ge(y_done, UNITS * n.it + UNITS // 2 * (n.j + 1))
                pool.wait_ge(d_wo[n.j], 16 * (n.it + 1))
                alone()
                pool.tensor_copy(wh[:, n.j, 3, :], wraw[:, n.j, 3, :]).then_inc(wo_high, 1)
                pool.wait_ge(wo_high, 2 * n.it + n.j + 1)
                pool.tensor_tensor(wl[:, n.j, 3, :], wraw[:, n.j, 3, :], wh[:, n.j, 3, :].bitcast(F32), ALU.subtract).then_inc(wo_split, 1)
                if more:
                    pool.wait_ge(job_done, n.job + NF)
                    split_q(n.it + 1, n.j)

            def inputs(b):
                for m in range(NX):
                    low(Inputs(b), m)

            split_q(0, 0)
            split_q(0, 1)
            with pool.Fori(0, BATCH - 1) as b:
                inputs(b)
                with pool.Fori(0, PAIRS_H) as hp:
                    for j in range(2):
                        head(Head(b, hp, j), True)
            inputs(BATCH - 1)
            with pool.Fori(0, PAIRS_H - 1) as hp:
                for j in range(2):
                    head(Head(BATCH - 1, hp, j), True)
            for j in range(2):
                head(Head(BATCH - 1, PAIRS_H - 1, j), False)

        @block.scalar
        def _(act):
            act.wait_ge(d_in, 16 * ND)
            act.activation(tg[:, :], tg[:, :], ACT.Tanh).then_inc(tanhed, 1)
            act.wait_ge(stats, 1)
            act.activation(root[:, :], var[:, :], ACT.Sqrt).then_inc(rooted, 1)
            act.wait_ge(stats, 2)
            act.activation(root[:, 0:TILES], var[:, 0:TILES], ACT.Sqrt).then_inc(rooted, 1)
            act.wait_ge(tanhed, 2)

            def job(n, m):
                act.wait_ge(job_done, n.job + m + 1)
                if isinstance(n, Inputs):
                    k, lo, hi = XJOBS[m]
                    g = 0 if hi <= SEQ else 2
                    act.wait_ge(job_low, n.split + m + 1)
                    act.activation(full[:, m % 2, 0:hi - lo], bank(n, m)[:, 0:hi - lo], ACT.Identity,
                                   bias=cols[:, g + 1, k:k + 1], scale=cols[:, g, k:k + 1]).then_inc(job_full, 1)
                    return
                kind, lo, hi = JOBS[m]
                if kind == "t":
                    act.activation(vh[:, n.j, lo:hi], bank(n, m)[:, 0:hi - lo], ACT.Copy).then_inc(vt_high, 1)
                    return
                if kind == "v":
                    dst = vf[:, lo:hi]
                else:
                    act.wait_ge(job_low, n.split + m + 1)
                    dst = split_parts(n, m)[0]
                i = "qkv".index(kind)
                act.sem_inc(alone_act, 1)
                act.activation(dst, bank(n, m)[:, 0:hi - lo], ACT.Identity, bias=bias[:, i, bass.ds(n.h, 1)],
                               scale=R_SCALE if kind == "q" else 1.0).then_inc(job_full, 1)

            def step(w, b, it, blag, jobs, norm):
                for n, m in jobs:
                    job(n, m)
                v = w - LAG
                if (blag is not None or v >= 0) and v < STEPS:
                    for g, (lo, hi) in enumerate(GRP):
                        act.wait_ge(turned, 3 * (STEPS * it + v) + g + 1 + 12)
                        act.activation(pth[:, (v // 2) % 2, lo:hi, (v % 2) * P:(v % 2 + 1) * P],
                                       ps[:, TURN + (v + g) % 2, 0:(hi - lo) * P].rearrange("p (n t) -> p n t", t=P),
                                       ACT.Copy).then_inc(hi_done, 1)
                if w < STEPS:
                    act.wait_ge(s_read, STEPS * it + w + 1 + 1)
                    act.activation(p[:, w % 4, 0:R_KV], p[:, w % 4, 0:R_KV], ACT.Exp, bias=nmx[:, w % 2:w % 2 + 1], scale=-1.0,
                                   accum_out=sums[:, w:w + 1]).then_inc(exp_done, 1)
                u = (w - LAG - 2) // 2
                if w % 2 == 0 and (blag is not None or u >= 0):
                    act.wait_ge(pv_done, UNITS * it + u + 1)
                    act.activation(oh[:, :], ps[:, PV, 0:2 * P], ACT.Copy).then_inc(o_high, 1)

            def first(jobs):
                for n, m in jobs:
                    job(n, m)

            run(act, first, step)

        @block.vector
        def _(dve):
            own = Chain(dve, dve_own)
            dve.sem_inc(s_read, 1)
            dve.sem_inc(lo_done, 2)
            dve.sem_inc(y_added, 1)
            own.link(dve.memset(mv[:, :, :], 1.0))
            for t in range(TPB):
                if t == 0:
                    dve.wait_ge(d_x[0], 16)
                own.step(dve.bn_stats(st[:, t, :], xres[:, t, :]))
            dve.wait_ge(d_in, 16 * ND)
            for b in range(BATCH):
                own.step(dve.bn_stats(st[:, TILES + b, :], cA[:, b, :]))
                own.step(dve.bn_stats(st[0:CTX - P, TILES + BATCH + b, :], cB[:, b, :]))
            for t in range(TPB, TILES):
                if t % TPB == 0:
                    dve.wait_ge(d_x[t // TPB], 16)
                own.step(dve.bn_stats(st[:, t, :], xres[:, t, :]))
            own.wait()
            for n in range(NST):
                rows = slice(0, P) if n < TILES + BATCH else slice(0, CTX - P)
                own.step(dve.bn_aggr(mv[rows, n, :], st[rows, n, :]))
            own.wait()
            dve.tensor_scalar(var[:, :], mv[:, :, 1], EPS, None, ALU.add).then_inc(stats, 1)
            dve.wait_ge(rooted, 1)
            newton_rsqrt(own, dve, var[:, :], root[:, :], r1[:, :])
            x1, once = mv[:, 0:TILES, 1], r1[:, 0:TILES]
            own.link(dve.tensor_tensor(r2[:, :], x1, once, ALU.mult))
            own.link(dve.tensor_tensor(r2[:, :], r2[:, :], once, ALU.mult))
            own.link(dve.tensor_scalar(var[:, 0:TILES], r2[:, :], EPS, None, ALU.add))
            dve.sem_inc(stats, 1)
            dve.wait_ge(rooted, 2)
            newton_rsqrt(own, dve, var[:, 0:TILES], root[:, 0:TILES], r2[:, :])
            own.link(dve.tensor_tensor(once, once, r2[:, :], ALU.mult))
            dve.wait_ge(tanhed, 1)
            own.link(dve.tensor_scalar(tbo[:, :], tbo[:, :], tg[:, 0:1], None, ALU.mult))
            dve.tensor_scalar(bias[:, 0, :], bias[:, 0, :], R_SCALE, None, ALU.mult).then_inc(tanhed, 1)
            dve.wait_ge(set_up, 5)

            def normalise(b, i):
                for t in (2 * i, 2 * i + 1):
                    n = TPB * b + t
                    last = dve.tensor_scalar(z[:, t % (TPB // 2), :], xres[:, bass.ds(n, 1), :], mv[:, bass.ds(n, 1), 0], r1[:, bass.ds(n, 1)],
                                             ALU.subtract, ALU.mult)
                last.then_inc(z_ready, 1)
                dve.wait_ge(z_ready, (TPB // 2 + 1) * b + i + 1)
                part = xres[:, bass.ds(TPB * b + 2 * i, 2), :]
                dve.tensor_tensor(part, part, tbo[:, :].unsqueeze(1).broadcast_to([P, 2, DIM]), ALU.add)
                if i == TPB // 2 - 1:
                    dve.wait_ge(d_m, 32 * (b + 1))
                    for m, rows, at in ((mA, slice(0, P), TILES), (mB, slice(0, CTX - P), TILES + BATCH)):
                        last = dve.tensor_scalar(m[:, :], m[:, :], mv[rows, bass.ds(b + at, 1), 0], r1[rows, bass.ds(b + at, 1)],
                                                 ALU.subtract, ALU.mult)
                    last.then_inc(z_ready, 1)

            def job(n, m):
                if not isinstance(n, Inputs) and JOBS[m][0] == "t":
                    kind, lo, hi = JOBS[m]
                    dve.wait_ge(vt_high, n.vt + m - NF + 1)
                    dve.tensor_tensor(vl[:, n.j, lo:hi], bank(n, m)[:, 0:hi - lo], vh[:, n.j, lo:hi].bitcast(F32),
                                      ALU.subtract).then_inc(vt_low, 1)
                elif isinstance(n, Inputs) or JOBS[m][0] != "v":
                    f, h, l = split_parts(n, m)
                    dve.wait_ge(job_full, n.full + m + 1)
                    dve.tensor_copy(h, f).then_inc(job_high, 1)

            def lows(it, v, gs):
                for g in gs:
                    lo, hi = GRP[g]
                    dve.wait_ge(hi_done, 3 * (STEPS * it + v) + g + 1)
                    dst = (slice(None), (v // 2) % 2, slice(lo, hi), slice((v % 2) * P, (v % 2 + 1) * P))
                    dve.tensor_tensor(ptl[dst], ps[:, TURN + (v + g) % 2, 0:(hi - lo) * P].rearrange("p (n t) -> p n t", t=P),
                                      pth[dst].bitcast(F32), ALU.subtract).then_inc(lo_done, 1)

            def step(w, b, it, blag, jobs, norm):
                for n, m in jobs:
                    job(n, m)
                for n in norm:
                    normalise(*n)
                behind = blag is not None
                v = w - LAG
                if (behind or v >= 0) and v < STEPS:
                    lows(it, v, (0, 1))
                if w < STEPS:
                    W = STEPS * it + w
                    dve.wait_ge(s_done, W + 1)
                    dve.wait_ge(turned, 3 * W + 3)
                    dve.tensor_scalar(p[:, w % 4, 0:R_KV], scores, -1.0, R_BIG, ALU.mult, ALU.min,
                                      accum_out=nmx[:, w % 2:w % 2 + 1]).then_inc(s_read, 1)
                if (behind or v >= 0) and v < STEPS:
                    lows(it, v, (2,))
                u = (w - LAG - 2) // 2
                if w % 2 == 0 and (behind or u >= 0):
                    dve.wait_ge(o_high, UNITS * it + u + 1)
                    dve.tensor_tensor(ol[:, :], ps[:, PV, 0:2 * P], oh[:, :].bitcast(F32), ALU.subtract).then_inc(o_split, 1)
                u = (w - LAG - 3) // 2
                if w % 2 == 1 and (behind or u >= 0):
                    t, s = 2 * (u % (UNITS // 2)), 2 * (u % UNITS)
                    U = UNITS * it + u
                    dve.reciprocal(rt[:, :], sums[:, s:s + 2]).then_inc(rt_made, 1)
                    dve.wait_ge(rt_made, 2 * U + 1)
                    dve.tensor_scalar(rt[:, :], rt[:, :], tg[:, 0:1], None, ALU.mult).then_inc(rt_made, 1)
                    dve.wait_ge(rt_made, 2 * U + 2)
                    dve.wait_ge(y_done, U + 1 + UNITS)
                    for i in range(2):
                        part = xres[:, bass.ds(TPB * (b if u >= 0 else blag) + t + i, 1), :].rearrange("p a d -> p (a d)")
                        last = dve.scalar_tensor_tensor(part, ps[:, PV, i * DIM:(i + 1) * DIM], rt[:, i:i + 1], part,
                                                        ALU.mult, ALU.add)
                    last.then_inc(y_added, 1)

            def first(jobs):
                for n, m in jobs:
                    if n is jobs[0][0] and m in (0, 2):
                        normalise(0, m)
                        normalise(0, m + 1)
                    job(n, m)

            run(dve, first, step)

        @block.tensor
        def _(pe):
            pe.sem_inc(y_done, UNITS)
            pe.sem_inc(turned, 12)

            def job(n, m):
                out = bank(n, m)
                if isinstance(n, Inputs):
                    k, lo, hi = XJOBS[m]
                    if m >= 2:
                        pe.wait_ge(job_full, n.full + m - 1)
                    elif not (isinstance(n.b, int) and n.b == 0):
                        pe.wait_ge(vt_low, n.vt - 1 + m)
                    cut = slice(k * P, (k + 1) * P)
                    if hi <= SEQ:
                        pe.wait_ge(z_ready, (TPB // 2 + 1) * n.b + hi // P // 2)
                        for t in range(lo // P, hi // P):
                            last = pe.transpose(out[:, t * P - lo:(t + 1) * P - lo], z[:, t % (TPB // 2), cut], ident[:, :])
                    else:
                        pe.wait_ge(z_ready, (TPB // 2 + 1) * (n.b + 1))
                        pe.transpose(out[:, 0:P], mA[:, cut], ident[:, :])
                        last = pe.transpose(out[:, P:CTX], mB[:, cut], ident[0:CTX - P, 0:CTX - P])
                    last.then_inc(job_done, 1)
                    return
                kind, lo, hi = JOBS[m]
                if m >= 2:
                    if JOBS[m - 2][0] == "t":
                        pe.wait_ge(vt_low, n.vt + m - 2 - NF + 1)
                    else:
                        pe.wait_ge(job_full, n.full + m - 1)
                elif n.first:
                    pe.wait_ge(job_full, n.xfull + NX - 1 + m)
                else:
                    pe.wait_ge(vt_low, n.vt - 1 + m)
                if m == 0:
                    pe.wait_ge(wq_split, 2 * n.it + n.j + 1 + 2)
                    if n.first:
                        pe.wait_ge(job_low, n.split + 2)
                if kind == "t":
                    if m == NF:
                        pe.wait_ge(job_full, n.full + NF)
                    for c in range(lo, hi, P):
                        last = pe.transpose(out[:, c - lo:c - lo + P], vf[:, c:c + P], ident[:, :])
                else:
                    i = "qkv".index(kind)
                    s = 0
                    for k in range(KT):
                        for w, x in ((wh, kvh), (wh, kvl), (wl, kvh)):
                            last = pe.matmul(out[:, 0:hi - lo], w[:, n.j, i, k * P:(k + 1) * P], x[:, k, lo:hi],
                                             start=(s == 0), stop=(s == 5))
                            s += 1
                last.then_inc(job_done, 1)

            def turn(it, v, gs):
                V = STEPS * it + v
                for g in gs:
                    lo, hi = GRP[g]
                    if g == 0:
                        pe.wait_ge(exp_done, V + 1)
                    pe.wait_ge(lo_done, 3 * V + g + 1)
                    for n in range(lo, hi):
                        last = pe.transpose(ps[:, TURN + (v + g) % 2, (n - lo) * P:(n - lo + 1) * P],
                                            p[:, v % 4, n * P:(n + 1) * P], ident[:, :])
                    last.then_inc(turned, 1)

            def score(it, w):
                j, t = w // TPB, w % TPB
                pe.wait_ge(s_read, STEPS * it + w + 1)
                for n, (lo, hi) in enumerate(CUT):
                    for i, (q, k) in enumerate(((qh, kh), (qh, kl), (ql, kh))):
                        last = pe.matmul(ps[:, n, 0:hi - lo], q[:, j, t * P:(t + 1) * P], k[:, j, lo:hi],
                                         start=(i == 0), stop=(i == 2))
                last.then_inc(s_done, 1)

            def values(it, u):
                j = u % UNITS // (UNITS // 2)
                U = UNITS * it + u
                if u % (UNITS // 2) == 0:
                    pe.wait_ge(vt_low, 2 * NV * it + NV * (j + 1))
                pe.wait_ge(lo_done, 6 * (U + 1) + 2)
                pe.wait_ge(y_added, U + 1)
                for n in range(R_BLK):
                    for i, (v, x) in enumerate(((vh, pth), (vh, ptl), (vl, pth))):
                        last = pe.matmul(ps[:, PV, 0:2 * P], v[:, j, n * P:(n + 1) * P], x[:, u % 2, n, :],
                                         start=(n == 0 and i == 0), stop=(n == R_BLK - 1 and i == 2))
                last.then_inc(pv_done, 1)

            def project(it, u):
                j = u % UNITS // (UNITS // 2)
                U = UNITS * it + u
                if u % (UNITS // 2) == 0:
                    pe.wait_ge(wo_split, 2 * it + j + 1 + 2)
                pe.wait_ge(o_split, U + 1)
                for t in range(2):
                    for i, (o, w) in enumerate(((oh, wh), (oh, wl), (ol, wh))):
                        last = pe.matmul(ps[:, PV, t * DIM:(t + 1) * DIM], o[:, t * P:(t + 1) * P], w[:, j, 3, :],
                                         start=(i == 0), stop=(i == 2))
                last.then_inc(y_done, 1)

            def step(w, b, it, blag, jobs, norm):
                for n, m in jobs:
                    job(n, m)
                behind = blag is not None
                v = w - LAG
                if (behind or v >= 0) and v < STEPS:
                    turn(it, v, (0, 1))
                if w < STEPS:
                    if w % TPB == 0:
                        pe.wait_ge(job_low, 2 * NS * it + NX * (b + 1) + NS * (w // TPB + 1) + 2)
                    score(it, w)
                if (behind or v >= 0) and v < STEPS:
                    turn(it, v, (2,))
                u = (w - LAG - 2) // 2
                if w % 2 == 0 and (behind or u >= 0):
                    values(it, u)
                u = (w - LAG - 3) // 2
                if w % 2 == 1 and (behind or u >= 0):
                    project(it, u)

            def first(jobs):
                for n, m in jobs:
                    job(n, m)

            run(pe, first, step)


EXPERTS, TOPK, EH = 64, 8, 64
SHARED, SH = 2, 512
PAIRS = EXPERTS * EH // P
GB = 8
ROUTED = PAIRS // GB
GROUPS = ROUTED + SHARED * SH // P // GB
FREE = 2


def moe_stage(nc, xres, ident, A):
    with ExitStack() as ctx:
        def sb(name, shape, dt=F32):
            return ctx.enter_context(nc.sbuf_tensor("moe_" + name, shape, dt))

        def sem(name):
            return nc.alloc_semaphore("moe_" + name)

        lnT = sb("lnT", [P, KT, TOKENS])
        cwT = sb("cwT", [P, TOKENS], F32R)
        pick = sb("pick", [P, EXPERTS, EH], F32R)
        w1r, w2r = sb("w1r", [P, KT, GB * P]), sb("w2r", [P, GB, DIM])
        w1h, w1l = sb("w1h", [P, KT, GB * P], F32R), sb("w1l", [P, KT, GB * P], F32R)
        w2h, w2l = sb("w2h", [P, GB, DIM], F32R), sb("w2l", [P, GB, DIM], F32R)
        xh, xl = sb("xh", [P, 2, KT, CH], F32R), sb("xl", [P, 2, KT, CH], F32R)
        sil, gf = sb("sil", [P, 2, CH]), sb("gf", [P, 2, CH])
        gh, gl = sb("gh", [P, 2, CH], F32R), sb("gl", [P, 2, CH], F32R)
        stage = sb("stage", [P, KT, CH])
        rw, rb = sb("rw", [P, KT, EXPERTS]), sb("rb", [P, EXPERTS])
        b1, sb1 = sb("b1", [P, PAIRS]), sb("sb1", [P, GB])
        b2r, b2h, b2l = sb("b2r", [P, DIM]), sb("b2h", [P, DIM], F32R), sb("b2l", [P, DIM], F32R)
        sb2 = sb("sb2", [P, SHARED, KT])
        tg, tsb2 = sb("tg", [P, 1]), sb("tsb2", [P, KT])
        st, mv, rstd = sb("st", [P, TILES, 6]), sb("mv", [P, TILES, 2]), sb("rstd", [P, TILES])
        var, root = sb("var", [P, TILES]), sb("root", [P, TILES])
        lg, pr, rep = (sb(n, [P, TPC, EXPERTS]) for n in ("lg", "pr", "rep"))
        s4 = sb("s4", [P, TPC])
        top = sb("top", [P, TPC, TOPK])
        cwp = sb("cwp", [P, TPC, 2, EXPERTS], F32R)
        xn = sil[:, :, :].rearrange("p a c -> p (a c)").rearrange("p (t d) -> p t d", d=DIM)
        ps = ctx.enter_context(nc.psum_tensor("moe_ps", [P, 8, CH], F32))
        HID, REP, OUT, TURN = 0, 2, 4, 6

        d_const, d_w, w_high, w_split = sem("d_const"), sem("d_w"), sem("w_high"), sem("w_split")
        dve_own, act_own, pool_own = sem("dve_own"), sem("act_own"), sem("pool_own")
        alone_pool, alone_dve = sem("alone_pool"), sem("alone_dve")
        stats, rooted = sem("stats"), sem("rooted")
        pick_set, consts, b2_split = sem("pick_set"), sem("consts"), sem("b2_split")
        normed, turned, staged, routed, shifted, exped = (
            sem(n) for n in ("normed", "turned", "staged", "routed", "shifted", "exped"))
        cw_ready, cw_turned, cw_kept = sem("cw_ready"), sem("cw_turned"), sem("cw_kept")
        x_free, x_high, x_split = sem("x_free"), sem("x_high"), sem("x_split")
        hid_done, rep_done, silu_done, gate_done, high_done, g_split = (
            sem(n) for n in ("hid_done", "rep_done", "silu_done", "gate_done", "high_done", "g_split"))
        out_done, y_kept, y_turned, y_added = sem("out_done"), sem("y_kept"), sem("y_turned"), sem("y_added")
        block = ctx.enter_context(nc.Block())
        NCONST = 9

        @block.sync
        def _(sp):
            for dst, src in ((rw[:, :, :], A["L0_ffn_router_w"].rearrange("(k p) e -> p k e", p=P)),
                             (rb[:, :], A["L0_ffn_router_b"].partition_broadcast(P)),
                             (tg[:, :], A["g_ffn"][0:1].partition_broadcast(P)),
                             (b2r[0:EXPERTS, :], A["L0_ffn_b2"]), (b2r[EXPERTS:P, :], A["L0_ffn_b2"]),
                             (sb1[:, :], A["L0_ffn_sb1"].rearrange("s (b p) -> p (s b)", p=P)),
                             (sb2[:, 0, :], A["L0_ffn_sb2"][0].rearrange("(k p) -> p k", p=P)),
                             (sb2[:, 1, :], A["L0_ffn_sb2"][1].rearrange("(k p) -> p k", p=P)),
                             (b1[:, :], A["L0_ffn_b1"].rearrange("(q e) h -> (e h) q", e=2))):
                with nc.allow_non_contiguous_dma(reason='small columns'):
                    sp.dma_start(dst, src).then_inc(d_const, 16)
            for g in range(GROUPS):
                if g:
                    sp.wait_ge(w_split, 2 * g)
                for k in range(KT):
                    if g < ROUTED:
                        e = slice(2 * GB * g, 2 * GB * (g + 1))
                        src = A["L0_ffn_w1"][e, k * P:(k + 1) * P, :]
                    else:
                        src = A["L0_ffn_sw1"][:, k * P:(k + 1) * P, :]
                    sp.dma_start(w1r[:, k, :].rearrange("p (e h) -> p e h", h=src.shape[2]),
                                 src.rearrange("e p h -> p e h")).then_inc(d_w, 16)
                if g < ROUTED:
                    src = A["L0_ffn_w2"][e].rearrange("(q e) h d -> (e h) q d", e=2)
                else:
                    src = A["L0_ffn_sw2"].rearrange("s (b p) d -> p (s b) d", p=P)
                sp.dma_start(w2r[:, :, :], src).then_inc(d_w, 16)

        @block.gpsimd
        def _(pool):
            own = Chain(pool, pool_own)
            pool.sem_inc(x_free, FREE)
            one = lnT[:, 0, :].rearrange("p (e h) -> p e h", h=EH)
            own.link(pool.memset(one, 0.0))
            for part in (0, EXPERTS):
                own.link(pool.affine_select(out=one, in_=one, compare_op=ALU.not_equal, fill=1.0, base=-part,
                                            pattern=[[-1, EXPERTS], [0, EH]], channel_multiplier=1))
            pool.tensor_copy(pick[:, :, :], one).then_inc(pick_set, 1)
            pool.wait_ge(cw_kept, CHUNKS)
            for g in range(GROUPS):
                with pool.Fori(0, CHUNKS // 2) as cc:
                    for j in range(2):
                        n = g * CHUNKS + 2 * cc + j
                        src = lnT[:, :, bass.ds((2 * cc + j) * CH, CH)]
                        pool.wait_ge(x_free, n + 1)
                        pool.tensor_copy(xh[:, j, :, :], src).then_inc(x_high, 1)
                        pool.wait_ge(x_high, n + 1)
                        pool.sem_inc(alone_pool, 1)
                        pool.tensor_tensor(xl[:, j, :, :], src, xh[:, j, :, :].bitcast(F32), ALU.subtract).then_inc(x_split, 1)

        @block.scalar
        def _(act):
            own = Chain(act, act_own)
            act.sem_inc(silu_done, FREE)
            act.sem_inc(y_kept, FREE)
            act.wait_ge(d_const, 16 * NCONST)
            act.activation(tg[:, :], tg[:, :], ACT.Tanh).then_inc(consts, 1)
            act.wait_ge(pick_set, 1)
            act.wait_ge(stats, 1)
            act.activation(root[:, :], var[:, :], ACT.Sqrt).then_inc(rooted, 1)
            with act.Fori(0, CHUNKS) as c:
                for k in range(KT):
                    act.wait_ge(turned, 2 * c + k + 1)
                    act.activation(stage[:, k, :], ps[:, k, :], ACT.Copy).then_inc(staged, 1)
                for k in range(KT):
                    act.activation(lnT[:, k, bass.ds(c * CH, CH)], ps[:, k, :], ACT.Copy).then_inc(staged, 1)
                act.wait_ge(shifted, c + 1)
                act.activation(pr[:, :, :], lg[:, :, :], ACT.Exp).then_inc(exped, 1)
                act.wait_ge(cw_turned, c + 1)
                act.activation(cwT[:, bass.ds(c * CH, CH)], ps[:, 3, :], ACT.Copy).then_inc(cw_kept, 1)
            for g in range(GROUPS):
                act.wait_ge(d_w, 48 * (g + 1))
                if g:
                    act.wait_ge(out_done, g * CHUNKS * GB + FREE)
                act.activation(w1h[:, :, :], w1r[:, :, :], ACT.Copy).then_inc(w_high, 1)
                act.activation(w2h[:, :, :], w2r[:, :, :], ACT.Copy).then_inc(w_high, 1)
                act.wait_ge(consts, 2)
                with act.Fori(0, CHUNKS // 2) as cc:
                    for j in range(2):
                        n = g * CHUNKS + 2 * cc + j
                        for q in range(GB):
                            u = n * GB + q
                            act.wait_ge(hid_done, u + 1)
                            if g < ROUTED:
                                act.wait_ge(gate_done, u + 1)
                                dst, bias = sil, b1[:, g * GB + q:g * GB + q + 1]
                            else:
                                act.wait_ge(g_split, u + 1)
                                dst, bias = gf, sb1[:, q:q + 1]
                            act.activation(dst[:, q % 2, :], ps[:, HID + q % 2, :], ACT.Silu, bias=bias).then_inc(silu_done, 1)
                        act.wait_ge(out_done, GB * n + GB + FREE)
                        act.wait_ge(y_turned, 2 * n + FREE)
                        for k in range(KT):
                            bias = tsb2[:, k:k + 1] if g == GROUPS - 1 else 0.0
                            act.activation(stage[:, k, :], ps[:, OUT + k, :], ACT.Identity, bias=bias,
                                           scale=tg[:, 0:1]).then_inc(y_kept, 1)

        @block.vector
        def _(dve):
            own = Chain(dve, dve_own)
            dve.sem_inc(gate_done, FREE)
            dve.sem_inc(g_split, FREE)
            dve.sem_inc(y_added, FREE)
            dve.wait_ge(consts, 1)
            own.link(dve.tensor_tensor(tsb2[:, :], sb2[:, 0, :], sb2[:, 1, :], ALU.add))
            dve.tensor_scalar(tsb2[:, :], tsb2[:, :], tg[:, 0:1], None, ALU.mult).then_inc(consts, 1)
            own.link(dve.tensor_copy(b2h[:, :], b2r[:, :]))
            dve.tensor_tensor(b2l[:, :], b2r[:, :], b2h[:, :].bitcast(F32), ALU.subtract).then_inc(b2_split, 1)

            def over(x, n=EXPERTS):
                return x.unsqueeze(2).broadcast_to([P, TPC, n])

            for t in range(TILES):
                own.step(dve.bn_stats(st[:, t, :], xres[:, t, :]))
            own.wait()
            for t in range(TILES):
                own.step(dve.bn_aggr(mv[:, t, :], st[:, t, :]))
            own.wait()
            dve.tensor_scalar(var[:, :], mv[:, :, 1], EPS, None, ALU.add).then_inc(stats, 1)
            dve.wait_ge(rooted, 1)
            newton_rsqrt(own, dve, var[:, :], root[:, :], rstd[:, :])

            PER = 16
            with dve.Fori(0, CHUNKS) as c:
                own.enter(c, PER)
                for t in range(TPC):
                    dve.tensor_scalar(xn[:, t, :], xres[:, bass.ds(c * TPC + t, 1), :], mv[:, bass.ds(c * TPC + t, 1), 0],
                                      rstd[:, bass.ds(c * TPC + t, 1)],
                                      ALU.subtract, ALU.mult).then_inc(normed, 1)
                dve.wait_ge(routed, c + 1)
                logits = ps[:, 2, 0:TPC * EXPERTS].rearrange("p (t e) -> p t e", e=EXPERTS)
                own.link(dve.tensor_tensor(lg[:, :, :], logits, rb[:, :].unsqueeze(1).broadcast_to([P, TPC, EXPERTS]), ALU.add))
                own.link(dve.tensor_reduce(s4[:, :], lg[:, :, :], AX.X, ALU.max))
                dve.tensor_tensor(lg[:, :, :], lg[:, :, :], over(s4[:, :]), ALU.subtract).then_inc(shifted, 1)
                dve.wait_ge(exped, c + 1)
                own.link(dve.tensor_reduce(s4[:, :], pr[:, :, :], AX.X, ALU.add))
                own.link(dve.reciprocal(s4[:, :], s4[:, :]))
                own.link(dve.tensor_tensor(pr[:, :, :], pr[:, :, :], over(s4[:, :]), ALU.mult))
                dve.sem_inc(alone_dve, 1)
                for t in range(TPC):
                    k = own.step(dve.max(top[:, t, :], pr[:, t, :]))
                own.wait()
                dve.sem_inc(alone_dve, 1)
                for t in range(TPC):
                    last = dve.match_replace(rep[:, t, :], top[:, t, :], pr[:, t, :], -1.0)
                    if t == TPC - 1:
                        own.link(last)
                own.link(dve.tensor_tensor(rep[:, :, :], rep[:, :, :], pr[:, :, :], ALU.not_equal))
                own.link(dve.tensor_tensor(pr[:, :, :], pr[:, :, :], rep[:, :, :], ALU.mult))
                own.link(dve.tensor_reduce(s4[:, :], pr[:, :, :], AX.X, ALU.add))
                own.link(dve.reciprocal(s4[:, :], s4[:, :]))
                own.link(dve.tensor_tensor(rep[:, :, :], pr[:, :, :], over(s4[:, :]), ALU.mult))
                own.link(dve.tensor_copy(cwp[:, :, 0, :], rep[:, :, :]))
                dve.tensor_tensor(cwp[:, :, 1, :], rep[:, :, :], cwp[:, :, 0, :].bitcast(F32), ALU.subtract).then_inc(cw_ready, 1)
                own.leave(CHUNKS)

            def add_y(n, c):
                for b in range(2):
                    dve.wait_ge(y_turned, 2 * n + b + 1 + FREE)
                    part = xres[:, bass.ds(c * TPC + 2 * b, 2), :].rearrange("p t d -> p (t d)")
                    dve.tensor_tensor(part, part, ps[:, TURN + b, :], ALU.add).then_inc(y_added, 1)

            for g in range(GROUPS):
                for i, (r, h, l) in enumerate(((w1r, w1h, w1l), (w2r, w2h, w2l))):
                    dve.wait_ge(w_high, 2 * g + i + 1)
                    if g and i == 0:
                        dve.wait_ge(out_done, g * CHUNKS * GB + FREE)
                    dve.tensor_tensor(l[:, :, :], r[:, :, :], h[:, :, :].bitcast(F32), ALU.subtract).then_inc(w_split, 1)
                with dve.Fori(0, CHUNKS // 2) as cc:
                    for j in range(2):
                        n = g * CHUNKS + 2 * cc + j
                        for q in range(GB):
                            u = n * GB + q
                            dve.wait_ge(silu_done, u + 1 + FREE)
                            if g < ROUTED:
                                dve.wait_ge(rep_done, u + 1)
                                dve.tensor_tensor(gf[:, q % 2, :], sil[:, q % 2, :], ps[:, REP + q % 2, :], ALU.mult).then_inc(gate_done, 1)
                                dve.wait_ge(gate_done, u + 1 + FREE)
                            dve.wait_ge(out_done, u + 1)
                            dve.tensor_copy(gh[:, q % 2, :], gf[:, q % 2, :]).then_inc(high_done, 1)
                            dve.wait_ge(high_done, u + 1)
                            dve.tensor_tensor(gl[:, q % 2, :], gf[:, q % 2, :], gh[:, q % 2, :].bitcast(F32),
                                              ALU.subtract).then_inc(g_split, 1)
                            if j == 1 and q == 1:
                                add_y(n - 1, 2 * cc)
                    add_y(n, 2 * cc + 1)

        @block.tensor
        def _(pe):
            pe.sem_inc(out_done, FREE)
            pe.sem_inc(y_turned, FREE)
            pe.wait_ge(d_const, 16 * NCONST)
            with pe.Fori(0, CHUNKS) as c:
                for t in range(TPC):
                    pe.wait_ge(normed, TPC * c + t + 1)
                for k in range(KT):
                    for t in range(TPC):
                        last = pe.transpose(ps[:, k, t * P:(t + 1) * P], xn[:, t, k * P:(k + 1) * P], ident[:, :])
                    last.then_inc(turned, 1)
                pe.wait_ge(staged, 4 * c + 2)
                for t in range(TPC):
                    for k in range(KT):
                        last = pe.matmul(ps[:, 2, t * EXPERTS:(t + 1) * EXPERTS], stage[:, k, t * P:(t + 1) * P], rw[:, k, :],
                                         start=(k == 0), stop=(k == KT - 1))
                last.then_inc(routed, 1)
                pe.wait_ge(cw_ready, c + 1)
                for t in range(TPC):
                    last = pe.transpose(ps[:, 3, t * P:(t + 1) * P],
                                        cwp[:, t, :, :].bitcast(F32).rearrange("p a e -> p (a e)"), ident[:, :])
                last.then_inc(cw_turned, 1)
                pe.wait_ge(staged, 4 * c + 4)
                pe.wait_ge(cw_kept, c + 1)
            pe.wait_ge(b2_split, 1)
            pe.wait_ge(pick_set, 1)

            def hidden(g, n, j, q, cw):
                u = n * GB + q
                if g < ROUTED:
                    pe.wait_ge(gate_done, u + 1)
                    e = 2 * (g * GB + q)
                    pe.matmul(ps[:, REP + q % 2, :], pick[:, e:e + 2, :].rearrange("p e h -> p (e h)"), cw,
                              start=True, stop=True).then_inc(rep_done, 1)
                pe.wait_ge(silu_done, u + 1)
                if q == 0:
                    pe.wait_ge(x_split, n + 1)
                i = 0
                for k in range(KT):
                    for w, x in ((w1h, xh), (w1h, xl), (w1l, xh)):
                        last = pe.matmul(ps[:, HID + q % 2, :], w[:, k, q * P:(q + 1) * P], x[:, j, k, :],
                                         start=(i == 0), stop=(i == 3 * KT - 1))
                        i += 1
                last.then_inc(hid_done, 1)

            def project(g, n, q, cw):
                u = n * GB + q
                if q == 0:
                    pe.wait_ge(y_kept, 2 * n + FREE)
                if q == 0 and g == 0:
                    for k in range(KT):
                        for i, w in enumerate((b2h, b2l)):
                            pe.matmul(ps[:, OUT + k, :], w[:, k * P:(k + 1) * P], cw, start=(i == 0), stop=False)
                pe.wait_ge(g_split, u + 1 + FREE)
                for k in range(KT):
                    for i, (w, x) in enumerate(((w2h, gh), (w2h, gl), (w2l, gh))):
                        last = pe.matmul(ps[:, OUT + k, :], w[:, q, k * P:(k + 1) * P], x[:, q % 2, :],
                                         start=(g > 0 and q == 0 and i == 0), stop=(q == GB - 1 and i == 2))
                        if q == GB - 2 and k == 0 and i == 0:
                            last.then_inc(x_free, 1)
                last.then_inc(out_done, 1)

            def turn_y(n):
                pe.wait_ge(y_kept, 2 * n + 2 + FREE)
                for b in range(2):
                    pe.wait_ge(y_added, 2 * n + b + 1)
                    for t in range(2):
                        for k in range(KT):
                            last = pe.transpose(ps[:, TURN + b, (t * KT + k) * P:(t * KT + k + 1) * P],
                                                stage[:, k, (2 * b + t) * P:(2 * b + t + 1) * P], ident[:, :])
                    last.then_inc(y_turned, 1)

            for g in range(GROUPS):
                pe.wait_ge(w_split, 2 * (g + 1))
                with pe.Fori(0, CHUNKS // 2) as cc:
                    for j in range(2):
                        n = g * CHUNKS + 2 * cc + j
                        cw = cwT[:, bass.ds((2 * cc + j) * CH, CH)]
                        for q in range(GB):
                            hidden(g, n, j, q, cw)
                            if j == 1 and q == 1:
                                turn_y(n - 1)
                            if q >= 2:
                                project(g, n, q - 2, cw)
                        project(g, n, GB - 2, cw)
                        project(g, n, GB - 1, cw)
                    turn_y(n)


C_HEADS, C_DH = 16, 16
C_HPH = C_HEADS // 2
C_TAIL = 32
C_DUP = P + C_TAIL - CTX
C_NEG = -1.0e30


def ctx_attention_stage(nc, xres, ident, A):
    with ExitStack() as ctx:
        def sb(name, shape, dt=F32):
            return ctx.enter_context(nc.sbuf_tensor("x1_" + name, shape, dt))

        def sem(name):
            return nc.alloc_semaphore("x1_" + name)

        names = ("L1_xattn_Wq", "L1_xattn_Wk", "L1_xattn_Wv", "L1_xattn_Wo")
        ROW = C_HPH * (P + C_TAIL)
        p = sb("p", [P, 4, ROW])
        wraw = p[:, 0:2, :].rearrange("p a j -> p (a j)")[:, 0:4 * 2 * DIM].rearrange("p (w o d) -> p w o d", w=4, o=2)
        ctxA = p[:, 2:4, :].rearrange("p a j -> p (a j)")[:, 0:4 * DIM].rearrange("p (b d) -> p b d", b=4)
        ctxB = p[:, 2:4, :].rearrange("p a j -> p (a j)")[0:CTX - P, 4 * DIM:8 * DIM].rearrange("p (b d) -> p b d", b=4)
        NBLK = C_HPH + 2
        pth, ptl = sb("pth", [P, 2, NBLK, 2 * P], F32R), sb("ptl", [P, 2, NBLK, 2 * P], F32R)

        def early(t, at, shape):
            flat = t[:, :, :, :].rearrange("p a n c -> p (a n c)")[:, at:at + int(np.prod(shape))]
            names = " ".join("abc"[:len(shape)])
            return flat.rearrange(f"p ({names}) -> p {names}", **dict(zip("abc", shape)))

        xTh, xTl = (early(t, 0, (KT, SEQ)) for t in (pth, ptl))
        cth, ctl = (early(t, KT * SEQ, (KT, BATCH, CTX)) for t in (pth, ptl))
        at = KT * SEQ + KT * BATCH * CTX
        wh = [sb("wqh", [P, KT, DIM], F32R), early(pth, at, (KT, DIM)), early(pth, at + KT * DIM, (KT, DIM)), sb("woh", [P, KT, DIM], F32R)]
        wl = [sb("wql", [P, KT, DIM], F32R), early(ptl, at, (KT, DIM)), early(ptl, at + KT * DIM, (KT, DIM)), sb("wol", [P, KT, DIM], F32R)]
        kTh, kTl = sb("kTh", [P, 2, BATCH, CTX], F32R), sb("kTl", [P, 2, BATCH, CTX], F32R)
        vAh, vAl = sb("vAh", [P, BATCH, DIM], F32R), sb("vAl", [P, BATCH, DIM], F32R)
        vBh, vBl = sb("vBh", [P, BATCH, DIM], F32R), sb("vBl", [P, BATCH, DIM], F32R)
        hmask_one = sb("one_row", [P, P])
        hmask = sb("hmask", [P, C_HPH])
        onesT = sb("onesT", [P, 4, P], F32R)
        tmask = sb("tmask", [P, 4, P])[:, :, :].rearrange("p (a b) (h d) -> p a b h d", a=2, d=C_DH)
        DIAG = P + C_DH
        onesA = sb("onesA", [P, C_HPH * DIAG], F32R)
        zero = sb("zero", [P, DIAG])
        scratch = sb("scratch", [P, 4 * CTX])
        cm = scratch[:, :].rearrange("p (t h j) -> p t h j", t=2, h=2)
        causal = sb("causal", [P, 2, 2, CTX], F32R)
        identr = sb("identr", [P, P], F32R)
        kbh, kbl = sb("kbh", [P, 2, C_HPH, CTX], F32R), sb("kbl", [P, 2, C_HPH, CTX], F32R)
        vah, val = sb("vah", [P, 2, C_HPH * DIAG], F32R), sb("val", [P, 2, C_HPH * DIAG], F32R)
        vbh, vbl = sb("vbh", [P, 4, P], F32R), sb("vbl", [P, 4, P], F32R)
        bor = sb("bor", [1, DIM])
        boh, bol, one1 = sb("boh", [1, DIM], F32R), sb("bol", [1, DIM], F32R), sb("one1", [1, P], F32R)
        tg = sb("tg", [P, 1])
        st, mv = sb("st", [P, TILES, 6]), sb("mv", [P, TILES, 2])
        var, root, rstd = sb("var", [P, TILES]), sb("root", [P, TILES]), sb("rstd", [P, TILES])
        start = p[:, :, :].rearrange("p a j -> p (a j)")[:, 0:TPB * DIM]
        y, qf = start.rearrange("p (t d) -> p t d", d=DIM), start.rearrange("p (h c) -> p h c", h=2)
        qh, ql = sb("qh", [P, 2, SEQ], F32R), sb("ql", [P, 2, SEQ], F32R)
        tails = [t[:, :, 0:CH].rearrange("p k (b r j) -> p k b r j", b=BATCH, j=C_TAIL) for t in (qh, ql)]
        mx = sb("mx", [P, C_HPH])
        rs, of = scratch[:, 0:2 * P], scratch[:, 2 * P:4 * P]
        oh, ol = sb("oh", [P, 2, 2 * P], F32R), sb("ol", [P, 2, 2 * P], F32R)
        ps = ctx.enter_context(nc.psum_tensor("x1_ps", [P, 8, CH], F32))
        TURN, PV, WO = 4, 6, 7
        scores = ps[:, 0:4, 0:2 * CTX].rearrange("p b (h j) -> p b h j", j=CTX)

        d_in, set_up, dve_own, pool_own = sem("d_in"), sem("set_up"), sem("dve_own"), sem("pool_own")
        pre_done, pre_hi, pre_lo = sem("pre_done"), sem("pre_hi"), sem("pre_lo")
        tanhed, stats, rooted, ready = sem("tanhed"), sem("stats"), sem("rooted"), sem("ready")
        y_ready, x_turned, x_hi, x_lo = sem("y_ready"), sem("x_turned"), sem("x_hi"), sem("x_lo")
        q_done, q_full, q_split, k_spread, v_spread = (sem(n) for n in ("q_done", "q_full", "q_split", "k_spread", "v_spread"))
        s_done, s_read, exp_done, turned, hi_done, lo_done = (
            sem(n) for n in ("s_done", "s_read", "exp_done", "turned", "hi_done", "lo_done"))
        pv_done, o_read, o_split, wo_done, x_added, batch_done = (
            sem(n) for n in ("pv_done", "o_read", "o_split", "wo_done", "x_added", "batch_done"))
        tails_set = sem("tails_set")
        block = ctx.enter_context(nc.Block())
        STEPS = 2 * TPB
        LAG = 2
        NJOB = 16
        GRP = ((0, 4), (4, 8), (8, 10))

        def job_out(n):
            if n < 4:
                return 2 * DIM, wh[n][:, :, :].rearrange("p k d -> p (k d)"), wl[n][:, :, :].rearrange("p k d -> p (k d)")
            if n < 12:
                h, l = (cth, ctl) if n < 8 else (kTh, kTl)
                k, b = (n % 4) // 2, n % 2
                return 2 * CTX, *(t[:, k, 2 * b:2 * b + 2, :].rearrange("p b j -> p (b j)") for t in (h, l))
            h, l = (vAh, vAl) if n < 14 else (vBh, vBl)
            return 2 * DIM, *(t[:, 2 * (n % 2):2 * (n % 2) + 2, :].rearrange("p b d -> p (b d)") for t in (h, l))

        @block.sync
        def _(sp):
            for i, n in enumerate(names):
                sp.dma_start(wraw[:, i, :, :], A[n].rearrange("(o p) d -> p o d", p=P)).then_inc(d_in, 16)
            sp.dma_start(ctxA, A["ctx_1024"][:, 0:P, :].rearrange("b j d -> j b d")).then_inc(d_in, 16)
            sp.dma_start(ctxB, A["ctx_1024"][:, P:CTX, :].rearrange("b j d -> j b d")).then_inc(d_in, 16)
            sp.dma_start(bor[:, :], A["L1_xattn_bo"].rearrange("(a d) -> a d", a=1)).then_inc(d_in, 16)
            with nc.allow_non_contiguous_dma(reason="one column"):
                sp.dma_start(tg[:, :], A["g_xattn"][1:2].partition_broadcast(P)).then_inc(d_in, 16)
        ND = 8

        @block.gpsimd
        def _(pool):
            own = Chain(pool, pool_own)
            own.step(pool.memset(hmask[:, :], 1.0))
            own.step(pool.memset(tmask, 1.0))
            own.step(pool.memset(cm, 0.0))
            own.step(pool.memset(zero[:, :], 0.0))
            own.wait()
            own.link(pool.affine_select(out=hmask[:, :], in_=hmask[:, :], compare_op=ALU.is_ge, fill=0.0, base=0,
                                        pattern=[[-C_DH, C_HPH]], channel_multiplier=1))
            own.link(pool.affine_select(out=hmask[:, :], in_=hmask[:, :], compare_op=ALU.is_ge, fill=0.0, base=C_DH - 1,
                                        pattern=[[C_DH, C_HPH]], channel_multiplier=-1))
            for h in range(2):
                m = tmask[:, h, :, :, :]
                own.link(pool.affine_select(out=m, in_=m, compare_op=ALU.is_ge, fill=0.0, base=-C_DUP,
                                            pattern=[[P, 2], [-C_TAIL, C_HPH], [0, C_DH]], channel_multiplier=1))
                own.link(pool.affine_select(out=m, in_=m, compare_op=ALU.is_ge, fill=0.0, base=C_TAIL - 1,
                                            pattern=[[-P, 2], [C_TAIL, C_HPH], [0, C_DH]], channel_multiplier=-1))
            own.link(pool.affine_select(out=cm, in_=cm, compare_op=ALU.is_ge, fill=C_NEG, base=0,
                                        pattern=[[P, 2], [0, 2], [-1, CTX]], channel_multiplier=1))
            own.step(pool.tensor_copy(causal[:, :, :, :], cm))
            own.step(pool.tensor_copy(identr[:, :], ident[:, :]))
            own.step(pool.tensor_copy(onesT[:, :, :], tmask.rearrange("p a b h d -> p (a b) (h d)")))
            for h in range(C_HPH):
                own.step(pool.tensor_copy(onesA[:, h * DIAG:(h + 1) * DIAG], zero[:, :]))
                for t in (vah, val):
                    for i in range(2):
                        own.step(pool.tensor_copy(t[:, i, h * DIAG:(h + 1) * DIAG], zero[:, :]))
            own.link(pool.memset(hmask_one[:, :], 1.0))
            own.step(pool.tensor_copy(onesA[:, :].rearrange("p (h c) -> p h c", c=DIAG)[:, :, 0:C_DH],
                                      hmask_one[:, :].rearrange("p (h c) -> p h c", c=C_DH)))
            pool.tensor_copy(one1[:, :], hmask_one[0:1, :]).then_inc(set_up, 1)
            own.wait()
            pool.wait_ge(set_up, 1)
            pool.wait_ge(pre_lo, 8)
            for t, c in zip(tails, (cth, ctl)):
                for k in range(KT):
                    src = c[:, k, :, CTX - C_TAIL:CTX].bitcast(F32).unsqueeze(2).broadcast_to([P, BATCH, P // C_TAIL, C_TAIL])
                    pool.tensor_copy(t[:, k, :, :, :], src).then_inc(tails_set, 1)
            pool.wait_ge(pre_lo, NJOB)
            with pool.Fori(0, BATCH) as b:
                pool.wait_ge(batch_done, b + 1)
                hm = hmask[:, :].unsqueeze(2).broadcast_to([P, C_HPH, CTX])
                for h in range(2):
                    src = kTl[:, h, bass.ds(b, 1), :].bitcast(F32).broadcast_to([P, C_HPH, CTX])
                    pool.tensor_tensor(kbl[:, h, :, :], src, hm, ALU.mult).then_inc(k_spread, 1)
                for s, d in ((vAh, vah), (vAl, val)):
                    for h in range(2):
                        pool.tensor_copy(d[:, h, :].rearrange("p (h c) -> p h c", c=DIAG)[:, :, 0:C_DH],
                                         s[:, bass.ds(b, 1), h * P:(h + 1) * P].bitcast(F32).rearrange("p a (h c) -> p (a h) c", c=C_DH)).then_inc(v_spread, 1)
                for s, d in ((vBh, vbh), (vBl, vbl)):
                    for g in range(4):
                        h = g // 2
                        pool.tensor_tensor(d[:, g, :], s[:, bass.ds(b, 1), h * P:(h + 1) * P].bitcast(F32).rearrange("p a c -> p (a c)"),
                                           tmask[:, h, g % 2, :, :].rearrange("p h d -> p (h d)"), ALU.mult).then_inc(v_spread, 1)

        @block.scalar
        def _(act):
            act.wait_ge(d_in, 16 * ND)
            act.activation(tg[:, :], tg[:, :], ACT.Tanh).then_inc(tanhed, 1)
            for n in range(NJOB):
                size, h, _ = job_out(n)
                act.wait_ge(pre_done, n + 1)
                act.activation(h, ps[:, n % 8, 0:size], ACT.Copy).then_inc(pre_hi, 1)
            act.wait_ge(stats, 1)
            act.activation(root[:, :], var[:, :], ACT.Sqrt).then_inc(rooted, 1)
            with act.Fori(0, BATCH) as b:
                for i in range(4):
                    act.wait_ge(x_turned, 4 * b + i + 1)
                    act.activation(xTh[:, i // 2, (i % 2) * CH:(i % 2 + 1) * CH], ps[:, i, :], ACT.Copy).then_inc(x_hi, 1)
                for i in range(4):
                    act.wait_ge(q_done, 4 * b + i + 1)
                    act.activation(qf[:, i // 2, (i % 2) * CH:(i % 2 + 1) * CH], ps[:, 4 + i, :], ACT.Copy,
                                   scale=float(C_DH) ** -0.5).then_inc(q_full, 1)
                for w in range(STEPS + LAG):
                    W = STEPS * b + w
                    if w >= LAG:
                        v = w - LAG
                        for g, (lo, hi) in enumerate(GRP):
                            G = 3 * (W - LAG) + g
                            act.wait_ge(turned, G + 1 + 6)
                            act.activation(pth[:, (v // 2) % 2, lo:hi, (v % 2) * P:(v % 2 + 1) * P],
                                           ps[:, TURN + (v + g) % 2, 0:(hi - lo) * P].rearrange("p (n t) -> p n t", t=P),
                                           ACT.Copy).then_inc(hi_done, 1)
                    if w < STEPS:
                        act.wait_ge(s_read, W + 1 + 1)
                        act.activation(p[:, w % 4, :], p[:, w % 4, :], ACT.Exp).then_inc(exp_done, 1)

        @block.vector
        def _(dve):
            own = Chain(dve, dve_own)
            dve.sem_inc(s_read, 1)
            dve.sem_inc(lo_done, 2)
            dve.sem_inc(o_read, 1)
            dve.sem_inc(x_added, 1)
            for t in range(TILES):
                own.step(dve.bn_stats(st[:, t, :], xres[:, t, :]))
            own.wait()
            for t in range(TILES):
                own.step(dve.bn_aggr(mv[:, t, :], st[:, t, :]))
            own.wait()
            dve.tensor_scalar(var[:, :], mv[:, :, 1], EPS, None, ALU.add).then_inc(stats, 1)
            dve.wait_ge(d_in, 16 * ND)
            own.link(dve.tensor_copy(boh[:, :], bor[:, :]))
            dve.tensor_tensor(bol[:, :], bor[:, :], boh[:, :].bitcast(F32), ALU.subtract).then_inc(ready, 1)
            for n in range(NJOB):
                size, h, l = job_out(n)
                dve.wait_ge(pre_hi, n + 1)
                dve.tensor_tensor(l, ps[:, n % 8, 0:size], h.bitcast(F32), ALU.subtract).then_inc(pre_lo, 1)
            dve.wait_ge(rooted, 1)
            newton_rsqrt(own, dve, var[:, :], root[:, :], rstd[:, :])
            dve.wait_ge(set_up, 1)
            dve.wait_ge(tanhed, 1)
            dve.wait_ge(pre_lo, NJOB)

            PER = 16 + 4 + 2 * TPB
            with dve.Fori(0, BATCH) as b:
                own.enter(b, PER)
                for t in range(TPB):
                    n = TPB * b + t
                    dve.tensor_scalar(y[:, t, :], xres[:, bass.ds(n, 1), :], mv[:, bass.ds(n, 1), 0],
                                      rstd[:, bass.ds(n, 1)], ALU.subtract, ALU.mult).then_inc(y_ready, 1)
                for i in range(4):
                    dve.wait_ge(x_hi, 4 * b + i + 1)
                    h = xTh[:, i // 2, (i % 2) * CH:(i % 2 + 1) * CH]
                    dve.tensor_tensor(xTl[:, i // 2, (i % 2) * CH:(i % 2 + 1) * CH], ps[:, i, :], h.bitcast(F32),
                                      ALU.subtract).then_inc(x_lo, 1)
                dve.wait_ge(batch_done, b + 1)
                for h in range(2):
                    dve.tensor_tensor(kbh[:, h, :, :], kTh[:, h, bass.ds(b, 1), :].bitcast(F32).broadcast_to([P, C_HPH, CTX]),
                                      hmask[:, :].unsqueeze(2).broadcast_to([P, C_HPH, CTX]), ALU.mult).then_inc(k_spread, 1)
                for i in range(4):
                    dve.wait_ge(q_full, 4 * b + i + 1)
                    f, h, l = (t[:, i // 2, (i % 2) * CH:(i % 2 + 1) * CH] for t in (qf, qh, ql))
                    own.link(dve.tensor_copy(h, f))
                    dve.tensor_tensor(l, f, h.bitcast(F32), ALU.subtract).then_inc(q_split, 1)

                def lows(w, gs):
                    v = w - LAG
                    for g in gs:
                        lo, hi = GRP[g]
                        dve.wait_ge(hi_done, 3 * (STEPS * b + v) + g + 1)
                        dst = (slice(None), (v // 2) % 2, slice(lo, hi), slice((v % 2) * P, (v % 2 + 1) * P))
                        dve.tensor_tensor(ptl[dst], ps[:, TURN + (v + g) % 2, 0:(hi - lo) * P].rearrange("p (n t) -> p n t", t=P),
                                          pth[dst].bitcast(F32), ALU.subtract).then_inc(lo_done, 1)

                def outs(u):
                    V = TPB * b + u
                    dve.wait_ge(pv_done, V + 1)
                    own.link(dve.reciprocal(rs[:, :], ps[:, PV, 2 * P:4 * P]))
                    dve.tensor_tensor(of[:, :], ps[:, PV, 0:2 * P], rs[:, :], ALU.mult).then_inc(o_read, 1)
                    dve.wait_ge(o_read, V + 1 + 1)
                    own.link(dve.tensor_copy(oh[:, u % 2, :], of[:, :]))
                    dve.tensor_tensor(ol[:, u % 2, :], of[:, :], oh[:, u % 2, :].bitcast(F32), ALU.subtract).then_inc(o_split, 1)

                def add_x(s):
                    dve.wait_ge(wo_done, TPB // 2 * b + s + 1)
                    part = xres[:, bass.ds(TPB * b + 2 * s, 2), :].rearrange("p t d -> p (t d)")
                    dve.scalar_tensor_tensor(part, ps[:, WO, :], tg[:, 0:1], part, ALU.mult, ALU.add).then_inc(x_added, 1)

                for w in range(STEPS + LAG + 4):
                    W = STEPS * b + w
                    if LAG <= w < STEPS + LAG:
                        lows(w, (0, 1))
                    if w < STEPS:
                        dve.wait_ge(s_done, W + 1)
                        own.link(dve.tensor_reduce(mx[:, :], scores, AX.X, ALU.max))
                        dve.wait_ge(turned, 3 * W - 3 + 6)
                        m = mx[:, :].rearrange("p (b h) -> p b h", h=2).unsqueeze(3)
                        dve.tensor_tensor(p[:, w % 4, 0:C_HPH * P].rearrange("p (b h j) -> p b h j", h=2, j=P), scores[:, :, :, 0:P],
                                          m.broadcast_to([P, 4, 2, P]), ALU.subtract)
                        dve.tensor_tensor(p[:, w % 4, C_HPH * P:ROW].rearrange("p (b h j) -> p b h j", h=2, j=C_TAIL),
                                          scores[:, :, :, CTX - C_TAIL:CTX], m.broadcast_to([P, 4, 2, C_TAIL]),
                                          ALU.subtract).then_inc(s_read, 1)
                    if LAG <= w < STEPS + LAG:
                        lows(w, (2,))
                    z = w - LAG - 3
                    if z >= 0 and z % 2 == 0 and z // 2 < TPB:
                        outs(z // 2)
                    z = w - LAG - 6
                    if z >= 0 and z % 4 == 0:
                        add_x(z // 4)
                own.leave(BATCH)

        @block.tensor
        def _(pe):
            pe.sem_inc(turned, 6)
            pe.sem_inc(batch_done, 1)
            pe.wait_ge(d_in, 16 * ND)
            for n in range(NJOB):
                if n >= 8:
                    pe.wait_ge(pre_lo, n - 7)
                bank = ps[:, n % 8, :]
                if n < 4:
                    for k in range(KT):
                        for o in range(2):
                            last = pe.transpose(bank[:, k * DIM + o * P:k * DIM + (o + 1) * P], wraw[:, n, o, k * P:(k + 1) * P], ident[:, :])
                elif n < 8:
                    k = (n % 4) // 2
                    for i in range(2):
                        b = 2 * (n % 2) + i
                        pe.transpose(bank[:, i * CTX:i * CTX + P], ctxA[:, b, k * P:(k + 1) * P], ident[:, :])
                        last = pe.transpose(bank[:, i * CTX + P:(i + 1) * CTX], ctxB[:, b, k * P:(k + 1) * P], ident[0:CTX - P, 0:CTX - P])
                elif n < 12:
                    if n == 8:
                        pe.wait_ge(pre_lo, 8)
                    h, b = (n % 4) // 2, 2 * (n % 2)
                    i = 0
                    for k in range(KT):
                        for w, x in ((wh, cth), (wh, ctl), (wl, cth)):
                            last = pe.matmul(bank[:, 0:2 * CTX], w[1][:, k, h * P:(h + 1) * P],
                                             x[:, k, b:b + 2, :].rearrange("p b j -> p (b j)"), start=(i == 0), stop=(i == 5))
                            i += 1
                else:
                    if n == 14:
                        pe.wait_ge(tails_set, 4)
                    for b2 in range(2):
                        b, i = 2 * (n % 2) + b2, 0
                        for k in range(KT):
                            for w, x in ((wh, cth), (wh, ctl), (wl, cth)):
                                if n < 14:
                                    lhs = x[:, k, b, 0:P]
                                else:
                                    lhs = tails[x is ctl][:, k, b, :, :].rearrange("p r j -> p (r j)")
                                last = pe.matmul(bank[:, b2 * DIM:(b2 + 1) * DIM], lhs, w[2][:, k, :], start=(i == 0), stop=(i == 5))
                                i += 1
                last.then_inc(pre_done, 1)
            pe.wait_ge(ready, 1)
            pe.wait_ge(pre_lo, NJOB)
            pe.wait_ge(set_up, 1)

            with pe.Fori(0, BATCH) as b:
                for i in range(4):
                    k, c = i // 2, i % 2
                    if k == 0:
                        pe.wait_ge(y_ready, TPB * b + 4 * (c + 1))
                    if i == 0:
                        pe.wait_ge(s_read, STEPS * b + 1)
                    for t in range(4):
                        last = pe.transpose(ps[:, i, t * P:(t + 1) * P], y[:, 4 * c + t, k * P:(k + 1) * P], ident[:, :])
                    last.then_inc(x_turned, 1)
                pe.wait_ge(x_lo, 4 * (b + 1))
                pe.wait_ge(lo_done, 3 * STEPS * b + 2)
                pe.wait_ge(o_read, TPB * b + 1)
                pe.wait_ge(x_added, TPB // 2 * b + 1)
                for j in range(4):
                    h, c, i = j // 2, j % 2, 0
                    for k in range(KT):
                        for w, x in ((wh, xTh), (wh, xTl), (wl, xTh)):
                            last = pe.matmul(ps[:, 4 + j, :], w[0][:, k, h * P:(h + 1) * P], x[:, k, c * CH:(c + 1) * CH],
                                             start=(i == 0), stop=(i == 5))
                            i += 1
                    last.then_inc(q_done, 1)
                pe.wait_ge(k_spread, 4 * (b + 1))
                pe.wait_ge(q_split, 4 * (b + 1))

                def turn(w, gs):
                    v = w - LAG
                    V = STEPS * b + v
                    for g in gs:
                        lo, hi = GRP[g]
                        if g == 0:
                            pe.wait_ge(exp_done, V + 1)
                        pe.wait_ge(lo_done, 3 * V + g + 1)
                        for n in range(lo, hi):
                            last = pe.transpose(ps[:, TURN + (v + g) % 2, (n - lo) * P:(n - lo + 1) * P],
                                                p[:, v % 4, n * P:(n + 1) * P], ident[:, :])
                        last.then_inc(turned, 1)

                def score(w):
                    W = STEPS * b + w
                    u, h = w // 2, (w // 2) % 2
                    t = 2 * (u // 2) + w % 2
                    pe.wait_ge(s_read, W + 1)
                    for n in range(4):
                        out = ps[:, n, 0:2 * CTX]
                        for i, (q, k) in enumerate(((qh, kbh), (qh, kbl), (ql, kbh))):
                            last = pe.matmul(out, q[:, h, t * P:(t + 1) * P], k[:, h, 2 * n:2 * n + 2, :].rearrange("p h j -> p (h j)"),
                                             start=(i == 0), stop=(i == 2 and t > 1))
                        if t < 2:
                            last = pe.matmul(out, identr[:, :], causal[:, t, :, :].rearrange("p h j -> p (h j)"), start=False, stop=True)
                    last.then_inc(s_done, 1)

                def stat(h, n, vals):
                    if n < C_HPH:
                        return vals[0][:, h, n * P:(n + 1) * P]
                    return vals[1][:, 2 * h + n - C_HPH, :]

                def values(u):
                    V, h = TPB * b + u, u % 2
                    if u == 0:
                        pe.wait_ge(v_spread, 12 * (b + 1))
                    pe.wait_ge(lo_done, 6 * (V + 1) + 2)
                    pe.wait_ge(o_read, V + 1)
                    for n in range(NBLK):
                        for i, (v, x) in enumerate((((vah, vbh), pth), ((vah, vbh), ptl), ((val, vbl), pth))):
                            pe.matmul(ps[:, PV, 0:2 * P], stat(h, n, v), x[:, u % 2, n, :], start=(n == 0 and i == 0), stop=(n == NBLK - 1 and i == 2))

                def sums(u):
                    for n in range(NBLK):
                        w = onesA[:, n * P:(n + 1) * P] if n < C_HPH else onesT[:, n - C_HPH, :]
                        for i, x in enumerate((pth, ptl)):
                            last = pe.matmul(ps[:, PV, 2 * P:4 * P], w, x[:, u % 2, n, :], start=(n == 0 and i == 0), stop=(n == NBLK - 1 and i == 1))
                    last.then_inc(pv_done, 1)

                def project(s):
                    pe.wait_ge(o_split, TPB * b + 2 * (s + 1))
                    pe.wait_ge(x_added, TPB // 2 * b + s + 1)
                    for t in range(2):
                        out = ps[:, WO, t * DIM:(t + 1) * DIM]
                        pe.matmul(out, one1[:, :], boh[:, :], start=True, stop=False)
                        pe.matmul(out, one1[:, :], bol[:, :], start=False, stop=False)
                        for k in range(KT):
                            for i, (o, w) in enumerate(((oh, wh), (oh, wl), (ol, wh))):
                                last = pe.matmul(out, o[:, k, t * P:(t + 1) * P], w[3][:, k, :], start=False, stop=(k == 1 and i == 2))
                    last.then_inc(wo_done, 1)

                for w in range(STEPS + LAG + 4):
                    if LAG <= w < STEPS + LAG:
                        turn(w, (0, 1))
                    if w < STEPS:
                        score(w)
                    if LAG <= w < STEPS + LAG:
                        turn(w, (2,))
                    z = w - LAG - 2
                    if z >= 0 and z % 2 == 0 and z // 2 < TPB:
                        values(z // 2)
                    z = w - LAG - 3
                    if z >= 0 and z % 2 == 0 and z // 2 < TPB:
                        sums(z // 2)
                    z = w - LAG - 6
                    if z >= 0 and z % 4 == 0:
                        project(z // 4)
                pe.drain().then_inc(batch_done, 1)


HID = 1024
HB = HID // P
MAGIC = 1.5 * 2.0 ** 23
QMAX, QMIN = 127.0, -128.0
TINY = 1e-5


def ffn_stage(nc, xres, ident, A):
    with ExitStack() as ctx:
        def sb(name, shape, dt=F32):
            return ctx.enter_context(nc.sbuf_tensor("ffn_" + name, shape, dt))

        def sem(name):
            return nc.alloc_semaphore("ffn_" + name)

        w1, w2 = sb("w1", [P, HB, DIM]), sb("w2", [P, KT, HID])
        w1q, w2q = sb("w1q", [P, HB, DIM], BF16), sb("w2q", [P, KT, HID], BF16)
        w1T, w2T = sb("w1T", [P, KT, HID], BF16), sb("w2T", [P, HB, DIM], BF16)
        conv_w, conv_b = sb("conv_w", [P, HB, 3]), sb("conv_b", [P, HB])
        tg = sb("tg", [P, 1])
        wsum, winv, wsc, fac = sb("wsum", [P, 2]), sb("winv", [P, 2]), sb("wsc", [P, 2]), sb("fac", [P, 1])
        ones, identb = sb("ones", [P, P]), sb("identb", [P, P], BF16)
        st, mv = sb("st", [P, TILES, 6]), sb("mv", [P, TILES, 2])
        var, root, rstd = sb("var", [P, TILES]), sb("root", [P, TILES]), sb("rstd", [P, TILES])
        y = sb("y", [P, TPB, DIM])
        yq = sb("yq", [P, TPB, DIM], BF16)
        am, sc, d1 = sb("am", [P, TPB]), sb("sc", [P, TPB]), sb("d1", [P, TPB])
        diag = sb("diag", [P, TPB, P])
        rsc = sb("rsc", [P, SEQ])
        yT = sb("yT", [P, KT, SEQ], BF16)
        hb = [sb(f"hb{i}", [P, SEQ + 2]) for i in range(2)]
        acc = sb("acc", [P, 2, SEQ])
        hs = sb("hs", [P, HB, SEQ])
        am2, sc2, d2 = sb("am2", [P, TPB]), sb("sc2", [P, TPB]), sb("d2", [P, TPB])
        u = sb("u", [P, 2, HID])
        r2 = sb("r2", [P, 2, HID], BF16)
        r2T = sb("r2T", [P, 2, HB, P], BF16)
        ps = ctx.enter_context(nc.psum_tensor("ffn_ps", [P, 8, CH], F32))
        wide = [ps[:, 0:2, :].rearrange("p b c -> p (b c)"), ps[:, 2:4, :].rearrange("p b c -> p (b c)")]
        half = [ps[:, 4, :].bitcast(BF16), ps[:, 5, :].bitcast(BF16)]
        outp = [ps[:, 6, 0:DIM], ps[:, 7, 0:DIM]]

        d_w, dve_own = sem("d_w"), sem("dve_own")
        set_up, summed, totalled, w_quant, w_turned, w_kept, tanhed = (
            sem(n) for n in ("set_up", "summed", "totalled", "w_quant", "w_turned", "w_kept", "tanhed"))
        stats, rooted = sem("stats"), sem("rooted")
        y_quant, diag_set, y_turned, y_kept, rsc_done, rsc_kept = (
            sem(n) for n in ("y_quant", "diag_set", "y_turned", "y_kept", "rsc_done", "rsc_kept"))
        hid_done, h_done, conv_mid, conv_done, hs_done = (
            sem(n) for n in ("hid_done", "h_done", "conv_mid", "conv_done", "hs_done"))
        t_done, t_read, b_done, r2_done, r2_turned, r2_kept, out_done, out_added = (
            sem(n) for n in ("t_done", "t_read", "b_done", "r2_done", "r2_turned", "r2_kept", "out_done", "out_added"))
        block = ctx.enter_context(nc.Block())

        @block.sync
        def _(sp):
            sp.dma_start(w1[:, :, :], A["L1_ffn_w1"].rearrange("(b p) d -> p b d", p=P)).then_inc(d_w, 16)
            sp.dma_start(w2[:, :, :], A["L1_ffn_w2"].rearrange("(k p) h -> p k h", p=P)).then_inc(d_w, 16)
            sp.dma_start(conv_w[:, :, :], A["L1_ffn_conv_w"].rearrange("(b p) o w -> p b (o w)", p=P)).then_inc(d_w, 16)
            with nc.allow_non_contiguous_dma(reason="small columns"):
                sp.dma_start(conv_b[:, :], A["L1_ffn_conv_b"].rearrange("(b p) -> p b", p=P)).then_inc(d_w, 16)
                sp.dma_start(tg[:, :], A["g_ffn"][1:2].partition_broadcast(P)).then_inc(d_w, 16)

        @block.gpsimd
        def _(pool):
            pool.memset(ones[:, :], 1.0).then_inc(set_up, 1)
            pool.tensor_copy(identb[:, :], ident[:, :]).then_inc(set_up, 1)
            for h in hb:
                pool.memset(h[:, 0:1], 0.0).then_inc(set_up, 1)
                pool.memset(h[:, SEQ + 1:SEQ + 2], 0.0).then_inc(set_up, 1)

        @block.scalar
        def _(act):
            act.wait_ge(d_w, 80)
            act.activation(tg[:, :], tg[:, :], ACT.Tanh).then_inc(tanhed, 1)
            act.wait_ge(stats, 1)
            act.activation(root[:, :], var[:, :], ACT.Sqrt).then_inc(rooted, 1)
            for i, dst in enumerate((w1T, w2T)):
                n = dst.shape[1] // 2 if i else 1
                for k in range(2):
                    act.wait_ge(w_turned, 2 * i + k + 1)
                    act.activation(dst[:, k * n:(k + 1) * n, :].rearrange("p k h -> p (k h)"), half[k], ACT.Copy).then_inc(w_kept, 1)
            with act.Fori(0, BATCH) as b:
                for k in range(KT):
                    act.wait_ge(y_turned, KT * b + k + 1)
                    act.activation(yT[:, k, :], half[k], ACT.Copy).then_inc(y_kept, 1)
                act.wait_ge(rsc_done, b + 1)
                act.activation(rsc[:, :], wide[0], ACT.Copy).then_inc(rsc_kept, 1)

                def middle(q):
                    act.wait_ge(h_done, HB * b + q + 1)
                    act.activation(acc[:, q % 2, :], hb[q % 2][:, 1:SEQ + 1], ACT.Identity, bias=conv_b[:, q:q + 1],
                                   scale=conv_w[:, q, 1:2]).then_inc(conv_mid, 1)

                middle(0)
                for q in range(HB):
                    if q + 1 < HB:
                        if q:
                            act.wait_ge(hs_done, HB * b + q)
                        middle(q + 1)
                    act.wait_ge(conv_done, HB * b + q + 1)
                    act.activation(hs[:, q, :], acc[:, q % 2, :], ACT.Silu).then_inc(hs_done, 1)
                for t in range(TPB):
                    n = TPB * b + t
                    act.wait_ge(b_done, n + 1)
                    act.activation(r2[:, t % 2, :], u[:, t % 2, :], ACT.Copy, bias=-MAGIC).then_inc(r2_done, 1)
                    act.wait_ge(r2_turned, n + 1)
                    act.activation(r2T[:, t % 2, :, :].rearrange("p b t -> p (b t)"), half[t % 2], ACT.Copy).then_inc(r2_kept, 1)

        @block.vector
        def _(dve):
            own = Chain(dve, dve_own)
            for t in range(TILES):
                own.step(dve.bn_stats(st[:, t, :], xres[:, t, :]))
            own.wait()
            for t in range(TILES):
                own.step(dve.bn_aggr(mv[:, t, :], st[:, t, :]))
            own.wait()
            dve.tensor_scalar(var[:, :], mv[:, :, 1], EPS, None, ALU.add).then_inc(stats, 1)
            dve.wait_ge(d_w, 80)
            own.step(dve.tensor_reduce(wsum[:, 0:1], w1[:, :, :], AX.XY, ALU.add, apply_absolute_value=True))
            dve.tensor_reduce(wsum[:, 1:2], w2[:, :, :], AX.XY, ALU.add, apply_absolute_value=True).then_inc(summed, 1)
            own.wait()
            dve.wait_ge(totalled, 1)
            own.link(dve.tensor_scalar(winv[:, :], outp[0][:, 0:2], 1.0 / (HID * DIM), TINY, ALU.mult, ALU.max))
            own.link(dve.reciprocal(wsc[:, :], winv[:, :]))
            for i, (w, wq) in enumerate(((w1, w1q), (w2, w2q))):
                own.link(dve.tensor_scalar(w[:, :, :], w[:, :, :], wsc[:, i:i + 1], 1.0, ALU.mult, ALU.min))
                own.link(dve.tensor_scalar(w[:, :, :], w[:, :, :], -1.0, MAGIC, ALU.max, ALU.add))
                dve.tensor_scalar(wq[:, :, :], w[:, :, :], MAGIC, None, ALU.subtract).then_inc(w_quant, 1)
            dve.wait_ge(tanhed, 1)
            own.link(dve.tensor_scalar(fac[:, :], winv[:, 1:2], tg[:, 0:1], 1.0 / QMAX, ALU.mult, ALU.mult))
            dve.wait_ge(rooted, 1)
            newton_rsqrt(own, dve, var[:, :], root[:, :], rstd[:, :])
            dve.wait_ge(set_up, 6)

            PER = 71
            with dve.Fori(0, BATCH) as b:
                own.enter(b, PER)
                for t in range(TPB):
                    n = TPB * b + t
                    own.step(dve.tensor_scalar(y[:, t, :], xres[:, bass.ds(n, 1), :], mv[:, bass.ds(n, 1), 0],
                                               rstd[:, bass.ds(n, 1)], ALU.subtract, ALU.mult))
                own.wait()
                own.link(dve.tensor_reduce(am[:, :], y[:, :, :], AX.X, ALU.max, apply_absolute_value=True))
                own.link(dve.tensor_scalar(am[:, :], am[:, :], TINY, None, ALU.max))
                own.link(dve.reciprocal(sc[:, :], am[:, :]))
                own.link(dve.tensor_scalar(sc[:, :], sc[:, :], QMAX, None, ALU.mult))
                own.link(dve.reciprocal(d1[:, :], sc[:, :]))
                own.link(dve.tensor_scalar(d1[:, :], d1[:, :], winv[:, 0:1], None, ALU.mult))
                for t in range(TPB):
                    own.step(dve.tensor_scalar(y[:, t, :], y[:, t, :], sc[:, t:t + 1], QMAX, ALU.mult, ALU.min))
                own.wait()
                own.link(dve.tensor_scalar(y[:, :, :], y[:, :, :], QMIN, MAGIC, ALU.max, ALU.add))
                dve.tensor_scalar(yq[:, :, :], y[:, :, :], MAGIC, None, ALU.subtract).then_inc(y_quant, 1)
                for t in range(TPB):
                    dve.tensor_scalar(diag[:, t, :], ident[:, :], d1[:, t:t + 1], None, ALU.mult).then_inc(diag_set, 1)

                def scale(q):
                    dve.wait_ge(hid_done, HB * b + q + 1)
                    dve.tensor_tensor(hb[q % 2][:, 1:SEQ + 1], wide[q % 2], rsc[:, :], ALU.mult).then_inc(h_done, 1)

                dve.wait_ge(rsc_kept, b + 1)
                scale(0)
                for q in range(HB):
                    if q + 1 < HB:
                        scale(q + 1)
                    a = acc[:, q % 2, :]
                    dve.wait_ge(conv_mid, HB * b + q + 1)
                    own.link(dve.scalar_tensor_tensor(a, hb[q % 2][:, 0:SEQ], conv_w[:, q, 0:1], a, ALU.mult, ALU.add))
                    dve.scalar_tensor_tensor(a, hb[q % 2][:, 2:SEQ + 2], conv_w[:, q, 2:3], a, ALU.mult, ALU.add).then_inc(conv_done, 1)
                    if q + 2 < HB:
                        dve.wait_ge(conv_done, HB * b + q + 1)

                def add_out(t):
                    n = TPB * b + t
                    dve.wait_ge(out_done, n + 1)
                    part = xres[:, bass.ds(n, 1), :].rearrange("p a d -> p (a d)")
                    dve.scalar_tensor_tensor(part, outp[t % 2], d2[:, t:t + 1], part, ALU.mult, ALU.add).then_inc(out_added, 1)

                for t in range(TPB):
                    n = TPB * b + t
                    c = slice(t, t + 1)
                    dve.wait_ge(t_done, n + 1)
                    own.link(dve.tensor_reduce(am2[:, c], wide[t % 2], AX.X, ALU.max, apply_absolute_value=True))
                    own.link(dve.tensor_scalar(am2[:, c], am2[:, c], TINY, None, ALU.max))
                    own.link(dve.reciprocal(sc2[:, c], am2[:, c]))
                    own.link(dve.tensor_scalar(sc2[:, c], sc2[:, c], QMAX, None, ALU.mult))
                    if t >= 2:
                        dve.wait_ge(r2_done, n - 1)
                    dve.tensor_scalar(u[:, t % 2, :], wide[t % 2], sc2[:, c], QMAX, ALU.mult, ALU.min).then_inc(t_read, 1)
                    dve.wait_ge(t_read, n + 1)
                    dve.tensor_scalar(u[:, t % 2, :], u[:, t % 2, :], QMIN, MAGIC, ALU.max, ALU.add).then_inc(b_done, 1)
                    own.step(dve.tensor_scalar(d2[:, c], am2[:, c], fac[:, 0:1], None, ALU.mult))
                    if t:
                        if t == 1:
                            own.wait()
                        add_out(t - 1)
                own.wait()
                add_out(TPB - 1)
                own.leave(BATCH)

        @block.tensor
        def _(pe):
            pe.wait_ge(set_up, 6)
            pe.wait_ge(summed, 1)
            pe.wait_ge(d_w, 80)
            pe.matmul(outp[0][:, 0:2], ones[:, :], wsum[:, :], start=True, stop=True).then_inc(totalled, 1)
            pe.wait_ge(w_quant, 1)
            for k in range(KT):
                for b in range(HB):
                    last = pe.transpose(half[k][:, b * P:(b + 1) * P], w1q[:, b, k * P:(k + 1) * P], identb[:, :])
                last.then_inc(w_turned, 1)
            pe.wait_ge(w_quant, 2)
            for i in range(2):
                pe.wait_ge(w_kept, i + 1)
                for b in range(HB // 2):
                    for k in range(KT):
                        q = i * (HB // 2) + b
                        last = pe.transpose(half[i][:, (b * KT + k) * P:(b * KT + k + 1) * P], w2q[:, k, q * P:(q + 1) * P], identb[:, :])
                last.then_inc(w_turned, 1)
            pe.wait_ge(w_kept, 4)
            with pe.Fori(0, BATCH) as b:
                pe.wait_ge(y_quant, b + 1)
                for k in range(KT):
                    for t in range(TPB):
                        last = pe.transpose(half[k][:, t * P:(t + 1) * P], yq[:, t, k * P:(k + 1) * P], identb[:, :])
                    last.then_inc(y_turned, 1)
                pe.wait_ge(diag_set, TPB * (b + 1))
                for t in range(TPB):
                    last = pe.matmul(wide[0][:, t * P:(t + 1) * P], ones[:, :], diag[:, t, :], start=True, stop=True)
                last.then_inc(rsc_done, 1)
                pe.wait_ge(y_kept, KT * (b + 1))
                for q in range(HB):
                    if q == 0:
                        pe.wait_ge(rsc_kept, b + 1)
                    if q >= 2:
                        pe.wait_ge(h_done, HB * b + q - 1)
                    for c in range(SEQ // CH):
                        for k in range(KT):
                            last = pe.matmul(wide[q % 2][:, c * CH:(c + 1) * CH], w1T[:, k, q * P:(q + 1) * P],
                                             yT[:, k, c * CH:(c + 1) * CH], start=(k == 0), stop=(k == KT - 1))
                    last.then_inc(hid_done, 1)

                def turn(t):
                    n = TPB * b + t
                    if t >= 2:
                        pe.wait_ge(t_read, n - 1)
                    for q in range(HB):
                        last = pe.transpose(wide[t % 2][:, q * P:(q + 1) * P], hs[:, q, t * P:(t + 1) * P], ident[:, :])
                    last.then_inc(t_done, 1)

                pe.wait_ge(h_done, HB * (b + 1))
                pe.wait_ge(hs_done, HB * (b + 1))
                turn(0)
                for t in range(TPB):
                    n = TPB * b + t
                    if t + 1 < TPB:
                        turn(t + 1)
                    pe.wait_ge(r2_done, n + 1)
                    if t >= 2:
                        pe.wait_ge(r2_kept, n - 1)
                    for q in range(HB):
                        last = pe.transpose(half[t % 2][:, q * P:(q + 1) * P], r2[:, t % 2, q * P:(q + 1) * P], identb[:, :])
                    last.then_inc(r2_turned, 1)
                    pe.wait_ge(r2_kept, n + 1)
                    if t >= 2:
                        pe.wait_ge(out_added, n - 1)
                    for q in range(HB):
                        last = pe.matmul(outp[t % 2], r2T[:, t % 2, q, :], w2T[:, q, :], start=(q == 0), stop=(q == HB - 1))
                    last.then_inc(out_done, 1)
                pe.wait_ge(out_added, TPB * (b + 1))


def flamingo_program(nc, A, out):
    with ExitStack() as ctx:
        xres = ctx.enter_context(nc.sbuf_tensor("xres", [P, TILES, DIM], F32))
        ident = ctx.enter_context(nc.sbuf_tensor("ident", [P, P], F32))
        ident_set, stored = nc.alloc_semaphore("ident_set"), nc.alloc_semaphore("stored")
        with nc.Block() as block:
            @block.gpsimd
            def _(pool):
                pool.memset(ident[:, :], 0.0).then_inc(ident_set, 1)
                pool.wait_ge(ident_set, 1)
                pool.affine_select(out=ident[:, :], in_=ident[:, :], compare_op=ALU.not_equal, fill=1.0, base=0,
                                   pattern=[[-1, P]], channel_multiplier=1).then_inc(ident_set, 1)
                pool.wait_ge(ident_set, 2)
        resample_stage(nc, xres, ident, A)
        moe_stage(nc, xres, ident, A)
        ctx_attention_stage(nc, xres, ident, A)
        ffn_stage(nc, xres, ident, A)
        with nc.Block() as block:
            @block.sync
            def _(sp):
                sp.dma_start(out.rearrange("b (t p) d -> p (b t) d", p=P), xres[:, :, :]).then_inc(stored, 16)
                sp.wait_ge(stored, 16)


def kernel(**inputs):
    import concourse.bacc as bacc
    from concourse.bass_utils import run_bass_kernel_spmd

    nc = bacc.Bacc("TRN2", target_bir_lowering=False, num_devices=1)
    arrays, A = {}, {}
    for name, value in inputs.items():
        a = np.ascontiguousarray(value)
        arrays[f"in_{name}_dram"] = a
        A[name] = nc.dram_tensor(f"in_{name}_dram", a.shape, mybir.dt.from_np(a.dtype), kind="ExternalInput").ap()
    out = nc.dram_tensor("out_dram", (BATCH, SEQ, DIM), F32, kind="ExternalOutput").ap()
    flamingo_program(nc, A, out)
    r = run_bass_kernel_spmd(nc, [arrays], core_ids=[0])
    return r.results[0]["out_dram"]
```

```python
from contextlib import ExitStack
import numpy as np
import concourse.bass as bass
from concourse import mybir

F32 = mybir.dt.float32
F32R = mybir.dt.float32r
BF16 = mybir.dt.bfloat16
ACT = mybir.ActivationFunctionType
ALU = mybir.AluOpType
AX = mybir.AxisListType

P = 128
BATCH, SEQ, DIM = 4, 1024, 256
CTX = 154
TOKENS = BATCH * SEQ
TILES = TOKENS // P
KT = DIM // P
CH = 512
CHUNKS = TOKENS // CH
TPC = CH // P
TPB = SEQ // P
EPS = 1e-5


class Chain:

    def __init__(self, eng, sem):
        self.eng, self.sem, self.base, self.k, self.start, self.per = eng, sem, 0, 0, 0, 0

    def step(self, ins):
        ins.then_inc(self.sem, 1)
        self.k += 1
        return self.k

    def wait(self, k=None):
        self.eng.wait_ge(self.sem, self.base + (self.k if k is None else k))

    def link(self, ins):
        self.step(ins)
        self.wait()

    def enter(self, it, per):
        self.start, self.per, self.base, self.k = self.base + self.k, per, it * per + (self.base + self.k), 0

    def leave(self, rounds):
        assert self.k == self.per, (self.k, self.per)
        self.base, self.k = self.start + rounds * self.per, 0


def newton_rsqrt(own, dve, var, root, r):
    own.link(dve.reciprocal(r, root))
    own.link(dve.tensor_tensor(root, r, r, ALU.mult))
    own.link(dve.tensor_tensor(root, root, var, ALU.mult))
    own.link(dve.tensor_scalar(root, root, -0.5, 1.5, ALU.mult, ALU.add))
    own.link(dve.tensor_tensor(r, r, root, ALU.mult))


R_HEADS, R_DH = 8, 128
R_INNER = R_HEADS * R_DH
R_KV = SEQ + CTX
R_BLK = -(-R_KV // P)
R_ROW = R_BLK * P
SN = 2 * -(-R_KV // 6)
DUP = 3 * SN - R_KV
R_SCALE = float(R_DH) ** -0.5
R_BIG = 3.0e38


def resample_stage(nc, xres, ident, A):
    with ExitStack() as ctx:
        def sb(name, shape, dt=F32):
            return ctx.enter_context(nc.sbuf_tensor("x0_" + name, shape, dt))

        def sem(name):
            return nc.alloc_semaphore("x0_" + name)

        p = sb("p", [P, 4, DUP + R_ROW])
        z = sb("z", [P, TPB // 2, DIM])
        mA, mB = sb("mA", [P, DIM]), sb("mB", [CTX - P, DIM])
        kvh, kvl = sb("kvh", [P, KT, R_KV], F32R), sb("kvl", [P, KT, R_KV], F32R)
        wraw, wh, wl = sb("wraw", [P, 2, 4, DIM]), sb("wh", [P, 2, 4, DIM], F32R), sb("wl", [P, 2, 4, DIM], F32R)
        full = sb("full", [P, 2, CH])
        vf = sb("vf", [P, R_ROW])
        kh, kl = sb("kh", [P, 2, R_KV], F32R), sb("kl", [P, 2, R_KV], F32R)
        qh, ql = sb("qh", [P, 2, SEQ], F32R), sb("ql", [P, 2, SEQ], F32R)
        vh, vl = sb("vh", [P, 2, R_ROW], F32R), sb("vl", [P, 2, R_ROW], F32R)
        pth, ptl = sb("pth", [P, 2, R_BLK, 2 * P], F32R), sb("ptl", [P, 2, R_BLK, 2 * P], F32R)
        oh, ol = sb("oh", [P, 2 * P], F32R), sb("ol", [P, 2 * P], F32R)
        cA, cB = p[:, :, 0:DIM], p[0:CTX - P, :, DIM:2 * DIM]
        cols = sb("cols", [P, 4, KT])
        bias = sb("bias", [P, 3, R_HEADS])
        tbo = sb("tbo", [P, DIM])
        tg = sb("tg", [P, 1])
        NST = TILES + 2 * BATCH
        mv = p[:, 0, DUP + R_KV:DUP + R_KV + 2 * NST].rearrange("p (n s) -> p n s", s=2)
        r1 = p[:, 1, DUP + R_KV:DUP + R_KV + NST]
        st = vf[:, 0:6 * NST].rearrange("p (n s) -> p n s", s=6)
        var, root, r2 = vf[:, 6 * NST:7 * NST], vf[:, 7 * NST:8 * NST], vf[:, 8 * NST:8 * NST + TILES]
        nmx, sums, rt = sb("nmx", [P, 2]), sb("sums", [P, 2 * TPB]), sb("rt", [P, 2])
        ps = ctx.enter_context(nc.psum_tensor("x0_ps", [P, 8, CH], F32))
        scores = ps[:, 0:3, 0:SN]
        SFROM = (R_KV - SN, 0, SN)
        PORDER = ((2 * SN, R_KV, 0), (0, SN, SN - DUP), (SN, 2 * SN, 2 * SN - DUP))
        TURN, PV, JOB = 3, 5, 6

        d_m, d_x, d_in = sem("d_m"), [sem(f"d_x{i}") for i in range(BATCH)], sem("d_in")
        d_wq, d_wo = [sem("d_wq0"), sem("d_wq1")], [sem("d_wo0"), sem("d_wo1")]
        alone = sem("alone")
        dve_own, set_up, tanhed, stats, rooted = sem("dve_own"), sem("set_up"), sem("tanhed"), sem("stats"), sem("rooted")
        z_ready, rt_made = sem("z_ready"), sem("rt_made")
        wq_high, wq_split, wo_high, wo_split = (sem(n) for n in ("wq_high", "wq_split", "wo_high", "wo_split"))
        job_done, job_full, job_high, job_low, vt_high, vt_low = (
            sem(n) for n in ("job_done", "job_full", "job_high", "job_low", "vt_high", "vt_low"))
        s_done, s_read, exp_done, turned, hi_done, lo_done = (
            sem(n) for n in ("s_done", "s_read", "exp_done", "turned", "hi_done", "lo_done"))
        pv_done, o_high, o_split, y_done, y_added = (sem(n) for n in ("pv_done", "o_high", "o_split", "y_done", "y_added"))
        block = ctx.enter_context(nc.Block())

        STEPS = 2 * TPB
        UNITS = STEPS // 2
        LAG = 2
        SPILL = LAG + 2
        PAIRS_H = R_HEADS // 2
        GRP = ((0, 4), (4, 8), (8, R_BLK))
        CUT = ((0, CH), (CH, 2 * CH), (2 * CH, R_KV))
        KCUT = [(n * SN, min(R_KV, (n + 1) * SN)) for n in range(3)]
        JOBS = [("k", *KCUT[0]), ("k", *KCUT[1]), ("k", *KCUT[2]), ("q", *CUT[0]), ("q", *CUT[1]),
                ("v", *PORDER[0][:2]), ("v", *PORDER[1][:2]), ("v", *PORDER[2][:2])] + [("t", lo * P, hi * P) for lo, hi in GRP]
        XJOBS = [(k, lo, hi) for lo, hi in CUT for k in range(KT)]
        NX, NF, NS, NV, NJ = len(XJOBS), 8, 5, 3, len(JOBS)
        PLAN = [[0], [1], [2, 3], [4], [5], [6], [7, 8], [9, 10]]
        XPLAN = [[0, 1], [2, 3], [4, 5]]
        PLAN_AFTER_X = [[], [], [], [0, 1], [2, 3, 4], [5, 6], [7, 8], [9, 10]]

        class Head:

            def __init__(self, b, hp, j):
                self.j, self.hp, self.h, self.it = j, hp, hp * 2 + j, b * PAIRS_H + hp
                self.first = isinstance(hp, int) and hp == 0 and j == 0
                self.job, self.full, self.split = (2 * n * self.it + NX * (b + 1) + n * j for n in (NJ, NF, NS))
                self.vt = 2 * NV * self.it + NV * j
                self.xfull = 2 * NF * self.it + NX * b

        class Inputs:

            def __init__(self, b):
                self.b = b
                self.job, self.full, self.split = (2 * n * PAIRS_H * b + NX * b for n in (NJ, NF, NS))
                self.vt = 2 * NV * PAIRS_H * b

        def walk(part, b, hp):
            if part != "start":
                for w in range(SPILL, STEPS):
                    s, jobs, norm = w % TPB, [], []
                    if w < TPB:
                        jobs = [(Head(b, hp, 1), m) for m in PLAN[s]]
                        norm = [(b + 1, s - SPILL)] if part == "cross" and s < SPILL + 2 else []
                    elif part == "body":
                        jobs = [(Head(b, hp + 1, 0), m) for m in PLAN[s]]
                    elif part == "cross":
                        jobs = [(Inputs(b + 1), m) for m in (XPLAN[s] if s < len(XPLAN) else ())]
                        jobs += [(Head(b + 1, 0, 0), m) for m in PLAN_AFTER_X[s]]
                        norm = [(b + 1, 2), (b + 1, 3)] if s == 0 else []
                    yield w, b, b * PAIRS_H + hp, b, jobs, norm
            if part == "end":
                for w in range(STEPS, STEPS + SPILL):
                    yield w, b, b * PAIRS_H + hp, b, [], []
            else:
                nb, nhp = {"start": (b, hp), "body": (b, hp + 1), "cross": (b + 1, 0)}[part]
                for w in range(SPILL):
                    yield w, nb, nb * PAIRS_H + nhp, None if part == "start" else b, [(Head(nb, nhp, 1), m) for m in PLAN[w]], []

        def run(eng, first, step):
            x0, h0 = Inputs(0), Head(0, 0, 0)
            first([(x0, m) for m in range(NX)] + [(h0, m) for m in range(NJ)])
            for s in walk("start", 0, 0):
                step(*s)
            with eng.Fori(0, BATCH - 1) as b:
                with eng.Fori(0, PAIRS_H - 1) as hp:
                    for s in walk("body", b, hp):
                        step(*s)
                for s in walk("cross", b, PAIRS_H - 1):
                    step(*s)
            with eng.Fori(0, PAIRS_H - 1) as hp:
                for s in walk("body", BATCH - 1, hp):
                    step(*s)
            for s in walk("end", BATCH - 1, PAIRS_H - 1):
                step(*s)

        @block.sync
        def _(sp):
            xt = A["x"].rearrange("b (t p) d -> p (b t) d", p=P)
            sp.dma_start(xres[:, 0:TPB, :], xt[:, 0:TPB, :]).then_inc(d_x[0], 16)
            sp.dma_start(cA, A["ctx_1024"][:, 0:P, :].rearrange("b j d -> j b d")).then_inc(d_in, 16)
            sp.dma_start(cB, A["ctx_1024"][:, P:CTX, :].rearrange("b j d -> j b d")).then_inc(d_in, 16)
            sp.dma_start(tbo[:, :], A["L0_xattn_bo"].partition_broadcast(P)).then_inc(d_in, 16)
            with nc.allow_non_contiguous_dma(reason="small columns"):
                sp.dma_start(tg[:, :], A["g_xattn"][0:1].partition_broadcast(P)).then_inc(d_in, 16)
                for i, n in enumerate(("gamma_lat", "beta_lat", "gamma_media", "beta_media")):
                    sp.dma_start(cols[:, i, :], A["L0_xattn_" + n].rearrange("(k p) -> p k", p=P)).then_inc(d_in, 16)
                sp.dma_start(bias[:, 0, :], A["L0_xattn_bq"].rearrange("(h p) -> p h", p=P)).then_inc(d_in, 16)
                sp.dma_start(bias[:, 1:3, :], A["L0_xattn_bkv"].rearrange("(i h p) -> p i h", p=P, i=2)).then_inc(d_in, 16)
            for i in range(1, BATCH):
                sp.dma_start(xres[:, TPB * i:TPB * (i + 1), :], xt[:, TPB * i:TPB * (i + 1), :]).then_inc(d_x[i], 16)
            wq = A["L0_xattn_Wq"].rearrange("(k p) n -> p k n", p=P)
            wkv = A["L0_xattn_Wkv"].rearrange("(k p) n -> p k n", p=P)
            wo = A["L0_xattn_Wo"].rearrange("(h p) n -> p h n", p=P)
            with sp.Fori(0, BATCH) as b:
                sp.dma_start(mA[:, :], A["ctx_1024"][bass.ds(b, 1), 0:P, :].rearrange("b j d -> (b j) d")).then_inc(d_m, 16)
                sp.dma_start(mB[:, :], A["ctx_1024"][bass.ds(b, 1), P:CTX, :].rearrange("b j d -> (b j) d")).then_inc(d_m, 16)
                with sp.Fori(0, PAIRS_H) as hp:
                    for j in range(2):
                        n = Head(b, hp, j)
                        raw = wraw[:, j, :, :].rearrange("p w (k n) -> p w k n", k=KT)
                        sp.wait_ge(wq_split, 2 * n.it + j + 1)
                        sp.dma_start(raw[:, 0, :, :], wq[:, :, bass.ds(n.h * P, P)]).then_inc(d_wq[j], 16)
                        sp.dma_start(raw[:, 1, :, :], wkv[:, :, bass.ds(n.h * P, P)]).then_inc(d_wq[j], 16)
                        sp.dma_start(raw[:, 2, :, :], wkv[:, :, bass.ds(n.h * P + R_INNER, P)]).then_inc(d_wq[j], 16)
                        sp.wait_ge(wo_split, 2 * n.it + j + 1)
                        sp.dma_start(wraw[:, j, 3, :], wo[:, bass.ds(n.h, 1), :]).then_inc(d_wo[j], 16)
                sp.wait_ge(job_done, Inputs(b).job + NX)
                sp.sem_inc(alone, 1)
        ND = 10

        def split_parts(n, m):
            if isinstance(n, Inputs):
                k, lo, hi = XJOBS[m]
                return full[:, m % 2, 0:hi - lo], kvh[:, k, lo:hi], kvl[:, k, lo:hi]
            kind, lo, hi = JOBS[m]
            h, l = {"k": (kh, kl), "q": (qh, ql)}[kind]
            return full[:, (NS * n.j + m) % 2, 0:hi - lo], h[:, n.j, lo:hi], l[:, n.j, lo:hi]

        def bank(n, m):
            if isinstance(n, Inputs):
                return ps[:, JOB + m % 2, :]
            return ps[:, JOB + (NX + NJ * n.j + m) % 2, :]

        @block.gpsimd
        def _(pool):
            pool.sem_inc(wq_split, 2)
            pool.sem_inc(wo_split, 2)
            pool.sem_inc(job_low, 2)
            for i in range(4):
                pool.memset(p[:, i, DUP + R_KV + (2 * NST, NST, 0, 0)[i]:], 0.0).then_inc(set_up, 1)
            pool.memset(vf[:, R_KV:R_ROW], 0.0).then_inc(set_up, 1)

            def stand_alone():
                pool.sem_inc(alone, 1)

            def split_q(it, j):
                pool.wait_ge(d_wq[j], 48 * (it + 1))
                stand_alone()
                pool.tensor_copy(wh[:, j, 0:3, :], wraw[:, j, 0:3, :]).then_inc(wq_high, 1)
                pool.wait_ge(wq_high, 2 * it + j + 1)
                pool.tensor_tensor(wl[:, j, 0:3, :], wraw[:, j, 0:3, :], wh[:, j, 0:3, :].bitcast(F32), ALU.subtract).then_inc(wq_split, 1)

            def low(n, m):
                f, h, l = split_parts(n, m)
                pool.wait_ge(job_high, n.split + m + 1)
                pool.tensor_tensor(l, f, h.bitcast(F32), ALU.subtract).then_inc(job_low, 1)

            def head(n, more):
                for m in range(NS):
                    low(n, m)
                pool.wait_ge(y_done, UNITS * n.it + UNITS // 2 * (n.j + 1))
                pool.wait_ge(d_wo[n.j], 16 * (n.it + 1))
                stand_alone()
                pool.tensor_copy(wh[:, n.j, 3, :], wraw[:, n.j, 3, :]).then_inc(wo_high, 1)
                pool.wait_ge(wo_high, 2 * n.it + n.j + 1)
                pool.tensor_tensor(wl[:, n.j, 3, :], wraw[:, n.j, 3, :], wh[:, n.j, 3, :].bitcast(F32), ALU.subtract).then_inc(wo_split, 1)
                if more:
                    pool.wait_ge(job_done, n.job + NF)
                    split_q(n.it + 1, n.j)

            def inputs(b):
                for m in range(NX):
                    low(Inputs(b), m)

            split_q(0, 0)
            split_q(0, 1)
            with pool.Fori(0, BATCH - 1) as b:
                inputs(b)
                with pool.Fori(0, PAIRS_H) as hp:
                    for j in range(2):
                        head(Head(b, hp, j), True)
            inputs(BATCH - 1)
            with pool.Fori(0, PAIRS_H - 1) as hp:
                for j in range(2):
                    head(Head(BATCH - 1, hp, j), True)
            for j in range(2):
                head(Head(BATCH - 1, PAIRS_H - 1, j), False)

        @block.scalar
        def _(act):
            act.wait_ge(d_in, 16 * ND)
            act.activation(tg[:, :], tg[:, :], ACT.Tanh).then_inc(tanhed, 1)
            act.wait_ge(stats, 1)
            act.activation(root[:, :], var[:, :], ACT.Sqrt).then_inc(rooted, 1)
            act.wait_ge(stats, 2)
            act.activation(root[:, 0:TILES], var[:, 0:TILES], ACT.Sqrt).then_inc(rooted, 1)
            act.wait_ge(tanhed, 2)

            def job(n, m):
                act.wait_ge(job_done, n.job + m + 1)
                if isinstance(n, Inputs):
                    k, lo, hi = XJOBS[m]
                    g = 0 if hi <= SEQ else 2
                    act.wait_ge(job_low, n.split + m + 1)
                    act.activation(full[:, m % 2, 0:hi - lo], bank(n, m)[:, 0:hi - lo], ACT.Identity,
                                   bias=cols[:, g + 1, k:k + 1], scale=cols[:, g, k:k + 1]).then_inc(job_full, 1)
                    return
                kind, lo, hi = JOBS[m]
                if kind == "t":
                    act.activation(vh[:, n.j, lo:hi], bank(n, m)[:, 0:hi - lo], ACT.Copy).then_inc(vt_high, 1)
                    return
                if kind == "v":
                    at = PORDER[m - NS][2]
                    dst = vf[:, at:at + hi - lo]
                else:
                    act.wait_ge(job_low, n.split + m + 1)
                    dst = split_parts(n, m)[0]
                i = "qkv".index(kind)
                act.sem_inc(alone, 1)
                act.activation(dst, bank(n, m)[:, 0:hi - lo], ACT.Identity, bias=bias[:, i, bass.ds(n.h, 1)],
                               scale=R_SCALE if kind == "q" else 1.0).then_inc(job_full, 1)

            def step(w, b, it, blag, jobs, norm):
                for n, m in jobs:
                    job(n, m)
                v = w - LAG
                if (blag is not None or v >= 0) and v < STEPS:
                    for g, (lo, hi) in enumerate(GRP):
                        act.wait_ge(turned, 3 * (STEPS * it + v) + g + 1 + 12)
                        act.activation(pth[:, (v // 2) % 2, lo:hi, (v % 2) * P:(v % 2 + 1) * P],
                                       ps[:, TURN + (v + g) % 2, 0:(hi - lo) * P].rearrange("p (n t) -> p n t", t=P),
                                       ACT.Copy).then_inc(hi_done, 1)
                if w < STEPS:
                    act.wait_ge(s_read, STEPS * it + w + 1 + 1)
                    act.activation(p[:, w % 4, DUP:DUP + R_KV], p[:, w % 4, DUP:DUP + R_KV], ACT.Exp, bias=nmx[:, w % 2:w % 2 + 1], scale=-1.0,
                                   accum_out=sums[:, w:w + 1]).then_inc(exp_done, 1)
                u = (w - LAG - 2) // 2
                if w % 2 == 0 and (blag is not None or u >= 0):
                    act.wait_ge(pv_done, UNITS * it + u + 1)
                    act.activation(oh[:, :], ps[:, PV, 0:2 * P], ACT.Copy).then_inc(o_high, 1)

            def first(jobs):
                for n, m in jobs:
                    job(n, m)

            run(act, first, step)

        @block.vector
        def _(dve):
            own = Chain(dve, dve_own)
            dve.sem_inc(s_read, 1)
            dve.sem_inc(lo_done, 2)
            dve.sem_inc(y_added, 1)
            own.link(dve.memset(mv[:, :, :], 1.0))
            for t in range(TPB):
                if t == 0:
                    dve.wait_ge(d_x[0], 16)
                own.step(dve.bn_stats(st[:, t, :], xres[:, t, :]))
            dve.wait_ge(d_in, 16 * ND)
            for b in range(BATCH):
                own.step(dve.bn_stats(st[:, TILES + b, :], cA[:, b, :]))
                own.step(dve.bn_stats(st[0:CTX - P, TILES + BATCH + b, :], cB[:, b, :]))
            for t in range(TPB, TILES):
                if t % TPB == 0:
                    dve.wait_ge(d_x[t // TPB], 16)
                own.step(dve.bn_stats(st[:, t, :], xres[:, t, :]))
            own.wait()
            for n in range(NST):
                rows = slice(0, P) if n < TILES + BATCH else slice(0, CTX - P)
                own.step(dve.bn_aggr(mv[rows, n, :], st[rows, n, :]))
            own.wait()
            dve.tensor_scalar(var[:, :], mv[:, :, 1], EPS, None, ALU.add).then_inc(stats, 1)
            dve.wait_ge(rooted, 1)
            newton_rsqrt(own, dve, var[:, :], root[:, :], r1[:, :])
            x1, once = mv[:, 0:TILES, 1], r1[:, 0:TILES]
            own.link(dve.tensor_tensor(r2[:, :], x1, once, ALU.mult))
            own.link(dve.tensor_tensor(r2[:, :], r2[:, :], once, ALU.mult))
            own.link(dve.tensor_scalar(var[:, 0:TILES], r2[:, :], EPS, None, ALU.add))
            dve.sem_inc(stats, 1)
            dve.wait_ge(rooted, 2)
            newton_rsqrt(own, dve, var[:, 0:TILES], root[:, 0:TILES], r2[:, :])
            own.link(dve.tensor_tensor(once, once, r2[:, :], ALU.mult))
            dve.wait_ge(tanhed, 1)
            own.link(dve.tensor_scalar(tbo[:, :], tbo[:, :], tg[:, 0:1], None, ALU.mult))
            dve.tensor_scalar(bias[:, 0, :], bias[:, 0, :], R_SCALE, None, ALU.mult).then_inc(tanhed, 1)
            dve.wait_ge(set_up, 5)

            def normalise(b, i):
                for t in (2 * i, 2 * i + 1):
                    n = TPB * b + t
                    last = dve.tensor_scalar(z[:, t % (TPB // 2), :], xres[:, bass.ds(n, 1), :], mv[:, bass.ds(n, 1), 0], r1[:, bass.ds(n, 1)],
                                             ALU.subtract, ALU.mult)
                last.then_inc(z_ready, 1)
                dve.wait_ge(z_ready, (TPB // 2 + 1) * b + i + 1)
                part = xres[:, bass.ds(TPB * b + 2 * i, 2), :]
                dve.tensor_tensor(part, part, tbo[:, :].unsqueeze(1).broadcast_to([P, 2, DIM]), ALU.add)
                if i == TPB // 2 - 1:
                    dve.wait_ge(d_m, 32 * (b + 1))
                    for m, rows, at in ((mA, slice(0, P), TILES), (mB, slice(0, CTX - P), TILES + BATCH)):
                        last = dve.tensor_scalar(m[:, :], m[:, :], mv[rows, bass.ds(b + at, 1), 0], r1[rows, bass.ds(b + at, 1)],
                                                 ALU.subtract, ALU.mult)
                    last.then_inc(z_ready, 1)

            def job(n, m):
                if not isinstance(n, Inputs) and JOBS[m][0] == "t":
                    kind, lo, hi = JOBS[m]
                    dve.wait_ge(vt_high, n.vt + m - NF + 1)
                    dve.tensor_tensor(vl[:, n.j, lo:hi], bank(n, m)[:, 0:hi - lo], vh[:, n.j, lo:hi].bitcast(F32),
                                      ALU.subtract).then_inc(vt_low, 1)
                elif isinstance(n, Inputs) or JOBS[m][0] != "v":
                    f, h, l = split_parts(n, m)
                    dve.wait_ge(job_full, n.full + m + 1)
                    dve.tensor_copy(h, f).then_inc(job_high, 1)

            def lows(it, v, gs):
                for g in gs:
                    lo, hi = GRP[g]
                    dve.wait_ge(hi_done, 3 * (STEPS * it + v) + g + 1)
                    dst = (slice(None), (v // 2) % 2, slice(lo, hi), slice((v % 2) * P, (v % 2 + 1) * P))
                    dve.tensor_tensor(ptl[dst], ps[:, TURN + (v + g) % 2, 0:(hi - lo) * P].rearrange("p (n t) -> p n t", t=P),
                                      pth[dst].bitcast(F32), ALU.subtract).then_inc(lo_done, 1)

            def step(w, b, it, blag, jobs, norm):
                for n, m in jobs:
                    job(n, m)
                for n in norm:
                    normalise(*n)
                behind = blag is not None
                v = w - LAG
                if (behind or v >= 0) and v < STEPS:
                    lows(it, v, (0, 1))
                if w < STEPS:
                    W = STEPS * it + w
                    dve.wait_ge(s_done, W + 1)
                    dve.wait_ge(turned, 3 * W + 3)
                    dve.tensor_scalar(p[:, w % 4, 0:3 * SN].rearrange("p (b c) -> p b c", c=SN), scores, -1.0, R_BIG, ALU.mult, ALU.min,
                                      accum_out=nmx[:, w % 2:w % 2 + 1]).then_inc(s_read, 1)
                if (behind or v >= 0) and v < STEPS:
                    lows(it, v, (2,))
                u = (w - LAG - 2) // 2
                if w % 2 == 0 and (behind or u >= 0):
                    dve.wait_ge(o_high, UNITS * it + u + 1)
                    dve.tensor_tensor(ol[:, :], ps[:, PV, 0:2 * P], oh[:, :].bitcast(F32), ALU.subtract).then_inc(o_split, 1)
                u = (w - LAG - 3) // 2
                if w % 2 == 1 and (behind or u >= 0):
                    t, s = 2 * (u % (UNITS // 2)), 2 * (u % UNITS)
                    U = UNITS * it + u
                    dve.reciprocal(rt[:, :], sums[:, s:s + 2]).then_inc(rt_made, 1)
                    dve.wait_ge(rt_made, 2 * U + 1)
                    dve.tensor_scalar(rt[:, :], rt[:, :], tg[:, 0:1], None, ALU.mult).then_inc(rt_made, 1)
                    dve.wait_ge(rt_made, 2 * U + 2)
                    dve.wait_ge(y_done, U + 1 + UNITS)
                    for i in range(2):
                        part = xres[:, bass.ds(TPB * (b if u >= 0 else blag) + t + i, 1), :].rearrange("p a d -> p (a d)")
                        last = dve.scalar_tensor_tensor(part, ps[:, PV, i * DIM:(i + 1) * DIM], rt[:, i:i + 1], part,
                                                        ALU.mult, ALU.add)
                    last.then_inc(y_added, 1)

            def first(jobs):
                for n, m in jobs:
                    if n is jobs[0][0] and m in (0, 2):
                        normalise(0, m)
                        normalise(0, m + 1)
                    job(n, m)

            run(dve, first, step)

        @block.tensor
        def _(pe):
            pe.sem_inc(y_done, UNITS)
            pe.sem_inc(turned, 12)

            def job(n, m):
                out = bank(n, m)
                if isinstance(n, Inputs):
                    k, lo, hi = XJOBS[m]
                    if m >= 2:
                        pe.wait_ge(job_full, n.full + m - 1)
                    elif not (isinstance(n.b, int) and n.b == 0):
                        pe.wait_ge(vt_low, n.vt - 1 + m)
                    cut = slice(k * P, (k + 1) * P)
                    if hi <= SEQ:
                        pe.wait_ge(z_ready, (TPB // 2 + 1) * n.b + hi // P // 2)
                        for t in range(lo // P, hi // P):
                            last = pe.transpose(out[:, t * P - lo:(t + 1) * P - lo], z[:, t % (TPB // 2), cut], ident[:, :])
                    else:
                        pe.wait_ge(z_ready, (TPB // 2 + 1) * (n.b + 1))
                        pe.transpose(out[:, 0:P], mA[:, cut], ident[:, :])
                        last = pe.transpose(out[:, P:CTX], mB[:, cut], ident[0:CTX - P, 0:CTX - P])
                    last.then_inc(job_done, 1)
                    return
                kind, lo, hi = JOBS[m]
                if m >= 2:
                    if JOBS[m - 2][0] == "t":
                        pe.wait_ge(vt_low, n.vt + m - 2 - NF + 1)
                    else:
                        pe.wait_ge(job_full, n.full + m - 1)
                elif n.first:
                    pe.wait_ge(job_full, n.xfull + NX - 1 + m)
                else:
                    pe.wait_ge(vt_low, n.vt - 1 + m)
                if m == 0:
                    pe.wait_ge(wq_split, 2 * n.it + n.j + 1 + 2)
                    if n.first:
                        pe.wait_ge(job_low, n.split + 2)
                if kind == "t":
                    if m == NF:
                        pe.wait_ge(job_full, n.full + NF)
                    for c in range(lo, hi, P):
                        last = pe.transpose(out[:, c - lo:c - lo + P], vf[:, c:c + P], ident[:, :])
                else:
                    i = "qkv".index(kind)
                    s = 0
                    for k in range(KT):
                        for w, x in ((wh, kvh), (wh, kvl), (wl, kvh)):
                            last = pe.matmul(out[:, 0:hi - lo], w[:, n.j, i, k * P:(k + 1) * P], x[:, k, lo:hi],
                                             start=(s == 0), stop=(s == 5))
                            s += 1
                last.then_inc(job_done, 1)

            def turn(it, v, gs):
                V = STEPS * it + v
                for g in gs:
                    lo, hi = GRP[g]
                    if g == 0:
                        pe.wait_ge(exp_done, V + 1)
                    pe.wait_ge(lo_done, 3 * V + g + 1)
                    for n in range(lo, hi):
                        last = pe.transpose(ps[:, TURN + (v + g) % 2, (n - lo) * P:(n - lo + 1) * P],
                                            p[:, v % 4, DUP + n * P:DUP + (n + 1) * P], ident[:, :])
                    last.then_inc(turned, 1)

            def score(it, w):
                j, t = w // TPB, w % TPB
                pe.wait_ge(s_read, STEPS * it + w + 1)
                for n in range(3):
                    for i, (q, k) in enumerate(((qh, kh), (qh, kl), (ql, kh))):
                        last = pe.matmul(scores[:, n, :], q[:, j, t * P:(t + 1) * P], k[:, j, SFROM[n]:SFROM[n] + SN],
                                         start=(i == 0), stop=(i == 2))
                last.then_inc(s_done, 1)

            def values(it, u):
                j = u % UNITS // (UNITS // 2)
                U = UNITS * it + u
                if u % (UNITS // 2) == 0:
                    pe.wait_ge(vt_low, 2 * NV * it + NV * (j + 1))
                pe.wait_ge(lo_done, 6 * (U + 1) + 2)
                pe.wait_ge(y_added, U + 1)
                for n in range(R_BLK):
                    for i, (v, x) in enumerate(((vh, pth), (vh, ptl), (vl, pth))):
                        last = pe.matmul(ps[:, PV, 0:2 * P], v[:, j, n * P:(n + 1) * P], x[:, u % 2, n, :],
                                         start=(n == 0 and i == 0), stop=(n == R_BLK - 1 and i == 2))
                last.then_inc(pv_done, 1)

            def project(it, u):
                j = u % UNITS // (UNITS // 2)
                U = UNITS * it + u
                if u % (UNITS // 2) == 0:
                    pe.wait_ge(wo_split, 2 * it + j + 1 + 2)
                pe.wait_ge(o_split, U + 1)
                for t in range(2):
                    for i, (o, w) in enumerate(((oh, wh), (oh, wl), (ol, wh))):
                        last = pe.matmul(ps[:, PV, t * DIM:(t + 1) * DIM], o[:, t * P:(t + 1) * P], w[:, j, 3, :],
                                         start=(i == 0), stop=(i == 2))
                last.then_inc(y_done, 1)

            def step(w, b, it, blag, jobs, norm):
                for n, m in jobs:
                    job(n, m)
                behind = blag is not None
                v = w - LAG
                if (behind or v >= 0) and v < STEPS:
                    turn(it, v, (0, 1))
                if w < STEPS:
                    if w % TPB == 0:
                        pe.wait_ge(job_low, 2 * NS * it + NX * (b + 1) + NS * (w // TPB + 1) + 2)
                    score(it, w)
                if (behind or v >= 0) and v < STEPS:
                    turn(it, v, (2,))
                u = (w - LAG - 2) // 2
                if w % 2 == 0 and (behind or u >= 0):
                    values(it, u)
                u = (w - LAG - 3) // 2
                if w % 2 == 1 and (behind or u >= 0):
                    project(it, u)

            def first(jobs):
                for n, m in jobs:
                    job(n, m)

            run(pe, first, step)


EXPERTS, TOPK, EH = 64, 8, 64
SHARED, SH = 2, 512
PAIRS = EXPERTS * EH // P
GB = 8
ROUTED = PAIRS // GB
GROUPS = ROUTED + SHARED * SH // P // GB
FREE = 2


def moe_stage(nc, xres, ident, A):
    with ExitStack() as ctx:
        def sb(name, shape, dt=F32):
            return ctx.enter_context(nc.sbuf_tensor("moe_" + name, shape, dt))

        def sem(name):
            return nc.alloc_semaphore("moe_" + name)

        lnT = sb("lnT", [P, KT, TOKENS])
        cwT = sb("cwT", [P, TOKENS], F32R)
        pick = sb("pick", [P, EXPERTS, EH], F32R)
        w1r, w2r = sb("w1r", [P, KT, GB * P]), sb("w2r", [P, GB, DIM])
        w1h, w1l = sb("w1h", [P, KT, GB * P], F32R), sb("w1l", [P, KT, GB * P], F32R)
        w2h, w2l = sb("w2h", [P, GB, DIM], F32R), sb("w2l", [P, GB, DIM], F32R)
        xh, xl = sb("xh", [P, 2, KT, CH], F32R), sb("xl", [P, 2, KT, CH], F32R)
        sil, gf = sb("sil", [P, 2, CH]), sb("gf", [P, 2, CH])
        gh, gl = sb("gh", [P, 2, CH], F32R), sb("gl", [P, 2, CH], F32R)
        stage = sb("stage", [P, KT, CH])
        rw, rb = sb("rw", [P, KT, EXPERTS]), sb("rb", [P, EXPERTS])
        b1, sb1 = sb("b1", [P, PAIRS]), sb("sb1", [P, GB])
        b2r, b2h, b2l = sb("b2r", [P, DIM]), sb("b2h", [P, DIM], F32R), sb("b2l", [P, DIM], F32R)
        sb2 = sb("sb2", [P, SHARED, KT])
        tg, tsb2 = sb("tg", [P, 1]), sb("tsb2", [P, KT])
        st, mv, rstd = sb("st", [P, TILES, 6]), sb("mv", [P, TILES, 2]), sb("rstd", [P, TILES])
        var, root = sb("var", [P, TILES]), sb("root", [P, TILES])
        lg, pr, rep = (sb(n, [P, TPC, EXPERTS]) for n in ("lg", "pr", "rep"))
        s4 = sb("s4", [P, TPC])
        top = sb("top", [P, TPC, TOPK])
        cwp = sb("cwp", [P, TPC, 2, EXPERTS], F32R)
        xn = [t[:, :, :].rearrange("p a c -> p (a c)").rearrange("p (t d) -> p t d", d=DIM) for t in (sil, gf)]
        lgT = sb("lgT", [EXPERTS, CH])
        ps = ctx.enter_context(nc.psum_tensor("moe_ps", [P, 8, CH], F32))
        HID, REP, OUT, TURN = 0, 2, 4, 6

        d_const, d_w, w_highs, w_split = sem("d_const"), sem("d_w"), sem("w_high"), sem("w_split")
        dve_own, act_own, pool_own = sem("dve_own"), sem("act_own"), sem("pool_own")
        alone = sem("alone")
        stats, rooted, pick_raw = sem("stats"), sem("rooted"), sem("pick_raw")
        pick_set, consts, b2_split = sem("pick_set"), sem("consts"), sem("b2_split")
        normed, turned, kept, routed, lg_kept, lg_turned, shifted, exped = (
            sem(n) for n in ("normed", "turned", "kept", "routed", "lg_kept", "lg_turned", "shifted", "exped"))
        route_sem = sem("route_own")
        cw_ready, cw_turned, cw_kept = sem("cw_ready"), sem("cw_turned"), sem("cw_kept")
        x_free, x_high, x_split = sem("x_free"), sem("x_high"), sem("x_split")
        hid_done, rep_done, silu_done, gate_done, high_done, g_split = (
            sem(n) for n in ("hid_done", "rep_done", "silu_done", "gate_done", "high_done", "g_split"))
        out_done, y_kept, y_turned, y_added = sem("out_done"), sem("y_kept"), sem("y_turned"), sem("y_added")
        block = ctx.enter_context(nc.Block())
        NCONST = 9
        R0 = CHUNKS * GB
        ROUTE_STEPS, ROUTE_DONE = 16, (0, 2, 9, 12)

        LAG = 2
        ENTRY = 4

        def blocks(eng, step):
            for q in range(ENTRY):
                step(0, 0, q, False)
            with eng.Fori(0, CHUNKS // 2 - 1) as cc:
                for q in range(ENTRY, GB):
                    step(2 * cc, 0, q, True)
                for q in range(GB):
                    step(2 * cc + 1, 1, q, True)
                for q in range(ENTRY):
                    step(2 * cc + 2, 0, q, True)
            for q in range(ENTRY, GB):
                step(CHUNKS - 2, 0, q, True)
            for q in range(GB):
                step(CHUNKS - 1, 1, q, True)

        @block.sync
        def _(sp):
            for dst, src in ((rw[:, :, :], A["L0_ffn_router_w"].rearrange("(k p) e -> p k e", p=P)),
                             (rb[:, :], A["L0_ffn_router_b"].partition_broadcast(P)),
                             (tg[:, :], A["g_ffn"][0:1].partition_broadcast(P)),
                             (b2r[0:EXPERTS, :], A["L0_ffn_b2"]), (b2r[EXPERTS:P, :], A["L0_ffn_b2"]),
                             (sb1[:, :], A["L0_ffn_sb1"].rearrange("s (b p) -> p (s b)", p=P)),
                             (sb2[:, 0, :], A["L0_ffn_sb2"][0].rearrange("(k p) -> p k", p=P)),
                             (sb2[:, 1, :], A["L0_ffn_sb2"][1].rearrange("(k p) -> p k", p=P)),
                             (b1[:, :], A["L0_ffn_b1"].rearrange("(q e) h -> (e h) q", e=2))):
                with nc.allow_non_contiguous_dma(reason='small columns'):
                    sp.dma_start(dst, src).then_inc(d_const, 16)
            for g in range(GROUPS):
                if g:
                    sp.wait_ge(w_split, 2 * g)
                for k in range(KT):
                    if g:
                        e = slice(2 * GB * (g - 1), 2 * GB * g)
                        src = A["L0_ffn_w1"][e, k * P:(k + 1) * P, :]
                    else:
                        src = A["L0_ffn_sw1"][:, k * P:(k + 1) * P, :]
                    sp.dma_start(w1r[:, k, :].rearrange("p (e h) -> p e h", h=src.shape[2]),
                                 src.rearrange("e p h -> p e h")).then_inc(d_w, 16)
                if g:
                    src = A["L0_ffn_w2"][e].rearrange("(q e) h d -> (e h) q d", e=2)
                else:
                    src = A["L0_ffn_sw2"].rearrange("s (b p) d -> p (s b) d", p=P)
                sp.dma_start(w2r[:, :, :], src).then_inc(d_w, 16)

        @block.gpsimd
        def _(pool):
            own = Chain(pool, pool_own)
            pool.sem_inc(x_free, FREE)
            one = lnT[:, 0, :].rearrange("p (e h) -> p e h", h=EH)
            own.link(pool.memset(one, 0.0))
            for part in (0, EXPERTS):
                own.link(pool.affine_select(out=one, in_=one, compare_op=ALU.not_equal, fill=1.0, base=-part,
                                            pattern=[[-1, EXPERTS], [0, EH]], channel_multiplier=1))
            pool.sem_inc(pick_raw, 1)
            for g in range(GROUPS):
                with pool.Fori(0, CHUNKS // 2) as cc:
                    for j in range(2):
                        n = g * CHUNKS + 2 * cc + j
                        src = lnT[:, :, bass.ds((2 * cc + j) * CH, CH)]
                        pool.wait_ge(x_free, n + 1)
                        if g == 0:
                            pool.wait_ge(kept, 2 * (2 * cc + j) + 2)
                        pool.sem_inc(alone, 1)
                        pool.tensor_copy(xh[:, j, :, :], src).then_inc(x_high, 1)
                        pool.wait_ge(x_high, n + 1)
                        pool.sem_inc(alone, 1)
                        pool.tensor_tensor(xl[:, j, :, :], src, xh[:, j, :, :].bitcast(F32), ALU.subtract).then_inc(x_split, 1)

        @block.scalar
        def _(act):
            own = Chain(act, act_own)
            act.sem_inc(silu_done, FREE)
            act.sem_inc(y_kept, FREE)
            act.sem_inc(lg_kept, 1)
            act.sem_inc(cw_kept, 1)
            act.wait_ge(d_const, 16 * NCONST)
            act.activation(tg[:, :], tg[:, :], ACT.Tanh).then_inc(consts, 1)

            def w_high(g, part):
                if part == 0:
                    act.wait_ge(d_w, 48 * (g + 1))
                if g:
                    act.wait_ge((hid_done, out_done)[part], g * CHUNKS * GB + (0, FREE)[part])
                r, h = ((w1r, w1h), (w2r, w2h))[part]
                act.activation(h[:, :, :], r[:, :, :], ACT.Copy).then_inc(w_highs, 1)

            act.wait_ge(pick_raw, 1)
            act.activation(pick[:, :, :], lnT[:, 0, :].rearrange("p (e h) -> p e h", h=EH), ACT.Copy).then_inc(pick_set, 1)
            act.wait_ge(stats, 1)
            act.activation(root[:, :], var[:, :], ACT.Sqrt).then_inc(rooted, 1)
            w_high(0, 0)
            w_high(0, 1)
            act.wait_ge(pick_set, 1)
            for c in range(CHUNKS):
                for k in range(KT):
                    act.wait_ge(turned, KT * c + k + 1)
                    act.activation(lnT[:, k, c * CH:(c + 1) * CH], ps[:, KT * (c % 4) + k, :], ACT.Copy).then_inc(kept, 1)
            for g in range(GROUPS):
                act.wait_ge(consts, 2)

                def keep_y(n):
                    act.wait_ge(out_done, GB * n + GB + FREE)
                    act.wait_ge(y_turned, 2 * n + FREE)
                    for k in range(KT):
                        bias = tsb2[:, k:k + 1] if g == 0 else 0.0
                        act.activation(stage[:, k, :], ps[:, OUT + k, :], ACT.Identity, bias=bias,
                                       scale=tg[:, 0:1]).then_inc(y_kept, 1)

                def step(c, j, q, before):
                    n = g * CHUNKS + c
                    u = n * GB + q
                    act.wait_ge(hid_done, u + 1)
                    if g:
                        act.wait_ge(gate_done, u + 1 - R0)
                        dst, bias = sil, b1[:, (g - 1) * GB + q:(g - 1) * GB + q + 1]
                    else:
                        act.wait_ge(g_split, u + 1)
                        dst, bias = gf, sb1[:, q:q + 1]
                    act.activation(dst[:, q % 2, :], ps[:, HID + q % 2, :], ACT.Silu, bias=bias).then_inc(silu_done, 1)
                    if q == LAG - 1 and before:
                        keep_y(n - 1)
                    if g == 0 and q == 1:
                        act.wait_ge(routed, n + 1)
                        act.activation(lgT[:, :], ps[0:EXPERTS, REP, :], ACT.Copy).then_inc(lg_kept, 1)
                    if g == 0 and q == 4:
                        act.wait_ge(shifted, n + 1)
                        act.activation(pr[:, :, :], lg[:, :, :], ACT.Exp).then_inc(exped, 1)
                    if g == 0 and q == GB - 1:
                        act.wait_ge(cw_turned, n + 1)
                        act.activation(cwT[:, bass.ds(c * CH, CH)], ps[:, REP + 1, :], ACT.Copy).then_inc(cw_kept, 1)

                blocks(act, step)
                if g + 1 < GROUPS:
                    w_high(g + 1, 0)
                keep_y((g + 1) * CHUNKS - 1)
                if g + 1 < GROUPS:
                    w_high(g + 1, 1)

        @block.vector
        def _(dve):
            own = Chain(dve, dve_own)
            dve.sem_inc(gate_done, FREE)
            dve.sem_inc(g_split, FREE)
            dve.sem_inc(y_added, FREE)
            def over(x, n=EXPERTS):
                return x.unsqueeze(2).broadcast_to([P, TPC, n])

            for t in range(TILES):
                own.step(dve.bn_stats(st[:, t, :], xres[:, t, :]))
            own.wait()
            for t in range(TILES):
                own.step(dve.bn_aggr(mv[:, t, :], st[:, t, :]))
            own.wait()
            dve.tensor_scalar(var[:, :], mv[:, :, 1], EPS, None, ALU.add).then_inc(stats, 1)
            dve.wait_ge(consts, 1)
            own.link(dve.tensor_tensor(tsb2[:, :], sb2[:, 0, :], sb2[:, 1, :], ALU.add))
            dve.tensor_scalar(tsb2[:, :], tsb2[:, :], tg[:, 0:1], None, ALU.mult).then_inc(consts, 1)
            own.link(dve.tensor_copy(b2h[:, :], b2r[:, :]))
            dve.tensor_tensor(b2l[:, :], b2r[:, :], b2h[:, :].bitcast(F32), ALU.subtract).then_inc(b2_split, 1)

            def w_low(g, part):
                r, h, l = ((w1r, w1h, w1l), (w2r, w2h, w2l))[part]
                dve.wait_ge(w_highs, 2 * g + part + 1)
                if g:
                    dve.wait_ge((hid_done, out_done)[part], g * CHUNKS * GB + (0, FREE)[part])
                dve.tensor_tensor(l[:, :, :], r[:, :, :], h[:, :, :].bitcast(F32), ALU.subtract).then_inc(w_split, 1)

            dve.wait_ge(rooted, 1)
            newton_rsqrt(own, dve, var[:, :], root[:, :], rstd[:, :])
            for c in range(CHUNKS):
                if c >= 2:
                    dve.wait_ge(turned, KT * (c - 1))
                for t in range(TPC):
                    n = TPC * c + t
                    dve.tensor_scalar(xn[c % 2][:, t, :], xres[:, n, :], mv[:, n, 0:1], rstd[:, n:n + 1],
                                      ALU.subtract, ALU.mult).then_inc(normed, 1)
                if c == 1:
                    w_low(0, 0)
                    w_low(0, 1)
            def route(c, part):
                own = Chain(dve, route_sem)
                own.base, own.k = ROUTE_STEPS * c, ROUTE_DONE[part]
                if part == 0:
                    dve.wait_ge(lg_turned, c + 1)
                    logits = ps[:, REP + 1, 0:TPC * EXPERTS].rearrange("p (t e) -> p t e", e=EXPERTS)
                    own.link(dve.tensor_tensor(lg[:, :, :], logits, rb[:, :].unsqueeze(1).broadcast_to([P, TPC, EXPERTS]), ALU.add))
                    own.link(dve.tensor_reduce(s4[:, :], lg[:, :, :], AX.X, ALU.max))
                    dve.tensor_tensor(lg[:, :, :], lg[:, :, :], over(s4[:, :]), ALU.subtract).then_inc(shifted, 1)
                elif part == 1:
                    dve.wait_ge(exped, c + 1)
                    own.link(dve.tensor_reduce(s4[:, :], pr[:, :, :], AX.X, ALU.add))
                    own.link(dve.reciprocal(s4[:, :], s4[:, :]))
                    own.link(dve.tensor_tensor(pr[:, :, :], pr[:, :, :], over(s4[:, :]), ALU.mult))
                    dve.sem_inc(alone, 1)
                    for t in range(TPC):
                        own.step(dve.max(top[:, t, :], pr[:, t, :]))
                elif part == 2:
                    own.wait()
                    dve.sem_inc(alone, 1)
                    for t in range(TPC):
                        last = dve.match_replace(rep[:, t, :], top[:, t, :], pr[:, t, :], -1.0)
                        if t == TPC - 1:
                            own.link(last)
                    own.link(dve.tensor_tensor(rep[:, :, :], rep[:, :, :], pr[:, :, :], ALU.not_equal))
                    own.link(dve.tensor_tensor(pr[:, :, :], pr[:, :, :], rep[:, :, :], ALU.mult))
                else:
                    own.link(dve.tensor_reduce(s4[:, :], pr[:, :, :], AX.X, ALU.add))
                    own.link(dve.reciprocal(s4[:, :], s4[:, :]))
                    own.link(dve.tensor_tensor(rep[:, :, :], pr[:, :, :], over(s4[:, :]), ALU.mult))
                    own.link(dve.tensor_copy(cwp[:, :, 0, :], rep[:, :, :]))
                    dve.tensor_tensor(cwp[:, :, 1, :], rep[:, :, :], cwp[:, :, 0, :].bitcast(F32), ALU.subtract).then_inc(cw_ready, 1)

            def add_y(n, c):
                for b in range(2):
                    dve.wait_ge(y_turned, 2 * n + b + 1 + FREE)
                    part = xres[:, bass.ds(c * TPC + 2 * b, 2), :].rearrange("p t d -> p (t d)")
                    dve.tensor_tensor(part, part, ps[:, TURN + b, :], ALU.add).then_inc(y_added, 1)

            for g in range(GROUPS):

                def step(c, j, q, before):
                    n = g * CHUNKS + c
                    u = n * GB + q
                    dve.wait_ge(silu_done, u + 1 + FREE)
                    if g:
                        dve.wait_ge(rep_done, u + 1 - R0)
                        dve.tensor_tensor(gf[:, q % 2, :], sil[:, q % 2, :], ps[:, REP + q % 2, :], ALU.mult).then_inc(gate_done, 1)
                        dve.wait_ge(gate_done, u + 1 - R0 + FREE)
                    dve.wait_ge(out_done, u + 1)
                    dve.tensor_copy(gh[:, q % 2, :], gf[:, q % 2, :]).then_inc(high_done, 1)
                    dve.wait_ge(high_done, u + 1)
                    dve.tensor_tensor(gl[:, q % 2, :], gf[:, q % 2, :], gh[:, q % 2, :].bitcast(F32),
                                      ALU.subtract).then_inc(g_split, 1)
                    if q == LAG + 1 and before:
                        add_y(n - 1, c - 1)
                    if g == 0 and 3 <= q < 7:
                        route(c, q - 3)

                blocks(dve, step)
                if g + 1 < GROUPS:
                    w_low(g + 1, 0)
                    w_low(g + 1, 1)
                add_y((g + 1) * CHUNKS - 1, CHUNKS - 1)

        @block.tensor
        def _(pe):
            pe.sem_inc(out_done, FREE)
            pe.sem_inc(y_turned, FREE)
            pe.wait_ge(d_const, 16 * NCONST)
            for c in range(CHUNKS):
                pe.wait_ge(normed, TPC * (c + 1))
                if c >= 4:
                    pe.wait_ge(kept, KT * (c - 3))
                for k in range(KT):
                    for t in range(TPC):
                        last = pe.transpose(ps[:, KT * (c % 4) + k, t * P:(t + 1) * P], xn[c % 2][:, t, k * P:(k + 1) * P], ident[:, :])
                    last.then_inc(turned, 1)
            pe.wait_ge(kept, KT * CHUNKS)
            pe.wait_ge(b2_split, 1)
            pe.wait_ge(pick_set, 1)

            def hidden(g, n, j, q, cw):
                u = n * GB + q
                if g:
                    pe.wait_ge(gate_done, u + 1 - R0)
                    e = 2 * ((g - 1) * GB + q)
                    pe.matmul(ps[:, REP + q % 2, :], pick[:, e:e + 2, :].rearrange("p e h -> p (e h)"), cw,
                              start=True, stop=True).then_inc(rep_done, 1)
                pe.wait_ge(silu_done, u + 1)
                if q == 0:
                    pe.wait_ge(x_split, n + 1)
                i = 0
                for k in range(KT):
                    for w, x in ((w1h, xh), (w1h, xl), (w1l, xh)):
                        last = pe.matmul(ps[:, HID + q % 2, :], w[:, k, q * P:(q + 1) * P], x[:, j, k, :],
                                         start=(i == 0), stop=(i == 3 * KT - 1))
                        i += 1
                last.then_inc(hid_done, 1)

            def project(g, n, q, cw):
                u = n * GB + q
                if q == 0:
                    pe.wait_ge(w_split, 2 * (g + 1))
                    pe.wait_ge(y_kept, 2 * n + FREE)
                if q == 0 and g == 1:
                    for k in range(KT):
                        for i, w in enumerate((b2h, b2l)):
                            pe.matmul(ps[:, OUT + k, :], w[:, k * P:(k + 1) * P], cw, start=(i == 0), stop=False)
                pe.wait_ge(g_split, u + 1 + FREE)
                for k in range(KT):
                    for i, (w, x) in enumerate(((w2h, gh), (w2h, gl), (w2l, gh))):
                        last = pe.matmul(ps[:, OUT + k, :], w[:, q, k * P:(k + 1) * P], x[:, q % 2, :],
                                         start=(g != 1 and q == 0 and i == 0), stop=(q == GB - 1 and i == 2))
                        if q == GB - 2 and k == 0 and i == 0:
                            last.then_inc(x_free, 1)
                last.then_inc(out_done, 1)

            def turn_y(n):
                pe.wait_ge(y_kept, 2 * n + 2 + FREE)
                for b in range(2):
                    pe.wait_ge(y_added, 2 * n + b + 1)
                    for t in range(2):
                        for k in range(KT):
                            last = pe.transpose(ps[:, TURN + b, (t * KT + k) * P:(t * KT + k + 1) * P],
                                                stage[:, k, (2 * b + t) * P:(2 * b + t + 1) * P], ident[:, :])
                    last.then_inc(y_turned, 1)

            def logits(c, x):
                pe.wait_ge(lg_kept, c + 1)
                for k in range(KT):
                    last = pe.matmul(ps[0:EXPERTS, REP, :], rw[:, k, :], x[:, k, :], start=(k == 0), stop=(k == KT - 1))
                last.then_inc(routed, 1)

            def turn_logits(c):
                pe.wait_ge(lg_kept, c + 2)
                pe.wait_ge(cw_kept, c + 1)
                pe.sem_inc(alone, 1)
                for t in range(TPC):
                    last = pe.transpose(ps[:, REP + 1, t * EXPERTS:(t + 1) * EXPERTS], lgT[:, t * P:(t + 1) * P],
                                        ident[0:EXPERTS, 0:EXPERTS])
                last.then_inc(lg_turned, 1)

            def turn_weights(c):
                pe.wait_ge(cw_ready, c + 1)
                for t in range(TPC):
                    last = pe.transpose(ps[:, REP + 1, t * P:(t + 1) * P],
                                        cwp[:, t, :, :].bitcast(F32).rearrange("p a e -> p (a e)"), ident[:, :])
                last.then_inc(cw_turned, 1)

            for g in range(GROUPS):
                pe.wait_ge(w_split, 2 * g + 1)
                if g == 1:
                    pe.wait_ge(cw_kept, CHUNKS + 1)

                def weights(c):
                    return cwT[:, bass.ds(c * CH, CH)] if g else None

                def step(c, j, q, before):
                    n = g * CHUNKS + c
                    hidden(g, n, j, q, weights(c))
                    if g == 0 and q == 1:
                        logits(n, lnT[:, :, bass.ds(c * CH, CH)])
                    if g == 0 and q == 2:
                        turn_logits(n)
                    if q == LAG + 1 and before:
                        turn_y(n - 1)
                    if q >= LAG:
                        project(g, n, q - LAG, weights(c))
                    elif before:
                        project(g, n - 1, GB - LAG + q, None)
                    if g == 0 and q == GB - 1:
                        turn_weights(n)

                blocks(pe, step)
                for q in range(GB - LAG, GB):
                    project(g, (g + 1) * CHUNKS - 1, q, None)
                turn_y((g + 1) * CHUNKS - 1)


C_HEADS, C_DH = 16, 16
C_HPH = C_HEADS // 2
C_TAIL = 32
C_DUP = P + C_TAIL - CTX
C_NEG = -1.0e30


def ctx_attention_stage(nc, xres, ident, A):
    with ExitStack() as ctx:
        def sb(name, shape, dt=F32):
            return ctx.enter_context(nc.sbuf_tensor("x1_" + name, shape, dt))

        def sem(name):
            return nc.alloc_semaphore("x1_" + name)

        names = ("L1_xattn_Wq", "L1_xattn_Wk", "L1_xattn_Wv", "L1_xattn_Wo")
        ROW = C_HPH * (P + C_TAIL)
        p = sb("p", [P, 4, ROW])
        wraw = p[:, 0:2, :].rearrange("p a j -> p (a j)")[:, 0:4 * 2 * DIM].rearrange("p (w o d) -> p w o d", w=4, o=2)
        ctxA = p[:, 2:4, :].rearrange("p a j -> p (a j)")[:, 0:4 * DIM].rearrange("p (b d) -> p b d", b=4)
        ctxB = p[:, 2:4, :].rearrange("p a j -> p (a j)")[0:CTX - P, 4 * DIM:8 * DIM].rearrange("p (b d) -> p b d", b=4)
        NBLK = C_HPH + 2
        pth, ptl = sb("pth", [P, 2, NBLK, 2 * P], F32R), sb("ptl", [P, 2, NBLK, 2 * P], F32R)

        def early(t, at, shape):
            flat = t[:, :, :, :].rearrange("p a n c -> p (a n c)")[:, at:at + int(np.prod(shape))]
            names = " ".join("abc"[:len(shape)])
            return flat.rearrange(f"p ({names}) -> p {names}", **dict(zip("abc", shape)))

        cth, ctl = (early(t, 0, (KT, BATCH, CTX)) for t in (pth, ptl))
        at = KT * BATCH * CTX
        wh = [sb("wqh", [P, KT, DIM], F32R), early(pth, at, (KT, DIM)), early(pth, at + KT * DIM, (KT, DIM)), sb("woh", [P, KT, DIM], F32R)]
        wl = [sb("wql", [P, KT, DIM], F32R), early(ptl, at, (KT, DIM)), early(ptl, at + KT * DIM, (KT, DIM)), sb("wol", [P, KT, DIM], F32R)]
        kTh, kTl = sb("kTh", [P, 2, BATCH, CTX], F32R), sb("kTl", [P, 2, BATCH, CTX], F32R)
        vAh, vAl = sb("vAh", [P, BATCH, DIM], F32R), sb("vAl", [P, BATCH, DIM], F32R)
        vBh, vBl = sb("vBh", [P, BATCH, DIM], F32R), sb("vBl", [P, BATCH, DIM], F32R)
        hmask_one = sb("one_row", [P, P])
        hmask = sb("hmask", [P, C_HPH])
        onesT = sb("onesT", [P, 4, P], F32R)
        tmask = sb("tmask", [P, 4, P])[:, :, :].rearrange("p (a b) (h d) -> p a b h d", a=2, d=C_DH)
        DIAG = P + C_DH
        onesA = sb("onesA", [P, C_HPH * DIAG], F32R)
        zero = sb("zero", [P, DIAG])
        scratch = sb("scratch", [P, 4 * CTX])
        cm = scratch[:, :].rearrange("p (t h j) -> p t h j", t=2, h=2)
        causal = sb("causal", [P, 2, 2, CTX], F32R)
        identr = sb("identr", [P, P], F32R)
        kbh, kbl = sb("kbh", [P, 2, C_HPH, CTX], F32R), sb("kbl", [P, 2, C_HPH, CTX], F32R)
        vah, val = sb("vah", [P, 2, C_HPH * DIAG], F32R), sb("val", [P, 2, C_HPH * DIAG], F32R)
        vbh, vbl = sb("vbh", [P, 4, P], F32R), sb("vbl", [P, 4, P], F32R)
        bor = sb("bor", [1, DIM])
        boh, bol, one1 = sb("boh", [1, DIM], F32R), sb("bol", [1, DIM], F32R), sb("one1", [1, P], F32R)
        tg = sb("tg", [P, 1])
        st, mv = sb("st", [P, TILES, 6]), sb("mv", [P, TILES, 2])
        var, root, rstd = sb("var", [P, TILES]), sb("root", [P, TILES]), sb("rstd", [P, TILES])
        y = sb("y", [P, 2, DIM])
        xTh, xTl = sb("xTh", [P, KT, 2 * P], F32R), sb("xTl", [P, KT, 2 * P], F32R)
        qh, ql = sb("qh", [P, 2, 2, 2 * P], F32R), sb("ql", [P, 2, 2, 2 * P], F32R)
        tails = [t[:, :, :, :].rearrange("p s h c -> p s (h c)").rearrange("p k (b r j) -> p k b r j", b=BATCH, j=C_TAIL) for t in (qh, ql)]
        mx = sb("mx", [P, C_HPH])
        of, rs = scratch[:, 0:2 * P], scratch[:, 2 * P:4 * P]
        oh, ol = sb("oh", [P, 2, 2 * P], F32R), sb("ol", [P, 2, 2 * P], F32R)
        ps = ctx.enter_context(nc.psum_tensor("x1_ps", [P, 8, CH], F32))
        TURN, PV, WO = 4, 6, 7
        scores = ps[:, 0:4, 0:2 * CTX].rearrange("p b (h j) -> p b h j", j=CTX)

        d_in, set_up, dve_own, pool_own = sem("d_in"), sem("set_up"), sem("dve_own"), sem("pool_own")
        pre_done, pre_hi, pre_lo = sem("pre_done"), sem("pre_hi"), sem("pre_lo")
        tanhed, stats, rooted, ready = sem("tanhed"), sem("stats"), sem("rooted"), sem("ready")
        y_ready, x_turned, x_hi, x_lo = sem("y_ready"), sem("x_turned"), sem("x_hi"), sem("x_lo")
        q_done, q_high, q_split, k_high, k_low, v_spread = (
            sem(n) for n in ("q_done", "q_high", "q_split", "k_high", "k_low", "v_spread"))
        s_done, s_read, exp_done, turned, hi_done, lo_done = (
            sem(n) for n in ("s_done", "s_read", "exp_done", "turned", "hi_done", "lo_done"))
        o_recip, o_normed, o_high = sem("o_recip"), sem("o_normed"), sem("o_high")
        alone_pool, zero_set, zeroed = sem("alone_pool"), sem("zero_set"), sem("zeroed")
        pv_done, o_read, o_split, wo_done, x_added, max_made = (
            sem(n) for n in ("pv_done", "o_read", "o_split", "wo_done", "x_added", "max_made"))
        tails_set = sem("tails_set")
        block = ctx.enter_context(nc.Block())
        STEPS = 2 * TPB
        CPB = TPB // 2
        VALUES, SUMS, PROJECT = 5, 6, 10
        LOOP = PROJECT

        def steps(eng, step):
            for w in range(LOOP):
                step(0, w, False, True)
            with eng.Fori(0, BATCH - 1) as b:
                for w in range(LOOP, STEPS):
                    step(b, w, True, True)
                for w in range(LOOP):
                    step(b + 1, w, True, True)
            for w in range(LOOP, STEPS + PROJECT - 2 + 1):
                step(BATCH - 1, w, True, False)

        def behind(w, lag, period, before):
            v = w - lag
            return v // period if v % period == 0 and v < STEPS and (before or v >= 0) else None
        NJOB = 16
        GRP = ((0, 4), (4, 8), (8, 10))

        def job_out(n):
            if n < 4:
                return 2 * DIM, wh[n][:, :, :].rearrange("p k d -> p (k d)"), wl[n][:, :, :].rearrange("p k d -> p (k d)")
            if n < 12:
                h, l = (cth, ctl) if n < 8 else (kTh, kTl)
                k, b = (n % 4) // 2, n % 2
                return 2 * CTX, *(t[:, k, 2 * b:2 * b + 2, :].rearrange("p b j -> p (b j)") for t in (h, l))
            h, l = (vAh, vAl) if n < 14 else (vBh, vBl)
            return 2 * DIM, *(t[:, 2 * (n % 2):2 * (n % 2) + 2, :].rearrange("p b d -> p (b d)") for t in (h, l))

        @block.sync
        def _(sp):
            for i, n in enumerate(names):
                sp.dma_start(wraw[:, i, :, :], A[n].rearrange("(o p) d -> p o d", p=P)).then_inc(d_in, 16)
            sp.dma_start(ctxA, A["ctx_1024"][:, 0:P, :].rearrange("b j d -> j b d")).then_inc(d_in, 16)
            sp.dma_start(ctxB, A["ctx_1024"][:, P:CTX, :].rearrange("b j d -> j b d")).then_inc(d_in, 16)
            sp.dma_start(bor[:, :], A["L1_xattn_bo"].rearrange("(a d) -> a d", a=1)).then_inc(d_in, 16)
            with nc.allow_non_contiguous_dma(reason="one column"):
                sp.dma_start(tg[:, :], A["g_xattn"][1:2].partition_broadcast(P)).then_inc(d_in, 16)
        ND = 8

        @block.gpsimd
        def _(pool):
            own = Chain(pool, pool_own)
            pool.memset(zero[:, :], 0.0).then_inc(zero_set, 1)
            own.step(pool.memset(hmask[:, :], 1.0))
            own.step(pool.memset(tmask, 1.0))
            own.step(pool.memset(cm, 0.0))
            own.wait()
            own.link(pool.affine_select(out=hmask[:, :], in_=hmask[:, :], compare_op=ALU.is_ge, fill=0.0, base=0,
                                        pattern=[[-C_DH, C_HPH]], channel_multiplier=1))
            own.link(pool.affine_select(out=hmask[:, :], in_=hmask[:, :], compare_op=ALU.is_ge, fill=0.0, base=C_DH - 1,
                                        pattern=[[C_DH, C_HPH]], channel_multiplier=-1))
            for h in range(2):
                m = tmask[:, h, :, :, :]
                own.link(pool.affine_select(out=m, in_=m, compare_op=ALU.is_ge, fill=0.0, base=-C_DUP,
                                            pattern=[[P, 2], [-C_TAIL, C_HPH], [0, C_DH]], channel_multiplier=1))
                own.link(pool.affine_select(out=m, in_=m, compare_op=ALU.is_ge, fill=0.0, base=C_TAIL - 1,
                                            pattern=[[-P, 2], [C_TAIL, C_HPH], [0, C_DH]], channel_multiplier=-1))
            own.link(pool.affine_select(out=cm, in_=cm, compare_op=ALU.is_ge, fill=C_NEG, base=0,
                                        pattern=[[P, 2], [0, 2], [-1, CTX]], channel_multiplier=1))
            own.step(pool.tensor_copy(causal[:, :, :, :], cm))
            own.step(pool.tensor_copy(identr[:, :], ident[:, :]))
            own.step(pool.tensor_copy(onesT[:, :, :], tmask.rearrange("p a b h d -> p (a b) (h d)")))
            pool.wait_ge(zeroed, 5)
            own.link(pool.memset(hmask_one[:, :], 1.0))
            own.step(pool.tensor_copy(onesA[:, :].rearrange("p (h c) -> p h c", c=DIAG)[:, :, 0:C_DH],
                                      hmask_one[:, :].rearrange("p (h c) -> p h c", c=C_DH)))
            pool.tensor_copy(one1[:, :], hmask_one[0:1, :]).then_inc(set_up, 1)
            own.wait()
            pool.wait_ge(set_up, 1)
            pool.wait_ge(pre_lo, NJOB)

            def spread_k(b, h):
                src = kTl[:, h, bass.ds(b, 1), :].bitcast(F32).broadcast_to([P, C_HPH, CTX])
                pool.tensor_tensor(kbl[:, h, :, :], src, hmask[:, :].unsqueeze(2).broadcast_to([P, C_HPH, CTX]), ALU.mult).then_inc(k_low, 1)

            def spread_v(b, h):
                for s, d in ((vAh, vah), (vAl, val)):
                    pool.tensor_copy(d[:, h, :].rearrange("p (h c) -> p h c", c=DIAG)[:, :, 0:C_DH],
                                     s[:, bass.ds(b, 1), h * P:(h + 1) * P].bitcast(F32).rearrange("p a (h c) -> p (a h) c", c=C_DH)).then_inc(v_spread, 1)
                for s, d in ((vBh, vbh), (vBl, vbl)):
                    for g in range(2):
                        pool.tensor_tensor(d[:, 2 * h + g, :], s[:, bass.ds(b, 1), h * P:(h + 1) * P].bitcast(F32).rearrange("p a c -> p (a c)"),
                                           tmask[:, h, g, :, :].rearrange("p h d -> p (h d)"), ALU.mult).then_inc(v_spread, 1)

            def step(b, w, before, after):
                if w in (STEPS - 2, STEPS - 1) and after:
                    pool.wait_ge(s_done, STEPS * b + 2 * w - (STEPS - 2))
                    pool.sem_inc(alone_pool, 1)
                    spread_k(b + 1, w - (STEPS - 2))
                u = behind(w, SUMS, 2, before)
                if u is not None:
                    U = TPB * b + u
                    pool.wait_ge(o_recip, U + 1)
                    pool.sem_inc(alone_pool, 1)
                    pool.tensor_tensor(of, of, rs, ALU.mult).then_inc(o_normed, 1)
                    pool.wait_ge(wo_done, CPB * b + u // 2 + 1)
                    pool.wait_ge(o_normed, U + 1)
                    pool.sem_inc(alone_pool, 1)
                    pool.tensor_copy(oh[:, u % 2, :], of).then_inc(o_high, 1)
                    pool.wait_ge(o_high, U + 1)
                    pool.sem_inc(alone_pool, 1)
                    pool.tensor_tensor(ol[:, u % 2, :], of, oh[:, u % 2, :].bitcast(F32), ALU.subtract).then_inc(o_split, 1)
                    if -2 <= u < 0:
                        spread_v(b, u + 2)

            for h in range(2):
                spread_k(0, h)
                spread_v(0, h)
            steps(pool, step)

        @block.scalar
        def _(act):
            act.wait_ge(zero_set, 1)
            for t in (onesA[:, :], vah[:, 0, :], vah[:, 1, :], val[:, 0, :], val[:, 1, :]):
                act.activation(t.rearrange("p (h c) -> p h c", c=DIAG), zero[:, :].unsqueeze(1).broadcast_to([P, C_HPH, DIAG]),
                               ACT.Copy).then_inc(zeroed, 1)
            act.wait_ge(d_in, 16 * ND)
            act.activation(tg[:, :], tg[:, :], ACT.Tanh).then_inc(tanhed, 1)
            for n in range(NJOB):
                size, h, _ = job_out(n)
                act.wait_ge(pre_done, n + 1)
                act.activation(h, ps[:, n % 8, 0:size], ACT.Copy).then_inc(pre_hi, 1)
                if n == 11:
                    for t, c in zip(tails, (cth, ctl)):
                        for k in range(KT):
                            src = c[:, k, :, CTX - C_TAIL:CTX].bitcast(F32).unsqueeze(2).broadcast_to([P, BATCH, P // C_TAIL, C_TAIL])
                            act.activation(t[:, k, :, :, :], src, ACT.Copy).then_inc(tails_set, 1)
            act.wait_ge(stats, 1)
            act.activation(root[:, :], var[:, :], ACT.Sqrt).then_inc(rooted, 1)

            def x_part(C):
                act.wait_ge(x_turned, C + 1)
                act.activation(xTh[:, :, :].rearrange("p k t -> p (k t)"), ps[:, WO, :], ACT.Copy).then_inc(x_hi, 1)

            def q_part(C, slot):
                act.wait_ge(q_done, C + 1)
                act.activation(qh[:, slot, :, :].rearrange("p h t -> p (h t)"), ps[:, WO, :], ACT.Copy,
                               scale=float(C_DH) ** -0.5).then_inc(q_high, 1)

            def high(b, v, g):
                if v is None:
                    return
                lo, hi = GRP[g]
                act.wait_ge(turned, 3 * (STEPS * b + v) + g + 1 + 12)
                act.activation(pth[:, (v // 2) % 2, lo:hi, (v % 2) * P:(v % 2 + 1) * P],
                               ps[:, TURN + (v + g) % 2, 0:(hi - lo) * P].rearrange("p (n t) -> p n t", t=P),
                               ACT.Copy).then_inc(hi_done, 1)

            def step(b, w, before, after):
                high(b, behind(w, 3, 1, before), 2)
                if w % 4 == 0 and w < STEPS and (after or w + 4 < STEPS):
                    q_part(CPB * b + w // 4 + 1, (w // 4 + 1) % 2)
                high(b, behind(w, 2, 1, before), 0)
                u = behind(w, SUMS, 2, before)
                if u is not None:
                    act.wait_ge(pv_done, TPB * b + u + 1)
                    act.wait_ge(o_split, TPB * b + u + 1)
                    act.activation(scratch[:, 0:4 * P], ps[:, PV, :], ACT.Copy).then_inc(o_read, 1)
                if w % 4 == 3 and w < STEPS and (after or w + 5 < STEPS):
                    x_part(CPB * b + (w + 5) // 4)
                high(b, behind(w, 2, 1, before), 1)
                if w < STEPS:
                    act.wait_ge(s_read, STEPS * b + w + 1 + 1)
                    act.activation(p[:, w % 4, :], p[:, w % 4, :], ACT.Exp).then_inc(exp_done, 1)

            x_part(0)
            q_part(0, 0)
            x_part(1)
            steps(act, step)

        @block.vector
        def _(dve):
            own = Chain(dve, dve_own)
            dve.sem_inc(s_read, 1)
            dve.sem_inc(lo_done, 2)
            dve.sem_inc(o_read, 1)
            dve.sem_inc(o_split, 1)
            dve.sem_inc(x_added, CPB)
            for t in range(TILES):
                own.step(dve.bn_stats(st[:, t, :], xres[:, t, :]))
            for n in range(NJOB):
                size, h, l = job_out(n)
                dve.wait_ge(pre_hi, n + 1)
                dve.tensor_tensor(l, ps[:, n % 8, 0:size], h.bitcast(F32), ALU.subtract).then_inc(pre_lo, 1)
                if n == 7:
                    own.wait()
                    for t in range(TILES):
                        own.step(dve.bn_aggr(mv[:, t, :], st[:, t, :]))
                    own.wait()
                    dve.tensor_scalar(var[:, :], mv[:, :, 1], EPS, None, ALU.add).then_inc(stats, 1)
                    dve.wait_ge(d_in, 16 * ND)
                    own.link(dve.tensor_copy(boh[:, :], bor[:, :]))
                    dve.tensor_tensor(bol[:, :], bor[:, :], boh[:, :].bitcast(F32), ALU.subtract).then_inc(ready, 1)
            dve.wait_ge(rooted, 1)
            newton_rsqrt(own, dve, var[:, :], root[:, :], rstd[:, :])
            dve.wait_ge(set_up, 1)
            dve.wait_ge(tanhed, 1)
            dve.wait_ge(pre_lo, NJOB)

            def normalise(C):
                for i in range(2):
                    n = 2 * C + i
                    last = dve.tensor_scalar(y[:, i, :], xres[:, bass.ds(n, 1), :], mv[:, bass.ds(n, 1), 0],
                                             rstd[:, bass.ds(n, 1)], ALU.subtract, ALU.mult)
                last.then_inc(y_ready, 1)

            def x_part(C):
                dve.wait_ge(x_hi, C + 1)
                dve.tensor_tensor(xTl[:, :, :].rearrange("p k t -> p (k t)"), ps[:, WO, :],
                                  xTh[:, :, :].bitcast(F32).rearrange("p k t -> p (k t)"), ALU.subtract).then_inc(x_lo, 1)

            def q_part(C, slot):
                dve.wait_ge(q_high, C + 1)
                dve.scalar_tensor_tensor(ql[:, slot, :, :].rearrange("p h t -> p (h t)"), ps[:, WO, :], float(C_DH) ** -0.5,
                                         qh[:, slot, :, :].bitcast(F32).rearrange("p h t -> p (h t)"),
                                         ALU.mult, ALU.subtract).then_inc(q_split, 1)

            def spread_k(b, h):
                dve.tensor_tensor(kbh[:, h, :, :], kTh[:, h, bass.ds(b, 1), :].bitcast(F32).broadcast_to([P, C_HPH, CTX]),
                                  hmask[:, :].unsqueeze(2).broadcast_to([P, C_HPH, CTX]), ALU.mult).then_inc(k_high, 1)

            def low(b, v, g):
                if v is None:
                    return
                lo, hi = GRP[g]
                dve.wait_ge(hi_done, 3 * (STEPS * b + v) + g + 1)
                dst = (slice(None), (v // 2) % 2, slice(lo, hi), slice((v % 2) * P, (v % 2 + 1) * P))
                dve.tensor_tensor(ptl[dst], ps[:, TURN + (v + g) % 2, 0:(hi - lo) * P].rearrange("p (n t) -> p n t", t=P),
                                  pth[dst].bitcast(F32), ALU.subtract).then_inc(lo_done, 1)

            def step(b, w, before, after):
                if w < STEPS:
                    W = STEPS * b + w
                    dve.wait_ge(s_done, W + 1)
                    dve.tensor_reduce(mx[:, :], scores, AX.X, ALU.max).then_inc(max_made, 1)
                    dve.wait_ge(max_made, W + 1)
                    dve.wait_ge(turned, 3 * W + 3)
                    m = mx[:, :].rearrange("p (b h) -> p b h", h=2).unsqueeze(3)
                    dve.tensor_tensor(p[:, w % 4, 0:C_HPH * P].rearrange("p (b h j) -> p b h j", h=2, j=P), scores[:, :, :, 0:P],
                                      m.broadcast_to([P, 4, 2, P]), ALU.subtract)
                    dve.tensor_tensor(p[:, w % 4, C_HPH * P:ROW].rearrange("p (b h j) -> p b h j", h=2, j=C_TAIL),
                                      scores[:, :, :, CTX - C_TAIL:CTX], m.broadcast_to([P, 4, 2, C_TAIL]),
                                      ALU.subtract).then_inc(s_read, 1)
                    if w >= STEPS - 2 and after:
                        spread_k(b + 1, w - (STEPS - 2))
                low(b, behind(w, 3, 1, before), 2)
                if w % 4 == 2 and w < STEPS and (after or w + 6 < STEPS):
                    normalise(CPB * b + (w + 6) // 4)
                if w % 4 == 0 and w < STEPS and (after or w + 4 < STEPS):
                    q_part(CPB * b + w // 4 + 1, (w // 4 + 1) % 2)
                low(b, behind(w, 2, 1, before), 0)
                if w % 4 == 3 and w < STEPS and (after or w + 5 < STEPS):
                    x_part(CPB * b + (w + 5) // 4)
                low(b, behind(w, 2, 1, before), 1)
                u = behind(w, SUMS, 2, before)
                if u is not None:
                    dve.wait_ge(o_read, TPB * b + u + 2)
                    dve.reciprocal(rs, rs).then_inc(o_recip, 1)
                c = behind(w, PROJECT, 4, before)
                if c is not None:
                    S = CPB * b + c
                    dve.wait_ge(wo_done, S + 2)
                    part = xres[:, bass.ds(2 * S, 2), :].rearrange("p t d -> p (t d)")
                    dve.scalar_tensor_tensor(part, ps[:, WO, :], tg[:, 0:1], part, ALU.mult, ALU.add).then_inc(x_added, 1)

            normalise(0)
            spread_k(0, 0)
            spread_k(0, 1)
            x_part(0)
            normalise(1)
            q_part(0, 0)
            x_part(1)
            steps(dve, step)

        @block.tensor
        def _(pe):
            pe.sem_inc(turned, 12)
            pe.sem_inc(wo_done, 1)
            pe.wait_ge(d_in, 16 * ND)
            for n in range(NJOB):
                if n >= 8:
                    pe.wait_ge(pre_lo, n - 7)
                bank = ps[:, n % 8, :]
                if n < 4:
                    for k in range(KT):
                        for o in range(2):
                            last = pe.transpose(bank[:, k * DIM + o * P:k * DIM + (o + 1) * P], wraw[:, n, o, k * P:(k + 1) * P], ident[:, :])
                elif n < 8:
                    k = (n % 4) // 2
                    for i in range(2):
                        b = 2 * (n % 2) + i
                        pe.transpose(bank[:, i * CTX:i * CTX + P], ctxA[:, b, k * P:(k + 1) * P], ident[:, :])
                        last = pe.transpose(bank[:, i * CTX + P:(i + 1) * CTX], ctxB[:, b, k * P:(k + 1) * P], ident[0:CTX - P, 0:CTX - P])
                elif n < 12:
                    if n == 8:
                        pe.wait_ge(pre_lo, 8)
                    h, b = (n % 4) // 2, 2 * (n % 2)
                    i = 0
                    for k in range(KT):
                        for w, x in ((wh, cth), (wh, ctl), (wl, cth)):
                            last = pe.matmul(bank[:, 0:2 * CTX], w[1][:, k, h * P:(h + 1) * P],
                                             x[:, k, b:b + 2, :].rearrange("p b j -> p (b j)"), start=(i == 0), stop=(i == 5))
                            i += 1
                else:
                    if n == 14:
                        pe.wait_ge(tails_set, 4)
                    for b2 in range(2):
                        b, i = 2 * (n % 2) + b2, 0
                        for k in range(KT):
                            for w, x in ((wh, cth), (wh, ctl), (wl, cth)):
                                if n < 14:
                                    lhs = x[:, k, b, 0:P]
                                else:
                                    lhs = tails[x is ctl][:, k, b, :, :].rearrange("p r j -> p (r j)")
                                last = pe.matmul(bank[:, b2 * DIM:(b2 + 1) * DIM], lhs, w[2][:, k, :], start=(i == 0), stop=(i == 5))
                                i += 1
                last.then_inc(pre_done, 1)
            pe.wait_ge(ready, 1)
            pe.wait_ge(pre_lo, NJOB)
            pe.wait_ge(set_up, 1)

            def turn(b, v, g):
                if v is None:
                    return
                V, (lo, hi) = STEPS * b + v, GRP[g]
                if g == 0:
                    pe.wait_ge(exp_done, V + 1)
                pe.wait_ge(lo_done, 3 * V + g + 1)
                for n in range(lo, hi):
                    last = pe.transpose(ps[:, TURN + (v + g) % 2, (n - lo) * P:(n - lo + 1) * P],
                                        p[:, v % 4, n * P:(n + 1) * P], ident[:, :])
                last.then_inc(turned, 1)

            def score(b, w):
                W = STEPS * b + w
                if w in (0, 2):
                    pe.wait_ge(k_high, 2 * b + w // 2 + 1)
                    pe.wait_ge(k_low, 2 * b + w // 2 + 1)
                if w % 4 == 0:
                    pe.wait_ge(q_split, CPB * b + w // 4 + 1)
                c, h, t = w // 4, (w // 2) % 2, w % 2
                pe.wait_ge(s_read, W + 1)
                for n in range(4):
                    out = ps[:, n, 0:2 * CTX]
                    for i, (q, k) in enumerate(((qh, kbh), (qh, kbl), (ql, kbh))):
                        last = pe.matmul(out, q[:, c % 2, h, t * P:(t + 1) * P], k[:, h, 2 * n:2 * n + 2, :].rearrange("p h j -> p (h j)"),
                                         start=(i == 0), stop=(i == 2 and c > 0))
                    if c == 0:
                        last = pe.matmul(out, identr[:, :], causal[:, t, :, :].rearrange("p h j -> p (h j)"), start=False, stop=True)
                last.then_inc(s_done, 1)

            def stat(h, n, vals):
                if n < C_HPH:
                    return vals[0][:, h, n * P:(n + 1) * P]
                return vals[1][:, 2 * h + n - C_HPH, :]

            def values(b, u):
                V, h = TPB * b + u, u % 2
                if u in (0, 1):
                    pe.wait_ge(v_spread, 12 * b + 6 * (u + 1))
                pe.wait_ge(lo_done, 6 * (V + 1) + 2)
                pe.wait_ge(o_read, V + 1)
                for n in range(NBLK):
                    for i, (v, x) in enumerate((((vah, vbh), pth), ((vah, vbh), ptl), ((val, vbl), pth))):
                        pe.matmul(ps[:, PV, 0:2 * P], stat(h, n, v), x[:, u % 2, n, :], start=(n == 0 and i == 0), stop=(n == NBLK - 1 and i == 2))

            def sums(b, u):
                for n in range(NBLK):
                    w = onesA[:, n * P:(n + 1) * P] if n < C_HPH else onesT[:, n - C_HPH, :]
                    for i, x in enumerate((pth, ptl)):
                        last = pe.matmul(ps[:, PV, 2 * P:4 * P], w, x[:, u % 2, n, :], start=(n == 0 and i == 0), stop=(n == NBLK - 1 and i == 1))
                last.then_inc(pv_done, 1)

            def project(b, c, more):
                S = CPB * b + c
                pe.wait_ge(o_split, 2 * (S + 1) + 1)
                pe.wait_ge(x_added, S + CPB)
                if more:
                    pe.wait_ge(q_split, S + 3)
                for t in range(2):
                    out = ps[:, WO, t * DIM:(t + 1) * DIM]
                    pe.matmul(out, one1[:, :], boh[:, :], start=True, stop=False)
                    pe.matmul(out, one1[:, :], bol[:, :], start=False, stop=False)
                    for k in range(KT):
                        for i, (o, w) in enumerate(((oh, wh), (oh, wl), (ol, wh))):
                            last = pe.matmul(out, o[:, k, t * P:(t + 1) * P], w[3][:, k, :], start=False, stop=(k == 1 and i == 2))
                last.then_inc(wo_done, 1)

            def x_turn(C):
                pe.wait_ge(y_ready, C + 1)
                if not isinstance(C, int) or C:
                    pe.wait_ge(q_split, C)
                    pe.wait_ge(x_added, C + 1)
                for k in range(KT):
                    for i in range(2):
                        last = pe.transpose(ps[:, WO, (2 * k + i) * P:(2 * k + i + 1) * P], y[:, i, k * P:(k + 1) * P], ident[:, :])
                last.then_inc(x_turned, 1)

            def query(C):
                pe.wait_ge(x_lo, C + 1)
                for h in range(2):
                    i = 0
                    for k in range(KT):
                        for w, x in ((wh, xTh), (wh, xTl), (wl, xTh)):
                            last = pe.matmul(ps[:, WO, 2 * h * P:2 * (h + 1) * P], w[0][:, k, h * P:(h + 1) * P], x[:, k, :],
                                             start=(i == 0), stop=(i == 5))
                            i += 1
                last.then_inc(q_done, 1)

            def step(b, w, before, after):
                if w < STEPS:
                    score(b, w)
                turn(b, behind(w, 3, 1, before), 2)
                c = behind(w, PROJECT, 4, before)
                if c is not None:
                    project(b, c, after or w < LOOP + 4)
                if w % 4 == 0 and w < STEPS and (after or w + 4 < STEPS):
                    query(CPB * b + w // 4 + 1)
                u = behind(w, SUMS, 2, before)
                if u is not None:
                    sums(b, u)
                turn(b, behind(w, 2, 1, before), 0)
                u = behind(w, VALUES, 2, before)
                if u is not None:
                    values(b, u)
                if w % 4 == 3 and w < STEPS and (after or w + 5 < STEPS):
                    x_turn(CPB * b + (w + 5) // 4)
                turn(b, behind(w, 2, 1, before), 1)

            x_turn(0)
            query(0)
            x_turn(1)
            steps(pe, step)


HID = 1024
HB = HID // P
MAGIC = 1.5 * 2.0 ** 23
QMAX, QMIN = 127.0, -128.0
TINY = 1e-5


def ffn_stage(nc, xres, ident, A):
    with ExitStack() as ctx:
        def sb(name, shape, dt=F32):
            return ctx.enter_context(nc.sbuf_tensor("ffn_" + name, shape, dt))

        def sem(name):
            return nc.alloc_semaphore("ffn_" + name)

        w1, w2 = sb("w1", [P, HB, DIM]), sb("w2", [P, KT, HID])
        w1q, w2q = sb("w1q", [P, HB, DIM], BF16), sb("w2q", [P, KT, HID], BF16)
        w1T, w2T = sb("w1T", [P, KT, HID], BF16), sb("w2T", [P, HB, DIM], BF16)
        conv_w, conv_b = sb("conv_w", [P, HB, 3]), sb("conv_b", [P, HB])
        tg = sb("tg", [P, 1])
        wsum, winv, wsc, fac = sb("wsum", [P, 2]), sb("winv", [P, 2]), sb("wsc", [P, 2]), sb("fac", [P, 1])
        ones, identb = sb("ones", [P, P]), sb("identb", [P, P], BF16)
        st, mv = sb("st", [P, TILES, 6]), sb("mv", [P, TILES, 2])
        var, root, rstd = sb("var", [P, TILES]), sb("root", [P, TILES]), sb("rstd", [P, TILES])
        y = sb("y", [P, TPB, DIM])
        yq = sb("yq", [P, TPB, DIM], BF16)
        am, sc, d1 = sb("am", [P, TPB]), sb("sc", [P, TPB]), sb("d1", [P, TPB])
        diag = sb("diag", [P, TPB, P])
        rsc = sb("rsc", [P, SEQ])
        yT = sb("yT", [P, KT, SEQ], BF16)
        hb = [sb(f"hb{i}", [P, SEQ + 2]) for i in range(2)]
        acc = sb("acc", [P, 2, SEQ])
        hs = sb("hs", [P, HB, SEQ])
        am2, sc2, d2 = sb("am2", [P, TPB]), sb("sc2", [P, TPB]), sb("d2", [P, TPB])
        u = sb("u", [P, 2, HID])
        r2 = sb("r2", [P, 2, HID], BF16)
        r2T = sb("r2T", [P, 2, HB, P], BF16)
        ps = ctx.enter_context(nc.psum_tensor("ffn_ps", [P, 8, CH], F32))
        wide = [ps[:, 0:2, :].rearrange("p b c -> p (b c)"), ps[:, 2:4, :].rearrange("p b c -> p (b c)")]
        half = [ps[:, 4, :].bitcast(BF16), ps[:, 5, :].bitcast(BF16)]
        outp = [ps[:, 6, 0:DIM], ps[:, 7, 0:DIM]]
        scales = ps[:, 6:8, :].rearrange("p b c -> p (b c)")

        d_w, dve_own = sem("d_w"), sem("dve_own")
        d1_made, alone_pool = sem("d1_made"), sem("alone_pool")
        a_own, b_own, c_own = sem("quantise_own"), sem("hidden_own"), sem("output_own")
        set_up, summed, totalled, w_quant, w_turned, w_kept, tanhed = (
            sem(n) for n in ("set_up", "summed", "totalled", "w_quant", "w_turned", "w_kept", "tanhed"))
        stats, rooted = sem("stats"), sem("rooted")
        y_quant, diag_set, y_turned, y_kept, rsc_done, rsc_kept = (
            sem(n) for n in ("y_quant", "diag_set", "y_turned", "y_kept", "rsc_done", "rsc_kept"))
        hid_done, h_done, conv_mid, conv_done, hs_done = (
            sem(n) for n in ("hid_done", "h_done", "conv_mid", "conv_done", "hs_done"))
        t_done, sc_done, t_read, b_done, r2_done, r2_turned, r2_kept, out_done, out_added = (
            sem(n) for n in ("t_done", "sc_done", "t_read", "b_done", "r2_done", "r2_turned", "r2_kept", "out_done", "out_added"))
        block = ctx.enter_context(nc.Block())

        def batches(eng, quantise, hidden, output):
            quantise(0)
            with eng.Fori(0, BATCH - 1) as b:
                hidden(b)
                output(b, lambda: quantise(b + 1))
            hidden(BATCH - 1)
            output(BATCH - 1, None)

        @block.sync
        def _(sp):
            sp.dma_start(w1[:, :, :], A["L1_ffn_w1"].rearrange("(b p) d -> p b d", p=P)).then_inc(d_w, 16)
            sp.dma_start(w2[:, :, :], A["L1_ffn_w2"].rearrange("(k p) h -> p k h", p=P)).then_inc(d_w, 16)
            sp.dma_start(conv_w[:, :, :], A["L1_ffn_conv_w"].rearrange("(b p) o w -> p b (o w)", p=P)).then_inc(d_w, 16)
            with nc.allow_non_contiguous_dma(reason="small columns"):
                sp.dma_start(conv_b[:, :], A["L1_ffn_conv_b"].rearrange("(b p) -> p b", p=P)).then_inc(d_w, 16)
                sp.dma_start(tg[:, :], A["g_ffn"][1:2].partition_broadcast(P)).then_inc(d_w, 16)

        @block.gpsimd
        def _(pool):
            pool.memset(ones[:, :], 1.0).then_inc(set_up, 1)
            pool.tensor_copy(identb[:, :], ident[:, :]).then_inc(set_up, 1)
            for h in hb:
                pool.memset(h[:, 0:1], 0.0).then_inc(set_up, 1)
                pool.memset(h[:, SEQ + 1:SEQ + 2], 0.0).then_inc(set_up, 1)
            with pool.Fori(0, BATCH) as b:
                pool.wait_ge(d1_made, b + 1)
                pool.sem_inc(alone_pool, 1)
                pool.tensor_tensor(diag[:, :, :], ident[:, :].unsqueeze(1).broadcast_to([P, TPB, P]),
                                   d1[:, :].unsqueeze(2).broadcast_to([P, TPB, P]), ALU.mult).then_inc(diag_set, 1)

        @block.scalar
        def _(act):
            act.wait_ge(d_w, 80)
            act.activation(tg[:, :], tg[:, :], ACT.Tanh).then_inc(tanhed, 1)
            act.wait_ge(stats, 1)
            act.activation(root[:, :], var[:, :], ACT.Sqrt).then_inc(rooted, 1)
            for i, dst in enumerate((w1T, w2T)):
                n = dst.shape[1] // 2 if i else 1
                for k in range(2):
                    act.wait_ge(w_turned, 2 * i + k + 1)
                    act.activation(dst[:, k * n:(k + 1) * n, :].rearrange("p k h -> p (k h)"), half[k], ACT.Copy).then_inc(w_kept, 1)

            def quantise(b):
                for k in range(KT):
                    act.wait_ge(y_turned, KT * b + k + 1)
                    act.activation(yT[:, k, :], half[k], ACT.Copy).then_inc(y_kept, 1)
                act.wait_ge(rsc_done, b + 1)
                act.activation(rsc[:, :], scales, ACT.Copy).then_inc(rsc_kept, 1)

            def hidden(b):
                def middle(q):
                    act.wait_ge(h_done, HB * b + q + 1)
                    act.activation(acc[:, q % 2, :], hb[q % 2][:, 1:SEQ + 1], ACT.Identity, bias=conv_b[:, q:q + 1],
                                   scale=conv_w[:, q, 1:2]).then_inc(conv_mid, 1)

                middle(0)
                for q in range(HB):
                    if q + 1 < HB:
                        if q:
                            act.wait_ge(hs_done, HB * b + q)
                        middle(q + 1)
                    act.wait_ge(conv_done, HB * b + q + 1)
                    act.activation(hs[:, q, :], acc[:, q % 2, :], ACT.Silu).then_inc(hs_done, 1)

            def output(b, between):
                if between:
                    between()
                for t in range(TPB + 1):
                    n = TPB * b + t
                    if t < TPB:
                        act.wait_ge(sc_done, n + 1)
                        if t >= 2:
                            act.wait_ge(r2_done, n - 1)
                        act.activation(u[:, t % 2, :], wide[t % 2], ACT.Copy, scale=sc2[:, t:t + 1]).then_inc(t_read, 1)
                    if t:
                        act.wait_ge(r2_turned, n)
                        act.activation(r2T[:, (t - 1) % 2, :, :].rearrange("p b t -> p (b t)"), half[(t - 1) % 2], ACT.Copy).then_inc(r2_kept, 1)

            batches(act, quantise, hidden, output)

        @block.vector
        def _(dve):
            own = Chain(dve, dve_own)
            for t in range(TILES):
                own.step(dve.bn_stats(st[:, t, :], xres[:, t, :]))
            own.wait()
            for t in range(TILES):
                own.step(dve.bn_aggr(mv[:, t, :], st[:, t, :]))
            own.wait()
            dve.tensor_scalar(var[:, :], mv[:, :, 1], EPS, None, ALU.add).then_inc(stats, 1)
            dve.wait_ge(d_w, 80)
            own.step(dve.tensor_reduce(wsum[:, 0:1], w1[:, :, :], AX.XY, ALU.add, apply_absolute_value=True))
            dve.tensor_reduce(wsum[:, 1:2], w2[:, :, :], AX.XY, ALU.add, apply_absolute_value=True).then_inc(summed, 1)
            own.wait()
            dve.wait_ge(totalled, 1)
            own.link(dve.tensor_scalar(winv[:, :], outp[0][:, 0:2], 1.0 / (HID * DIM), TINY, ALU.mult, ALU.max))
            own.link(dve.reciprocal(wsc[:, :], winv[:, :]))
            for i, (w, wq) in enumerate(((w1, w1q), (w2, w2q))):
                own.link(dve.tensor_scalar(w[:, :, :], w[:, :, :], wsc[:, i:i + 1], 1.0, ALU.mult, ALU.min))
                own.link(dve.tensor_scalar(w[:, :, :], w[:, :, :], -1.0, MAGIC, ALU.max, ALU.add))
                dve.tensor_scalar(wq[:, :, :], w[:, :, :], MAGIC, None, ALU.subtract).then_inc(w_quant, 1)
            dve.wait_ge(tanhed, 1)
            own.link(dve.tensor_scalar(fac[:, :], winv[:, 1:2], tg[:, 0:1], 1.0 / QMAX, ALU.mult, ALU.mult))
            dve.wait_ge(rooted, 1)
            newton_rsqrt(own, dve, var[:, :], root[:, :], rstd[:, :])
            dve.wait_ge(set_up, 6)

            A_OWN, C_OWN = 8 + 5 + 8 + 1, 3 * TPB

            def counted(sem, done):
                c = Chain(dve, sem)
                c.base = done
                return c

            def quantise(b):
                own = counted(a_own, A_OWN * b)
                for t in range(TPB):
                    n = TPB * b + t
                    own.step(dve.tensor_scalar(y[:, t, :], xres[:, bass.ds(n, 1), :], mv[:, bass.ds(n, 1), 0],
                                               rstd[:, bass.ds(n, 1)], ALU.subtract, ALU.mult))
                own.wait()
                own.link(dve.tensor_reduce(am[:, :], y[:, :, :], AX.X, ALU.max, apply_absolute_value=True))
                own.link(dve.tensor_scalar(am[:, :], am[:, :], TINY, None, ALU.max))
                own.link(dve.reciprocal(sc[:, :], am[:, :]))
                own.link(dve.tensor_scalar(sc[:, :], sc[:, :], QMAX, None, ALU.mult))
                own.link(dve.reciprocal(d1[:, :], sc[:, :]))
                dve.tensor_scalar(d1[:, :], d1[:, :], winv[:, 0:1], None, ALU.mult).then_inc(d1_made, 1)
                for t in range(TPB):
                    own.step(dve.tensor_scalar(y[:, t, :], y[:, t, :], sc[:, t:t + 1], QMAX, ALU.mult, ALU.min))
                own.wait()
                own.link(dve.tensor_scalar(y[:, :, :], y[:, :, :], QMIN, MAGIC, ALU.max, ALU.add))
                assert own.k == A_OWN
                dve.tensor_scalar(yq[:, :, :], y[:, :, :], MAGIC, None, ALU.subtract).then_inc(y_quant, 1)

            def hidden(b):
                def scale(q):
                    dve.wait_ge(hid_done, HB * b + q + 1)
                    dve.tensor_tensor(hb[q % 2][:, 1:SEQ + 1], wide[q % 2], rsc[:, :], ALU.mult).then_inc(h_done, 1)

                dve.wait_ge(rsc_kept, b + 1)
                scale(0)
                for q in range(HB):
                    if q + 1 < HB:
                        scale(q + 1)
                    a = acc[:, q % 2, :]
                    dve.wait_ge(conv_mid, HB * b + q + 1)
                    dve.scalar_tensor_tensor(a, hb[q % 2][:, 0:SEQ], conv_w[:, q, 0:1], a, ALU.mult, ALU.add).then_inc(b_own, 1)
                    dve.wait_ge(b_own, HB * b + q + 1)
                    dve.scalar_tensor_tensor(a, hb[q % 2][:, 2:SEQ + 2], conv_w[:, q, 2:3], a, ALU.mult, ALU.add).then_inc(conv_done, 1)
                    if q + 2 < HB:
                        dve.wait_ge(conv_done, HB * b + q + 1)

            def output(b, between):
                if between:
                    between()
                own = counted(c_own, C_OWN * b)

                def scale(t, part):
                    if t >= TPB:
                        return
                    c = slice(t, t + 1)
                    if part == 0:
                        dve.wait_ge(t_done, TPB * b + t + 1)
                        own.step(dve.tensor_reduce(am2[:, c], wide[t % 2], AX.X, ALU.max, apply_absolute_value=True))
                    elif part == 1:
                        own.wait()
                        own.step(dve.tensor_scalar(am2[:, c], am2[:, c], TINY, None, ALU.max))
                    elif part == 2:
                        own.wait()
                        own.step(dve.reciprocal(sc2[:, c], am2[:, c]))
                        dve.tensor_scalar(d2[:, c], am2[:, c], fac[:, 0:1], None, ALU.mult)
                    else:
                        own.wait()
                        dve.tensor_scalar(sc2[:, c], sc2[:, c], QMAX, None, ALU.mult).then_inc(sc_done, 1)

                for part in range(4):
                    scale(0, part)
                for t in range(TPB + 2):
                    n = TPB * b + t
                    scale(t + 1, 0)
                    if t < TPB:
                        dve.wait_ge(t_read, n + 1)
                        dve.tensor_scalar(u[:, t % 2, :], u[:, t % 2, :], QMAX, QMIN, ALU.min, ALU.max).then_inc(b_done, 1)
                    scale(t + 1, 1)
                    if t < TPB:
                        dve.wait_ge(b_done, n + 1)
                        if t >= 2:
                            dve.wait_ge(r2_turned, n - 1)
                        dve.tensor_scalar(r2[:, t % 2, :], u[:, t % 2, :], MAGIC, MAGIC, ALU.add, ALU.subtract).then_inc(r2_done, 1)
                    scale(t + 1, 2)
                    scale(t + 1, 3)
                    if t >= 2:
                        dve.wait_ge(out_done, n - 1)
                        part = xres[:, bass.ds(n - 2, 1), :].rearrange("p a d -> p (a d)")
                        dve.scalar_tensor_tensor(part, outp[t % 2], d2[:, t - 2:t - 1], part, ALU.mult, ALU.add).then_inc(out_added, 1)
                assert own.k == C_OWN

            batches(dve, quantise, hidden, output)

        @block.tensor
        def _(pe):
            pe.wait_ge(set_up, 6)
            pe.wait_ge(summed, 1)
            pe.wait_ge(d_w, 80)
            pe.matmul(outp[0][:, 0:2], ones[:, :], wsum[:, :], start=True, stop=True).then_inc(totalled, 1)
            pe.wait_ge(w_quant, 1)
            for k in range(KT):
                for b in range(HB):
                    last = pe.transpose(half[k][:, b * P:(b + 1) * P], w1q[:, b, k * P:(k + 1) * P], identb[:, :])
                last.then_inc(w_turned, 1)
            pe.wait_ge(w_quant, 2)
            for i in range(2):
                pe.wait_ge(w_kept, i + 1)
                for b in range(HB // 2):
                    for k in range(KT):
                        q = i * (HB // 2) + b
                        last = pe.transpose(half[i][:, (b * KT + k) * P:(b * KT + k + 1) * P], w2q[:, k, q * P:(q + 1) * P], identb[:, :])
                last.then_inc(w_turned, 1)
            pe.wait_ge(w_kept, 4)

            def quantise(b):
                pe.wait_ge(y_quant, b + 1)
                for k in range(KT):
                    for t in range(TPB):
                        last = pe.transpose(half[k][:, t * P:(t + 1) * P], yq[:, t, k * P:(k + 1) * P], identb[:, :])
                    last.then_inc(y_turned, 1)
                pe.wait_ge(diag_set, b + 1)
                for t in range(TPB):
                    last = pe.matmul(scales[:, t * P:(t + 1) * P], ones[:, :], diag[:, t, :], start=True, stop=True)
                last.then_inc(rsc_done, 1)
                pe.wait_ge(y_kept, KT * (b + 1))
                pe.wait_ge(rsc_kept, b + 1)

            def hidden(b):
                for q in range(HB):
                    if q >= 2:
                        pe.wait_ge(h_done, HB * b + q - 1)
                    for c in range(SEQ // CH):
                        for k in range(KT):
                            last = pe.matmul(wide[q % 2][:, c * CH:(c + 1) * CH], w1T[:, k, q * P:(q + 1) * P],
                                             yT[:, k, c * CH:(c + 1) * CH], start=(k == 0), stop=(k == KT - 1))
                    last.then_inc(hid_done, 1)

            def output(b, between):
                def turn(t):
                    n = TPB * b + t
                    if t >= 2:
                        pe.wait_ge(t_read, n - 1)
                    for q in range(HB):
                        last = pe.transpose(wide[t % 2][:, q * P:(q + 1) * P], hs[:, q, t * P:(t + 1) * P], ident[:, :])
                    last.then_inc(t_done, 1)

                pe.wait_ge(h_done, HB * (b + 1))
                pe.wait_ge(hs_done, HB * (b + 1))
                turn(0)
                turn(1)
                if between:
                    between()
                for t in range(TPB + 1):
                    n = TPB * b + t
                    if t + 2 < TPB:
                        turn(t + 2)
                    if t < TPB:
                        pe.wait_ge(r2_done, n + 1)
                        for q in range(HB):
                            last = pe.transpose(half[t % 2][:, q * P:(q + 1) * P], r2[:, t % 2, q * P:(q + 1) * P], identb[:, :])
                        last.then_inc(r2_turned, 1)
                    if t:
                        pe.wait_ge(r2_kept, n)
                        if t >= 3:
                            pe.wait_ge(out_added, n - 2)
                        for q in range(HB):
                            last = pe.matmul(outp[(t - 1) % 2], r2T[:, (t - 1) % 2, q, :], w2T[:, q, :], start=(q == 0), stop=(q == HB - 1))
                        last.then_inc(out_done, 1)
                pe.wait_ge(out_added, TPB * (b + 1))

            batches(pe, quantise, hidden, output)


def flamingo_program(nc, A, out):
    with ExitStack() as ctx:
        xres = ctx.enter_context(nc.sbuf_tensor("xres", [P, TILES, DIM], F32))
        ident = ctx.enter_context(nc.sbuf_tensor("ident", [P, P], F32))
        ident_set, stored = nc.alloc_semaphore("ident_set"), nc.alloc_semaphore("stored")
        with nc.Block() as block:
            @block.gpsimd
            def _(pool):
                pool.memset(ident[:, :], 0.0).then_inc(ident_set, 1)
                pool.wait_ge(ident_set, 1)
                pool.affine_select(out=ident[:, :], in_=ident[:, :], compare_op=ALU.not_equal, fill=1.0, base=0,
                                   pattern=[[-1, P]], channel_multiplier=1).then_inc(ident_set, 1)
                pool.wait_ge(ident_set, 2)
        resample_stage(nc, xres, ident, A)
        moe_stage(nc, xres, ident, A)
        ctx_attention_stage(nc, xres, ident, A)
        ffn_stage(nc, xres, ident, A)
        with nc.Block() as block:
            @block.sync
            def _(sp):
                sp.dma_start(out.rearrange("b (t p) d -> p (b t) d", p=P), xres[:, :, :]).then_inc(stored, 16)
                sp.wait_ge(stored, 16)


def kernel(**inputs):
    import concourse.bacc as bacc
    from concourse.bass_utils import run_bass_kernel_spmd

    nc = bacc.Bacc("TRN2", target_bir_lowering=False, num_devices=1)
    arrays, A = {}, {}
    for name, value in inputs.items():
        a = np.ascontiguousarray(value)
        arrays[f"in_{name}_dram"] = a
        A[name] = nc.dram_tensor(f"in_{name}_dram", a.shape, mybir.dt.from_np(a.dtype), kind="ExternalInput").ap()
    out = nc.dram_tensor("out_dram", (BATCH, SEQ, DIM), F32, kind="ExternalOutput").ap()
    flamingo_program(nc, A, out)
    r = run_bass_kernel_spmd(nc, [arrays], core_ids=[0])
    return r.results[0]["out_dram"]
```
